# Optimizing a Trainium2 kernel written in Bass

```python
import numpy as np
import jax
import jax.numpy as jnp

def _softmax(x, axis=-1):
    return jax.nn.softmax(x, axis=axis)

def _gelu(x):
    return jax.nn.gelu(x, approximate=True)

def _silu(x):
    return jax.nn.silu(x)

def _sigmoid(x):
    return jax.nn.sigmoid(x)

def _layernorm(x, axis=-1, eps=1e-05):
    m = jnp.mean(x, axis=axis, keepdims=True)
    v = jnp.var(x, axis=axis, keepdims=True)
    return (x - m) / jnp.sqrt(v + eps)

def _scatter_add(tgt, idx, src, axis=0):
    return tgt.at[idx].add(src)

def _segment_sum(src, seg, n):
    return jax.ops.segment_sum(src, seg, n)
kernel_name = 'mk_cond_seq_d4_seqx_r4_241ec6'

def setup_inputs(seed: int=0):
    np.random.seed(seed)
    _w = jnp.asarray

    def _rec_inputs():
        import jax
        import jax.numpy as jnp
        _rk = jax.random.key(seed)
        x = -0.0003482 + 1 * jax.random.normal(jax.random.fold_in(_rk, 1), (2, 1024, 288), jnp.float32)
        _lenS = 1024 - jax.random.randint(jax.random.fold_in(_rk, 7), (2,), 0, max(1, 1024 // 4) + 1, jnp.int32)
        _lenS2 = 1024 - jax.random.randint(jax.random.fold_in(_rk, 8), (2,), 0, max(1, 1024 // 4) + 1, jnp.int32)
        cond_1152 = 0.00257642 + 1.0011 * jax.random.normal(jax.random.fold_in(_rk, 11), (2, 288), jnp.float32)
        return (x, cond_1152)
    x, cond_1152 = _rec_inputs()

    def _L0_cond_setup():
        import jax, jax.numpy as jnp
        import numpy as np
        from jax.scipy.linalg import expm
        N, D, COND_DIM = (288, 64, 288)
        B, T = (16, 256)

        def _rotation(cond, W, b):
            v = jax.nn.silu(cond) @ W.T + b
            iu, ju = jnp.triu_indices(D, k=1)
            A = jnp.zeros((cond.shape[0], D, D), dtype=v.dtype)
            A = A.at[:, iu, ju].set(v).at[:, ju, iu].set(-v)
            return expm(A)
        key = jax.random.key(seed)
        k1, k2, k3, k4, k5 = jax.random.split(key, 5)
        x = jax.random.normal(k1, (B, T, N), dtype=jnp.float32)
        cond = jax.random.normal(k2, (B, COND_DIM), dtype=jnp.float32)
        P = jax.random.normal(k3, (N, D), dtype=jnp.float32)
        n_skew = D * (D - 1) // 2
        bound = 1.0 / np.sqrt(COND_DIM)
        W = jax.random.uniform(k4, (n_skew, COND_DIM), minval=-bound, maxval=bound, dtype=jnp.float32)
        b = jax.random.uniform(k5, (n_skew,), minval=-bound, maxval=bound, dtype=jnp.float32)
        return {'x': x, 'cond': cond, 'P': P, 'W': W, 'b': b}
    _L0_cond_all = _L0_cond_setup()
    _L0_cond_in = {k: v for k, v in _L0_cond_all.items() if k in ('P', 'W', 'b')}
    del _L0_cond_all

    def _L1_cond_setup():
        import jax, jax.numpy as jnp
        import numpy as np
        NUM_HEADS = 16
        NUM_EXPERTS = 4
        TOP_K = 2
        LN_EPS = 1e-06

        def _ln(h):
            mu = jnp.mean(h, axis=-1, keepdims=True)
            var = jnp.var(h, axis=-1, keepdims=True)
            return (h - mu) * jax.lax.rsqrt(var + LN_EPS)

        def _modulate(h, shift, scale):
            return h * (1.0 + scale[:, None, :]) + shift[:, None, :]
        key = jax.random.key(seed)
        ks = jax.random.split(key, 12)
        B, N, C = (8, 256, 288)
        H = 4 * C
        E = NUM_EXPERTS
        s = 0.02
        return {'x': jax.random.normal(ks[0], (B, N, C), jnp.float32), 'c': jax.random.normal(ks[1], (B, C), jnp.float32), 'w_adaln': jax.random.normal(ks[2], (C, 6 * C), jnp.float32) * s, 'b_adaln': jnp.zeros((6 * C,), jnp.float32), 'w_qkv': jax.random.normal(ks[3], (C, 3 * C), jnp.float32) * s, 'b_qkv': jnp.zeros((3 * C,), jnp.float32), 'w_proj': jax.random.normal(ks[4], (C, C), jnp.float32) * s, 'b_proj': jnp.zeros((C,), jnp.float32), 'w_gate': jax.random.normal(ks[5], (C, E), jnp.float32) * s, 'w1': jax.random.normal(ks[6], (E, C, H), jnp.float32) * s, 'b1': jnp.zeros((E, H), jnp.float32), 'w2': jax.random.normal(ks[7], (E, H, C), jnp.float32) * s, 'b2': jnp.zeros((E, C), jnp.float32)}
    _L1_cond_all = _L1_cond_setup()
    _L1_cond_in = {k: v for k, v in _L1_cond_all.items() if k in ('w_adaln', 'b_adaln', 'w_qkv', 'b_qkv', 'w_proj', 'b_proj', 'w_gate', 'w1', 'b1', 'w2', 'b2')}
    del _L1_cond_all

    def _L2_cond_setup():
        import jax, jax.numpy as jnp
        import numpy as np
        HID = 288
        HEADS = 16
        HD = HID // HEADS
        MLP = int(HID * 4.0)

        def _ln(x, eps, gamma=None, beta=None):
            mu = jnp.mean(x, axis=-1, keepdims=True)
            var = jnp.mean(jnp.square(x - mu), axis=-1, keepdims=True)
            y = (x - mu) / jnp.sqrt(var + eps)
            if gamma is not None:
                y = y * gamma + beta
            return y
        key = jax.random.key(seed)
        ks = jax.random.split(key, 12)
        B, N, C = (8, 256, HID)
        s = lambda k, *sh: jax.random.normal(k, sh, dtype=jnp.float32) * 0.02
        return {'x': jax.random.normal(ks[0], (B, N, C), dtype=jnp.float32), 'c': jax.random.normal(ks[1], (B, C), dtype=jnp.float32), 'w_qkv': s(ks[2], C, 3 * C), 'b_qkv': jnp.zeros((3 * C,), jnp.float32), 'w_proj': s(ks[3], C, C), 'b_proj': jnp.zeros((C,), jnp.float32), 'qn_g': jnp.ones((HD,), jnp.float32), 'qn_b': jnp.zeros((HD,), jnp.float32), 'kn_g': jnp.ones((HD,), jnp.float32), 'kn_b': jnp.zeros((HD,), jnp.float32), 'w1': s(ks[4], C, MLP), 'b1': jnp.zeros((MLP,), jnp.float32), 'w2': s(ks[5], MLP, C), 'b2': jnp.zeros((C,), jnp.float32), 'w_ada': s(ks[6], C, 6 * C), 'b_ada': jnp.zeros((6 * C,), jnp.float32)}
    _L2_cond_all = _L2_cond_setup()
    _L2_cond_in = {k: v for k, v in _L2_cond_all.items() if k in ('w_qkv', 'b_qkv', 'w_proj', 'b_proj', 'qn_g', 'qn_b', 'kn_g', 'kn_b', 'w1', 'b1', 'w2', 'b2', 'w_ada', 'b_ada')}
    del _L2_cond_all

    def _L3_cond_setup():
        import jax, jax.numpy as jnp
        import numpy as np
        B, L, C = (8, 256, 288)
        H = 16
        D = C // H
        FF = int(C * 4.0)
        EPS = 1e-06

        def _layernorm(x):
            mu = jnp.mean(x, axis=-1, keepdims=True)
            var = jnp.mean(jnp.square(x - mu), axis=-1, keepdims=True)
            return (x - mu) * jax.lax.rsqrt(var + EPS)

        def _modulate(x, shift, scale):
            return x * (1.0 + scale) + shift

        def _attention(h, W_qkv, b_qkv, W_proj, b_proj):
            b, l, c = h.shape
            qkv = h @ W_qkv + b_qkv
            qkv = qkv.reshape(b, l, 3, H, D)
            q, k, v = (qkv[:, :, 0], qkv[:, :, 1], qkv[:, :, 2])
            scale = D ** (-0.5)
            scores = jnp.einsum('blhd,bmhd->bhlm', q * scale, k)
            attn = jax.nn.softmax(scores, axis=-1)
            o = jnp.einsum('bhlm,bmhd->blhd', attn, v).reshape(b, l, c)
            return o @ W_proj + b_proj
        key = jax.random.key(seed)
        ks = jax.random.split(key, 12)
        s = 0.02
        return {'x': jax.random.normal(ks[0], (B, L, C), jnp.float32), 'c': jax.random.normal(ks[1], (B, 1, C), jnp.float32), 'W_qkv': jax.random.normal(ks[2], (C, 3 * C), jnp.float32) * s, 'b_qkv': jnp.zeros((3 * C,), jnp.float32), 'W_proj': jax.random.normal(ks[3], (C, C), jnp.float32) * s, 'b_proj': jnp.zeros((C,), jnp.float32), 'W_fc1': jax.random.normal(ks[4], (C, FF), jnp.float32) * s, 'b_fc1': jnp.zeros((FF,), jnp.float32), 'W_fc2': jax.random.normal(ks[5], (FF, C), jnp.float32) * s, 'b_fc2': jnp.zeros((C,), jnp.float32), 'W_ada': jax.random.normal(ks[6], (C, 6 * C), jnp.float32) * s, 'b_ada': jnp.zeros((6 * C,), jnp.float32)}
    _L3_cond_all = _L3_cond_setup()
    _L3_cond_in = {k: v for k, v in _L3_cond_all.items() if k in ('W_qkv', 'b_qkv', 'W_proj', 'b_proj', 'W_fc1', 'b_fc1', 'W_fc2', 'b_fc2', 'W_ada', 'b_ada')}
    del _L3_cond_all
    return {'x': x, 'cond_1152': cond_1152, 'L0_cond_P': _L0_cond_in['P'], 'L0_cond_W': _L0_cond_in['W'], 'L0_cond_b': _L0_cond_in['b'], 'L1_cond_w_adaln': _L1_cond_in['w_adaln'], 'L1_cond_b_adaln': _L1_cond_in['b_adaln'], 'L1_cond_w_qkv': _L1_cond_in['w_qkv'], 'L1_cond_b_qkv': _L1_cond_in['b_qkv'], 'L1_cond_w_proj': _L1_cond_in['w_proj'], 'L1_cond_b_proj': _L1_cond_in['b_proj'], 'L1_cond_w_gate': _L1_cond_in['w_gate'], 'L1_cond_w1': _L1_cond_in['w1'], 'L1_cond_b1': _L1_cond_in['b1'], 'L1_cond_w2': _L1_cond_in['w2'], 'L1_cond_b2': _L1_cond_in['b2'], 'L2_cond_w_qkv': _L2_cond_in['w_qkv'], 'L2_cond_b_qkv': _L2_cond_in['b_qkv'], 'L2_cond_w_proj': _L2_cond_in['w_proj'], 'L2_cond_b_proj': _L2_cond_in['b_proj'], 'L2_cond_qn_g': _L2_cond_in['qn_g'], 'L2_cond_qn_b': _L2_cond_in['qn_b'], 'L2_cond_kn_g': _L2_cond_in['kn_g'], 'L2_cond_kn_b': _L2_cond_in['kn_b'], 'L2_cond_w1': _L2_cond_in['w1'], 'L2_cond_b1': _L2_cond_in['b1'], 'L2_cond_w2': _L2_cond_in['w2'], 'L2_cond_b2': _L2_cond_in['b2'], 'L2_cond_w_ada': _L2_cond_in['w_ada'], 'L2_cond_b_ada': _L2_cond_in['b_ada'], 'L3_cond_W_qkv': _L3_cond_in['W_qkv'], 'L3_cond_b_qkv': _L3_cond_in['b_qkv'], 'L3_cond_W_proj': _L3_cond_in['W_proj'], 'L3_cond_b_proj': _L3_cond_in['b_proj'], 'L3_cond_W_fc1': _L3_cond_in['W_fc1'], 'L3_cond_b_fc1': _L3_cond_in['b_fc1'], 'L3_cond_W_fc2': _L3_cond_in['W_fc2'], 'L3_cond_b_fc2': _L3_cond_in['b_fc2'], 'L3_cond_W_ada': _L3_cond_in['W_ada'], 'L3_cond_b_ada': _L3_cond_in['b_ada']}

def reference(x, cond_1152, L0_cond_P, L0_cond_W, L0_cond_b, L1_cond_w_adaln, L1_cond_b_adaln, L1_cond_w_qkv, L1_cond_b_qkv, L1_cond_w_proj, L1_cond_b_proj, L1_cond_w_gate, L1_cond_w1, L1_cond_b1, L1_cond_w2, L1_cond_b2, L2_cond_w_qkv, L2_cond_b_qkv, L2_cond_w_proj, L2_cond_b_proj, L2_cond_qn_g, L2_cond_qn_b, L2_cond_kn_g, L2_cond_kn_b, L2_cond_w1, L2_cond_b1, L2_cond_w2, L2_cond_b2, L2_cond_w_ada, L2_cond_b_ada, L3_cond_W_qkv, L3_cond_b_qkv, L3_cond_W_proj, L3_cond_b_proj, L3_cond_W_fc1, L3_cond_b_fc1, L3_cond_W_fc2, L3_cond_b_fc2, L3_cond_W_ada, L3_cond_b_ada):
    import jax
    import jax.numpy as jnp

    def _L0_cond_ref(x, cond, P, W, b):
        import jax, jax.numpy as jnp
        import numpy as np
        from jax.scipy.linalg import expm
        N, D, COND_DIM = (288, 64, 288)
        B, T = (16, 256)

        def _rotation(cond, W, b):
            v = jax.nn.silu(cond) @ W.T + b
            iu, ju = jnp.triu_indices(D, k=1)
            A = jnp.zeros((cond.shape[0], D, D), dtype=v.dtype)
            A = A.at[:, iu, ju].set(v).at[:, ju, iu].set(-v)
            return expm(A)
        U, _ = jnp.linalg.qr(P)
        R = _rotation(cond, W, b)
        z = jnp.einsum('btn,nd->btd', x, U)
        z_rot = jnp.einsum('btd,bde->bte', z, R)
        x_rot = x + jnp.einsum('btd,nd->btn', z_rot - z, U)
        return x_rot

    def _L1_cond_ref(x, c, w_adaln, b_adaln, w_qkv, b_qkv, w_proj, b_proj, w_gate, w1, b1, w2, b2):
        import jax, jax.numpy as jnp
        import numpy as np
        NUM_HEADS = 16
        NUM_EXPERTS = 4
        TOP_K = 2
        LN_EPS = 1e-06

        def _ln(h):
            mu = jnp.mean(h, axis=-1, keepdims=True)
            var = jnp.var(h, axis=-1, keepdims=True)
            return (h - mu) * jax.lax.rsqrt(var + LN_EPS)

        def _modulate(h, shift, scale):
            return h * (1.0 + scale[:, None, :]) + shift[:, None, :]
        B, N, C = x.shape
        nh = NUM_HEADS
        hd = C // nh
        mod = jax.nn.silu(c) @ w_adaln + b_adaln
        sh_msa, sc_msa, g_msa, sh_mlp, sc_mlp, g_mlp = jnp.split(mod, 6, axis=-1)
        h = _modulate(_ln(x), sh_msa, sc_msa)
        qkv = (h @ w_qkv + b_qkv).reshape(B, N, 3, nh, hd).transpose(2, 0, 3, 1, 4)
        q, k, v = (qkv[0], qkv[1], qkv[2])
        attn = jax.nn.softmax(jnp.einsum('bhqd,bhkd->bhqk', q, k) * hd ** (-0.5), axis=-1)
        o = jnp.einsum('bhqk,bhkd->bhqd', attn, v).transpose(0, 2, 1, 3).reshape(B, N, C)
        o = o @ w_proj + b_proj
        x = x + g_msa[:, None, :] * o
        xn = _modulate(_ln(x), sh_mlp, sc_mlp)
        xf = xn.reshape(-1, C)
        gate_logits = xf @ w_gate
        topk_logits, topk_idx = jax.lax.top_k(gate_logits, TOP_K)
        gates = jax.nn.softmax(topk_logits, axis=-1)
        cw = jnp.sum(jax.nn.one_hot(topk_idx, NUM_EXPERTS, dtype=xf.dtype) * gates[..., None], axis=1)
        hmid = jax.nn.gelu(jnp.einsum('tc,ech->eth', xf, w1) + b1[:, None, :], approximate=True)
        eo = jnp.einsum('eth,ehc->etc', hmid, w2) + b2[:, None, :]
        moe = jnp.einsum('te,etc->tc', cw, eo).reshape(B, N, C)
        return x + g_mlp[:, None, :] * moe

    def _L2_cond_ref(x, c, w_qkv, b_qkv, w_proj, b_proj, qn_g, qn_b, kn_g, kn_b, w1, b1, w2, b2, w_ada, b_ada):
        import jax, jax.numpy as jnp
        import numpy as np
        HID = 288
        HEADS = 16
        HD = HID // HEADS
        MLP = int(HID * 4.0)

        def _ln(x, eps, gamma=None, beta=None):
            mu = jnp.mean(x, axis=-1, keepdims=True)
            var = jnp.mean(jnp.square(x - mu), axis=-1, keepdims=True)
            y = (x - mu) / jnp.sqrt(var + eps)
            if gamma is not None:
                y = y * gamma + beta
            return y
        B, N, C = x.shape
        H, hd = (HEADS, HD)
        scale = hd ** (-0.5)
        mod = jax.nn.silu(c) @ w_ada + b_ada
        sh_msa, sc_msa, g_msa, sh_mlp, sc_mlp, g_mlp = jnp.split(mod, 6, axis=1)
        xn = _ln(x, 1e-06)
        xn = xn * (1 + sc_msa[:, None, :]) + sh_msa[:, None, :]
        qkv = (xn @ w_qkv + b_qkv).reshape(B, N, 3, H, hd)
        q, k, v = (qkv[:, :, 0], qkv[:, :, 1], qkv[:, :, 2])
        q = _ln(q, 1e-05, qn_g, qn_b)
        k = _ln(k, 1e-05, kn_g, kn_b)
        attn = jnp.einsum('bqhd,bkhd->bhqk', q, k) * scale
        attn = jax.nn.softmax(attn, axis=-1)
        o = jnp.einsum('bhqk,bkhd->bqhd', attn, v).reshape(B, N, C)
        o = o @ w_proj + b_proj
        x = x + g_msa[:, None, :] * o
        xn2 = _ln(x, 1e-06)
        xn2 = xn2 * (1 + sc_mlp[:, None, :]) + sh_mlp[:, None, :]
        h = jax.nn.gelu(xn2 @ w1 + b1, approximate=False)
        m = h @ w2 + b2
        x = x + g_mlp[:, None, :] * m
        return x

    def _L3_cond_ref(x, c, W_qkv, b_qkv, W_proj, b_proj, W_fc1, b_fc1, W_fc2, b_fc2, W_ada, b_ada):
        import jax, jax.numpy as jnp
        import numpy as np
        B, L, C = (8, 256, 288)
        H = 16
        D = C // H
        FF = int(C * 4.0)
        EPS = 1e-06

        def _layernorm(x):
            mu = jnp.mean(x, axis=-1, keepdims=True)
            var = jnp.mean(jnp.square(x - mu), axis=-1, keepdims=True)
            return (x - mu) * jax.lax.rsqrt(var + EPS)

        def _modulate(x, shift, scale):
            return x * (1.0 + scale) + shift

        def _attention(h, W_qkv, b_qkv, W_proj, b_proj):
            b, l, c = h.shape
            qkv = h @ W_qkv + b_qkv
            qkv = qkv.reshape(b, l, 3, H, D)
            q, k, v = (qkv[:, :, 0], qkv[:, :, 1], qkv[:, :, 2])
            scale = D ** (-0.5)
            scores = jnp.einsum('blhd,bmhd->bhlm', q * scale, k)
            attn = jax.nn.softmax(scores, axis=-1)
            o = jnp.einsum('bhlm,bmhd->blhd', attn, v).reshape(b, l, c)
            return o @ W_proj + b_proj
        ada = jax.nn.silu(c) @ W_ada + b_ada
        shift_msa, scale_msa, gate_msa, shift_mlp, scale_mlp, gate_mlp = jnp.split(ada, 6, axis=-1)
        h = _modulate(_layernorm(x), shift_msa, scale_msa)
        x = x + gate_msa * _attention(h, W_qkv, b_qkv, W_proj, b_proj)
        h = _modulate(_layernorm(x), shift_mlp, scale_mlp)
        mlp = jax.nn.gelu(h @ W_fc1 + b_fc1, approximate=True) @ W_fc2 + b_fc2
        x = x + gate_mlp * mlp
        return x
    x = _L0_cond_ref(x, cond_1152, L0_cond_P, L0_cond_W, L0_cond_b)
    x = _L1_cond_ref(x, cond_1152, L1_cond_w_adaln, L1_cond_b_adaln, L1_cond_w_qkv, L1_cond_b_qkv, L1_cond_w_proj, L1_cond_b_proj, L1_cond_w_gate, L1_cond_w1, L1_cond_b1, L1_cond_w2, L1_cond_b2)
    x = _L2_cond_ref(x, cond_1152, L2_cond_w_qkv, L2_cond_b_qkv, L2_cond_w_proj, L2_cond_b_proj, L2_cond_qn_g, L2_cond_qn_b, L2_cond_kn_g, L2_cond_kn_b, L2_cond_w1, L2_cond_b1, L2_cond_w2, L2_cond_b2, L2_cond_w_ada, L2_cond_b_ada)
    x = _L3_cond_ref(x, cond_1152[:, None, :], L3_cond_W_qkv, L3_cond_b_qkv, L3_cond_W_proj, L3_cond_b_proj, L3_cond_W_fc1, L3_cond_b_fc1, L3_cond_W_fc2, L3_cond_b_fc2, L3_cond_W_ada, L3_cond_b_ada)
    return x

_drawn_inputs = setup_inputs


def setup_inputs(seed=0):
    import zlib

    import numpy as np

    out = dict(_drawn_inputs(seed))
    spreads = {'L1_cond_b_adaln': (0.0, 0.452),
     'L1_cond_b_qkv': (0.0, 0.8),
     'L1_cond_b_proj': (0.0, 0.381),
     'L1_cond_b1': (0.0, 0.8),
     'L1_cond_b2': (0.0, 0.517),
     'L2_cond_b_qkv': (0.0, 0.8),
     'L2_cond_b_proj': (0.0, 0.343),
     'L2_cond_qn_g': (1.0, 0.6),
     'L2_cond_qn_b': (0.0, 0.8),
     'L2_cond_kn_g': (1.0, 0.6),
     'L2_cond_kn_b': (0.0, 2.0),
     'L2_cond_b1': (0.0, 0.8),
     'L2_cond_b2': (0.0, 0.351),
     'L2_cond_b_ada': (0.0, 0.383),
     'L3_cond_b_qkv': (0.0, 0.8),
     'L3_cond_b_proj': (0.0, 0.356),
     'L3_cond_b_fc1': (0.0, 0.8),
     'L3_cond_b_fc2': (0.0, 0.347),
     'L3_cond_b_ada': (0.0, 0.374)}
    factors = {'L1_cond_w_qkv': 8.0,
     'L1_cond_w_proj': 5.8,
     'L1_cond_w_gate': 2.948,
     'L1_cond_w1': 2.854,
     'L1_cond_w2': 2.67,
     'L2_cond_w_qkv': 8.0,
     'L2_cond_w_proj': 5.136,
     'L3_cond_W_qkv': 7.793,
     'L3_cond_W_proj': 5.087,
     'L3_cond_W_fc1': 3.374}
    for name, (base, spread) in spreads.items():
        noise = np.random.default_rng([zlib.crc32(name.encode()), seed]).standard_normal(out[name].shape)
        drawn = base * np.exp(spread * noise) if base else spread * noise
        out[name] = jnp.asarray(drawn.astype(out[name].dtype))
    for name, factor in factors.items():
        out[name] = (out[name] * factor).astype(out[name].dtype)
    return out
```

```python
from contextlib import ExitStack, contextmanager
from itertools import count

import concourse.bass as bass
from concourse import mybir

F32 = mybir.dt.float32
F32R = mybir.dt.float32r
ACT = mybir.ActivationFunctionType
ALU = mybir.AluOpType
AX = mybir.AxisListType.X

P = 128
NB, SEQ, C = 2, 1024, 288
TOK = NB * SEQ
TILES = TOK // P
TPB = SEQ // P
NH, HD = 16, 18
HP = 32
QUADS = NH // 4
NQ = NB * QUADS
CH = 512
CPB = SEQ // CH
TPC = CH // P
FT = 3
CP = FT * P
TAIL = C - 2 * P
FF = 4 * C
KT = FF // P
NE = 4
RD = 64
SCALE = float(HD) ** -0.5
LN_EPS = 1e-6
QK_EPS = 1e-5
SCALINGS, TERMS = 5, 12
SUMCOL = HD


@contextmanager
def signals(nc, tag):
    made = []

    def make(name):
        made.append(nc.alloc_semaphore(tag + name))
        return made[-1]

    yield make
    nc.clear_and_free_semaphores(made)
    nc.all_engine_barrier()


def consts(nc, ctx, out):
    ident = ctx.enter_context(nc.sbuf_tensor("ident", [P, P], F32))
    blocks = ctx.enter_context(nc.sbuf_tensor("blocks", [P, P], F32))
    sumsel = ctx.enter_context(nc.sbuf_tensor("sumsel", [P, P], F32))
    eps = ctx.enter_context(nc.sbuf_tensor("eps", [P, 2], F32))
    made = ctx.enter_context(nc.semaphore("const_made"))
    with nc.Block() as block:

        @block.gpsimd
        def _(pool):
            pool.memset(ident[:, :], 0.0)
            pool.memset(sumsel[:, :], 0.0)
            pool.memset(eps[:, 0:1], LN_EPS)
            pool.memset(eps[:, 1:2], QK_EPS)
            pool.memset(blocks[:, :], 1.0 / HD).then_inc(made, 1)
            pool.wait_ge(made, 1)
            pool.affine_select(out=ident[:, :], in_=ident[:, :], compare_op=ALU.not_equal, fill=1.0,
                               base=0, pattern=[[-1, P]], channel_multiplier=1)
            v = sumsel[:, :].rearrange("p (a m) -> p a m", a=4)
            pool.affine_select(out=v, in_=v, compare_op=ALU.not_equal, fill=1.0,
                               base=-SUMCOL, pattern=[[-HP, 4], [0, HP]], channel_multiplier=1)
            b = blocks[:, :].rearrange("p (a m) -> p a m", a=4)
            pool.affine_select(out=b, in_=b, compare_op=ALU.is_ge, fill=0.0,
                               base=0, pattern=[[-HP, 4], [0, HP]], channel_multiplier=1).then_inc(made, 1)
            pool.wait_ge(made, 2)
            pool.affine_select(out=b, in_=b, compare_op=ALU.is_ge, fill=0.0,
                               base=HD - 1, pattern=[[HP, 4], [0, HP]], channel_multiplier=-1).then_inc(made, 1)
            pool.wait_ge(made, 3)
            pool.affine_select(out=b, in_=b, compare_op=ALU.is_ge, fill=0.0,
                               base=HD - 1, pattern=[[0, 4], [-1, HP]], channel_multiplier=0).then_inc(made, 1)
            pool.wait_ge(made, 4)

    center = ctx.enter_context(nc.sbuf_tensor("center", [P, P], F32))
    with nc.Block() as block:

        @block.vector
        def _(dve):
            dve.tensor_tensor(center[:, :], ident[:, :], blocks[:, :], ALU.subtract)

    out.update(ident=ident, blocks=blocks, sumsel=sumsel, eps=eps, center=center)


def condition(nc, ctx, d, k):
    silu = ctx.enter_context(nc.sbuf_tensor("siluT", [96, 3, NB], F32))
    fm = [ctx.enter_context(nc.sbuf_tensor(f"fm{l}", [P, FT, 4, NB], F32)) for l in range(3)]
    gate_scr = nc.dram_tensor("gate_scr", (3, 2, P, NB, C), F32, kind="Internal").ap()
    rot = ctx.enter_context(nc.sbuf_tensor("rot", [RD, NB, RD], F32))
    k.update(fm=fm, gate_scr=gate_scr, rot=rot)
    with ExitStack() as ph:
        sb = lambda n, s, dt=F32: ph.enter_context(nc.sbuf_tensor("c_" + n, s, dt))
        sem = ph.enter_context(signals(nc, "c_"))
        condT = sb("condT", [96, 3, NB])
        sig = sb("sig", [96, 3, NB])
        rep = sb("rep", [96, 3, NB, P])
        wfm = sb("wfm", [96, 2, 3, 4 * CP])
        wga = sb("wga", [96, 2, 3, 2 * C])
        bfm = sb("bfm", [P, 3, FT, 4])
        bga = sb("bga", [P, 3, 2, C])
        gates = [sb(f"gates{l}", [P, 2, NB, C]) for l in range(3)]
        wrot = sb("wrot", [96, 3, 2, 512])
        vrow = sb("vrow", [NB, RD * RD])
        brow = sb("brow", [NB, RD * RD])
        psf = ph.enter_context(nc.psum_tensor("c_psf", [P, 2, 512], F32))
        psg = ph.enter_context(nc.psum_tensor("c_psg", [P, 4, 512], F32))
        psv = ph.enter_context(nc.psum_tensor("c_psv", [P, 2, 512], F32))
        small, silu_done, sig_done, rep_done = sem("small"), sem("silu"), sem("sig"), sem("rep")
        ada = [sem(f"ada{p}") for p in range(2)]
        rw = [sem(f"rw{p}") for p in range(2)]
        mm_f, mm_g, mm_v, got_f, got_g, got_v, sent = (
            sem("mm_f"), sem("mm_g"), sem("mm_v"), sem("got_f"), sem("got_g"), sem("got_v"), sem("sent"))
        block = ph.enter_context(nc.Block())

        @block.sync
        def _(sp):
            sp.dma_start(condT[:, :, :], d["condT"].rearrange("(a p) b -> p a b", p=96)).then_inc(small, 16)
            sp.dma_start(brow[0:1, :], d["rot_b"]).then_inc(small, 16)
            sp.dma_start(brow[1:2, :], d["rot_b"]).then_inc(small, 16)
            for l in range(3):
                sp.dma_start(bfm[:, l, :, :], d[f"bfm{l}"]).then_inc(small, 16)
                sp.dma_start(bga[:, l, :, :], d[f"bga{l}"].partition_broadcast(P)).then_inc(small, 16)
            for l in range(3):
                if l == 2:
                    sp.wait_ge(mm_f, 1)
                    sp.wait_ge(mm_g, 4)
                sp.dma_start(wfm[:, l % 2, :, :], d[f"wfm{l}"].rearrange("(a p) n -> p a n", p=96)).then_inc(ada[l % 2], 16)
                sp.dma_start(wga[:, l % 2, :, :], d[f"wga{l}"].rearrange("(a p) n -> p a n", p=96)).then_inc(ada[l % 2], 16)
            sp.wait_ge(got_v, 8)
            for b in range(NB):
                sp.dma_start(rot[:, b, :], vrow[b:b + 1, :].rearrange("o (i j) -> o i j", i=RD)).then_inc(sent, 16)
            for l in range(3):
                sp.wait_ge(got_g, 4 * (l + 1))
                for g in range(2):
                    sp.dma_start(gate_scr[l, g], gates[l][:, g, :, :]).then_inc(sent, 16)
            sp.wait_ge(sent, 32 + 96)

        @block.gpsimd
        def _(pool):
            for j in range(8):
                if j >= 2:
                    pool.wait_ge(mm_v, j - 1)
                pool.dma_start(wrot[:, :, j % 2, :],
                               d["rot_w"][:, 512 * j:512 * j + 512].rearrange("(a p) n -> p a n", p=96)).then_inc(rw[j % 2], 16)

        @block.scalar
        def _(act):
            act.wait_ge(small, 16 * 9)
            act.activation(sig[:, :, :], condT[:, :, :], ACT.Sigmoid).then_inc(sig_done, 1)

        @block.vector
        def _(dve):
            dve.wait_ge(small, 16 * 9)
            dve.wait_ge(sig_done, 1)
            dve.tensor_tensor(silu[:, :, :], condT[:, :, :], sig[:, :, :], ALU.mult).then_inc(silu_done, 1)
            dve.wait_ge(silu_done, 1)
            dve.tensor_copy(rep[:, :, :, :], silu[:, :, :].unsqueeze(3).broadcast_to([96, 3, NB, P])).then_inc(rep_done, 1)
            for j in range(8):
                dve.wait_ge(mm_v, j + 1)
                dve.tensor_tensor(vrow[:, 512 * j:512 * j + 512], psv[0:NB, j % 2, :], brow[:, 512 * j:512 * j + 512],
                                  ALU.add).then_inc(got_v, 1)
            for l in range(3):
                dve.wait_ge(mm_f, l + 1)
                dve.tensor_tensor(fm[l][:, :, :, :], psf[:, l % 2, 0:FT * 4 * NB].rearrange("p (f m b) -> p f m b", f=FT, m=4),
                                  bfm[:, l, :, :].unsqueeze(3).broadcast_to([P, FT, 4, NB]), ALU.add).then_inc(got_f, 1)
                dve.wait_ge(got_f, 2 * l + 1)
                dve.tensor_scalar(fm[l][:, :, 1:4:2, :], fm[l][:, :, 1:4:2, :], 1.0, None, ALU.add).then_inc(got_f, 1)
                for g in range(2):
                    for b in range(NB):
                        n = 4 * l + 2 * g + b
                        dve.wait_ge(mm_g, n + 1)
                        dve.tensor_tensor(gates[l][:, g, b, :], psg[:, n % 4, 0:C], bga[:, l, g, :], ALU.add).then_inc(got_g, 1)

        @block.tensor
        def _(pe):
            pe.wait_ge(silu_done, 1)
            pe.wait_ge(rep_done, 1)
            for j in range(8):
                pe.wait_ge(rw[j % 2], 16 * (j // 2 + 1))
                if j >= 2:
                    pe.wait_ge(got_v, j - 1)
                for a in range(3):
                    mm = pe.matmul(psv[0:NB, j % 2, :], silu[:, a, :], wrot[:, a, j % 2, :], start=(a == 0), stop=(a == 2))
                mm.then_inc(mm_v, 1)
            for l in range(3):
                pe.wait_ge(ada[l % 2], 32 * (l // 2 + 1))
                if l >= 2:
                    pe.wait_ge(got_f, 1)
                for f in range(FT):
                    for m in range(4):
                        o = (f * 4 + m) * NB
                        for a in range(3):
                            mm = pe.matmul(psf[:, l % 2, o:o + NB], wfm[:, l % 2, a, m * CP + f * P:m * CP + f * P + P],
                                           silu[:, a, :], start=(a == 0), stop=(a == 2))
                mm.then_inc(mm_f, 1)
                for g in range(2):
                    for b in range(NB):
                        n = 4 * l + 2 * g + b
                        if n >= 4:
                            pe.wait_ge(got_g, n - 3)
                        for a in range(3):
                            mm = pe.matmul(psg[:, n % 4, 0:C], rep[:, a, b, :], wga[:, l % 2, a, g * C:g * C + C],
                                           start=(a == 0), stop=(a == 2))
                        mm.then_inc(mm_g, 1)


QR_UNROLL = 8


def rotate(nc, d, k, x):
    ident, rot = k["ident"], k["rot"]
    W = C
    with ExitStack() as ph:
        sb = lambda n, s, dt=F32: ph.enter_context(nc.sbuf_tensor("r_" + n, s, dt))
        sem = ph.enter_context(signals(nc, "r_"))
        pT = sb("pT", [RD, C])
        A = sb("A", [P, C + RD])
        sel = sb("sel", [P, P])
        scr = sb("scr", [P, C])
        scr2 = sb("scr2", [P, C])
        sc = sb("sc", [P, 16])
        xT = sb("xT", [96, 3, TOK])
        skew = sb("skew", [RD, 4, RD])
        ex = sb("ex", [RD, 2, 4, RD])
        N1 = sb("N1", [RD, 2, RD])
        N1T = sb("N1T", [RD, 2, RD])
        ZT = sb("ZT", [RD, 2, RD])
        rinv = sb("rinv", [RD, RD])
        U = sb("U", [96, 3, RD])
        UT = sb("UT", [RD, C])
        RmI = sb("RmI", [RD, NB, RD])
        W2 = sb("W2", [RD, NB, C])
        zT = sb("zT", [RD, TOK])
        psR = ph.enter_context(nc.psum_tensor("r_psR", [P, 512], F32))
        psQ = ph.enter_context(nc.psum_tensor("r_psQ", [P, 512], F32))
        psE = ph.enter_context(nc.psum_tensor("r_psE", [P, 512], F32))
        psN = ph.enter_context(nc.psum_tensor("r_psN", [P, 3, 512], F32))
        psZ = ph.enter_context(nc.psum_tensor("r_psZ", [P, 2, 512], F32))
        loaded, xloaded, dv, row, row2, sel_ok, nsq_ok, nrm_ok, upd, mm, dd, xo = (
            sem("loaded"), sem("xloaded"), sem("dve_self"), sem("row"), sem("row2"), sem("sel"), sem("nsq"), sem("nrm"),
            sem("updated"), sem("mm"), sem("dve_done"), sem("x_out"))
        block = ph.enter_context(nc.Block())

        @block.sync
        def _(sp):
            sp.dma_start(pT[:, :], d["PT"]).then_inc(loaded, 16)
            sp.dma_start(x[:, :, :], d["x"].rearrange("(t p) c -> p t c", p=P)).then_inc(xloaded, 16)
            sp.dma_start(xT[:, :, :], d["xT"].rearrange("(a p) n -> p a n", p=96)).then_inc(xloaded, 16)

        SELF = 9

        @block.gpsimd
        def _(pool):
            pool.memset(sel[:, :], 1.0).then_inc(sel_ok, 1)
            pool.wait_ge(sel_ok, 1)
            with pool.Fori(0, RD) as s:
                pool.wait_ge(row2, s + 1)
                pool.tensor_copy(sel[:, :], ident[:, bass.ds(s, 1)].broadcast_to([P, P])).then_inc(sel_ok, 1)
            pool.wait_ge(upd, RD + 1)
            pool.wait_ge(dv, 1 + SELF * RD)
            pool.affine_select(out=N1[:, 0, :], in_=A[0:RD, 0:RD], compare_op=ALU.is_gt, fill=0.0,
                               base=0, pattern=[[-1, RD]], channel_multiplier=1).then_inc(xo, 1)

        @block.scalar
        def _(act):
            with act.Fori(0, RD // QR_UNROLL) as i:
                for u in range(QR_UNROLL):
                    s = i * QR_UNROLL + u
                    act.wait_ge(row2, s + 2)
                    act.activation(scr2[:, :], psQ[:, 0:W], ACT.Square, accum_out=sc[:, 0:1]).then_inc(nsq_ok, 1)
                    act.wait_ge(nsq_ok, s + 1)
                    act.activation(sc[:, 1:2], sc[:, 0:1], ACT.Sqrt).then_inc(nrm_ok, 1)

        @block.vector
        def _(dve):
            dve.memset(A[:, :], 0.0).then_inc(dv, 1)
            dve.wait_ge(loaded, 16)
            dve.wait_ge(dv, 1)
            dve.tensor_copy(A[0:RD, 0:C], pT[:, :]).then_inc(upd, 1)
            with dve.Fori(0, RD // QR_UNROLL) as i:
                for u in range(QR_UNROLL):
                    s = i * QR_UNROLL + u
                    before = s * SELF + 1
                    a = A[:, bass.ds(s, W)]
                    akk = A[:, bass.ds(s, 1)]
                    dve.wait_ge(row, s + 1)
                    dve.scalar_tensor_tensor(out=scr[:, :], in0=psR[:, 0:W], scalar=1.0, in1=a,
                                             op0=ALU.mult, op1=ALU.mult, accum_out=sc[:, 2:3]).then_inc(dv, 1)
                    dve.tensor_copy(sc[:, 3:4], psR[:, 0:1]).then_inc(dv, 1)
                    dve.tensor_scalar(sc[:, 4:5], psR[:, 0:1], 0.0, 2.0, ALU.is_ge, ALU.mult).then_inc(dv, 1)
                    dve.wait_ge(nrm_ok, s + 1)
                    dve.wait_ge(dv, before + 3)
                    dve.tensor_scalar(sc[:, 5:6], sc[:, 4:5], 1.0, sc[:, 1:2], ALU.subtract, ALU.mult).then_inc(dv, 1)
                    dve.wait_ge(dv, before + 4)
                    dve.tensor_scalar(sc[:, 6:7], sc[:, 3:4], sc[:, 5:6], sc[:, 0:1], ALU.mult, ALU.add).then_inc(dv, 1)
                    dve.tensor_scalar(sc[:, 7:8], akk, sc[:, 5:6], sc[:, 2:3], ALU.mult, ALU.add).then_inc(dv, 1)
                    dve.wait_ge(dv, before + 6)
                    dve.reciprocal(sc[:, 8:9], sc[:, 6:7]).then_inc(dv, 1)
                    dve.wait_ge(dv, before + 7)
                    dve.tensor_scalar(sc[:, 9:10], sc[:, 7:8], sc[:, 8:9], -1.0, ALU.mult, ALU.mult).then_inc(dv, 1)
                    dve.wait_ge(dv, before + 8)
                    dve.scalar_tensor_tensor(out=a, in0=psR[:, 0:W], scalar=sc[:, 9:10], in1=a,
                                             op0=ALU.mult, op1=ALU.add).then_inc(upd, 1)
                    dve.wait_ge(upd, s + 2)
                    dve.tensor_scalar(akk, sc[:, 9:10], sc[:, 5:6], akk, ALU.mult, ALU.add).then_inc(dv, 1)
                    dve.wait_ge(dv, before + 9)

            done = count(1)

            f = 1.0 / 2 ** SCALINGS
            dve.wait_ge(mm, 1)
            for b in range(NB):
                dve.tensor_tensor(skew[:, 2 * b, :], rot[:, b, :], psE[0:RD, b * RD:(b + 1) * RD], ALU.subtract).then_inc(dd, 1)
                dve.wait_ge(dd, next(done))
                dve.tensor_scalar(skew[:, 2 * b + 1, :], skew[:, 2 * b, :], -f, None, ALU.mult).then_inc(dd, 1)
                dve.wait_ge(dd, next(done))
                dve.tensor_scalar(skew[:, 2 * b, :], skew[:, 2 * b, :], f, None, ALU.mult).then_inc(dd, 1)
                dve.wait_ge(dd, next(done))
                for j in range(2):
                    dve.tensor_copy(ex[:, 0, 2 * b + j, :], ident[0:RD, 0:RD]).then_inc(dd, 1)
                    dve.wait_ge(dd, next(done))
            q = 0
            idb = ident[0:RD, 0:RD].unsqueeze(1).broadcast_to([RD, 4, RD])
            for t in range(TERMS, 0, -1):
                dve.wait_ge(mm, 2 + q)
                dve.scalar_tensor_tensor(out=ex[:, 1 - q % 2, :, :], in0=psE[0:RD, 0:4 * RD].rearrange("p (a n) -> p a n", a=4),
                                         scalar=1.0 / t, in1=idb, op0=ALU.mult, op1=ALU.add).then_inc(dd, 1)
                dve.wait_ge(dd, next(done))
                q += 1
            for t in range(SCALINGS):
                dve.wait_ge(mm, 2 + q)
                dve.tensor_copy(ex[:, 1 - q % 2, :, :], psE[0:RD, 0:4 * RD].rearrange("p (a n) -> p a n", a=4)).then_inc(dd, 1)
                dve.wait_ge(dd, next(done))
                q += 1
            for b in range(NB):
                dve.tensor_tensor(RmI[:, b, :], ex[:, q % 2, 2 * b + 1, :], ident[0:RD, 0:RD], ALU.subtract).then_inc(dd, 1)
                dve.wait_ge(dd, next(done))
            dve.tensor_tensor(scr[0:RD, 0:RD], A[0:RD, 0:RD], ident[0:RD, 0:RD], ALU.mult).then_inc(dd, 1)
            dve.wait_ge(dd, next(done))
            dve.tensor_reduce(sc[0:RD, 10:11], scr[0:RD, 0:RD], AX, ALU.add).then_inc(dd, 1)
            dve.wait_ge(dd, next(done))
            dve.reciprocal(sc[0:RD, 11:12], sc[0:RD, 10:11]).then_inc(dd, 1)
            dve.wait_ge(dd, next(done))
            dve.wait_ge(xo, 1)
            dve.tensor_scalar(N1[:, 0, :], N1[:, 0, :], sc[0:RD, 11:12], -1.0, ALU.mult, ALU.mult).then_inc(dd, 1)
            dve.wait_ge(dd, next(done))
            m0 = 2 + q
            dve.wait_ge(mm, m0)
            dve.tensor_copy(N1T[:, 0, :], psN[0:RD, 0, 0:RD]).then_inc(dd, 1)
            dve.wait_ge(dd, next(done))
            dve.tensor_tensor(ZT[:, 0, :], N1T[:, 0, :], ident[0:RD, 0:RD], ALU.add).then_inc(dd, 1)
            dve.wait_ge(dd, next(done))
            for s in range(1, 6):
                c, o = s % 2, 1 - s % 2
                dve.wait_ge(mm, m0 + 2 * s - 1)
                dve.tensor_copy(N1[:, c, :], psN[0:RD, 0, 0:RD]).then_inc(dd, 1)
                dve.wait_ge(dd, next(done))
                dve.tensor_copy(N1T[:, c, :], psN[0:RD, 1, 0:RD]).then_inc(dd, 1)
                dve.wait_ge(dd, next(done))
                dve.wait_ge(mm, m0 + 2 * s)
                dve.tensor_tensor(ZT[:, c, :], ZT[:, o, :], psN[0:RD, 2, 0:RD], ALU.add).then_inc(dd, 1)
                dve.wait_ge(dd, next(done))
            dve.tensor_scalar(rinv[:, :], ZT[:, 1, :], sc[0:RD, 11:12], None, ALU.mult).then_inc(dd, 1)
            dve.wait_ge(dd, next(done))
            m1 = m0 + 11
            dve.wait_ge(mm, m1)
            dve.tensor_copy(U[:, :, :], psN[0:96, 0, 0:3 * RD].rearrange("p (a n) -> p a n", a=3)).then_inc(dd, 1)
            dve.wait_ge(dd, next(done))
            dve.tensor_copy(UT[:, :], psN[0:RD, 1, 0:C]).then_inc(dd, 1)
            dve.wait_ge(dd, next(done))
            dve.wait_ge(mm, m1 + 1)
            dve.tensor_copy(W2[:, :, :], psN[0:RD, 1:3, 0:C]).then_inc(dd, 1)
            dve.wait_ge(dd, next(done))
            for c in range(TOK // CH):
                dve.wait_ge(mm, m1 + 2 + c)
                dve.tensor_copy(zT[:, c * CH:(c + 1) * CH], psZ[0:RD, c % 2, :]).then_inc(dd, 1)
                dve.wait_ge(dd, next(done))
            dve.wait_ge(xloaded, 32)
            for t in range(TILES):
                dve.wait_ge(mm, m1 + 6 + t)
                dve.tensor_tensor(x[:, t, :], x[:, t, :], psZ[:, t % 2, 0:C], ALU.add).then_inc(dd, 1)
                dve.wait_ge(dd, next(done))

        @block.tensor
        def _(pe):
            pe.wait_ge(sel_ok, 1)
            pe.sem_inc(row2, 1)
            with pe.Fori(0, RD) as s:
                pe.wait_ge(sel_ok, s + 2)
                pe.wait_ge(upd, s + 1)
                pe.matmul(psR[:, 0:W], sel[:, :], A[:, bass.ds(s, W)], start=True, stop=True).then_inc(row, 1)
                pe.matmul(psQ[:, 0:W], sel[:, :], A[:, bass.ds(s, W)], start=True, stop=True).then_inc(row2, 1)
            for b in range(NB):
                t = pe.transpose(psE[0:RD, b * RD:(b + 1) * RD], rot[:, b, :], ident[0:RD, 0:RD])
            t.then_inc(mm, 1)
            after = 5 * NB
            q = 0
            for t in range(TERMS):
                pe.wait_ge(dd, after + q)
                for j in range(4):
                    m = pe.matmul(psE[0:RD, j * RD:(j + 1) * RD], skew[:, j ^ 1, :], ex[:, q % 2, j, :], start=True, stop=True)
                m.then_inc(mm, 1)
                q += 1
            for t in range(SCALINGS):
                pe.wait_ge(dd, after + q)
                for j in range(4):
                    m = pe.matmul(psE[0:RD, j * RD:(j + 1) * RD], ex[:, q % 2, j ^ 1, :], ex[:, q % 2, j, :], start=True, stop=True)
                m.then_inc(mm, 1)
                q += 1
            after += q + NB + 3 + 1
            pe.wait_ge(dd, after)
            pe.transpose(psN[0:RD, 0, 0:RD], N1[:, 0, :], ident[0:RD, 0:RD]).then_inc(mm, 1)
            after += 2
            for s in range(1, 6):
                c, o = s % 2, 1 - s % 2
                pe.wait_ge(dd, after)
                pe.matmul(psN[0:RD, 0, 0:RD], N1T[:, o, :], N1[:, o, :], start=True, stop=True)
                pe.matmul(psN[0:RD, 1, 0:RD], N1[:, o, :], N1T[:, o, :], start=True, stop=True).then_inc(mm, 1)
                pe.wait_ge(dd, after + 2)
                pe.matmul(psN[0:RD, 2, 0:RD], N1[:, c, :], ZT[:, o, :], start=True, stop=True).then_inc(mm, 1)
                after += 3
            after += 1
            pe.wait_ge(dd, after)
            for a in range(3):
                pe.matmul(psN[0:96, 0, a * RD:(a + 1) * RD], pT[:, a * 96:(a + 1) * 96], rinv[:, :], start=True, stop=True)
            pe.matmul(psN[0:RD, 1, 0:C], rinv[:, :], pT[:, :], start=True, stop=True).then_inc(mm, 1)
            after += 2
            pe.wait_ge(dd, after)
            for b in range(NB):
                m = pe.matmul(psN[0:RD, 1 + b, 0:C], RmI[:, b, :], UT[:, :], start=True, stop=True)
            m.then_inc(mm, 1)
            after += 1
            pe.wait_ge(xloaded, 32)
            for c in range(TOK // CH):
                if c >= 2:
                    pe.wait_ge(dd, after + c - 1)
                for a in range(3):
                    m = pe.matmul(psZ[0:RD, c % 2, :], U[:, a, :], xT[:, a, c * CH:(c + 1) * CH], start=(a == 0), stop=(a == 2))
                m.then_inc(mm, 1)
            after += TOK // CH
            pe.wait_ge(dd, after)
            for t in range(TILES):
                if t >= 2:
                    pe.wait_ge(dd, after + t - 1)
                pe.matmul(psZ[:, t % 2, 0:C], zT[:, t * P:(t + 1) * P], W2[:, t // TPB, :], start=True, stop=True).then_inc(mm, 1)


class Prep:

    def __init__(self, nc, ph, sem, k, l, which, x, tag):
        sb = lambda n, s, dt=F32: ph.enter_context(nc.sbuf_tensor(tag + n, s, dt))
        self.k, self.x, self.which, self.l = k, x, which, l
        self.stats = sb("stats", [P, TPB, 6])
        self.mv = sb("mv", [P, TPB, 2])
        self.std = sb("std", [P, TPB])
        self.rstd = sb("rstd", [P, TPB])
        self.mod = sb("mod", [P, FT, 2])
        self.xn = sb("xn", [P, CPB, TPC, CP])
        self.y = sb("y", [P, CPB, FT, CH])
        self.psT = ph.enter_context(nc.psum_tensor(tag + "psT", [P, FT, CH], F32))
        self.s_mv, self.s_std, self.s_self, self.s_xn, self.s_T, self.s_y, self.s_h, self.s_l, self.s_xl = (
            sem("mv"), sem("std"), sem("norm_self"), sem("xn"), sem("T"), sem("y"), sem("h"), sem("l"), sem("xl"))

    SELF = 3

    def normalise(self, dve, i):
        dve.wait_ge(self.s_y, i * CPB + 1)
        for t in range(TPB):
            r = dve.bn_stats(self.stats[:, t, :], self.x[:, bass.ds(i * TPB + t, 1), :].rearrange("p o c -> p (o c)"))
        r.then_inc(self.s_self, 1)
        dve.wait_ge(self.s_self, i * self.SELF + 1)
        b = 2 * self.which
        dve.tensor_copy(self.mod[:, :, :],
                        self.k["fm"][self.l][:, :, b:b + 2, bass.ds(i, 1)].rearrange("p f m o -> p f (m o)")).then_inc(self.s_self, 1)
        for t in range(TPB):
            r = dve.bn_aggr(self.mv[:, t, :], self.stats[:, t, :])
        r.then_inc(self.s_mv, 1)
        dve.wait_ge(self.s_std, i + 1)
        dve.reciprocal(self.rstd[:, :], self.std[:, :]).then_inc(self.s_self, 1)
        dve.wait_ge(self.s_self, i * self.SELF + 3)
        for c in range(CPB):
            for t in range(TPC):
                g = c * TPC + t
                xs = self.x[:, bass.ds(i * TPB + g, 1), :].rearrange("p o c -> p (o c)")
                dve.tensor_scalar(self.xn[:, c, t, 0:C], xs, self.mv[:, g, 0:1], self.rstd[:, g:g + 1],
                                  ALU.subtract, ALU.mult)
                r = dve.tensor_scalar(self.xn[:, c, t, C:CP].rearrange("p (a m) -> p a m", a=3),
                                      xs[:, 2 * P:C].unsqueeze(1).broadcast_to([P, 3, TAIL]),
                                      self.mv[:, g, 0:1], self.rstd[:, g:g + 1], ALU.subtract, ALU.mult)
            r.then_inc(self.s_xn, 1)

    def modulate(self, dve, i, c):
        dve.wait_ge(self.s_T, i * CPB + c + 1)
        dve.wait_ge(self.s_l, i * CPB + c + 1)
        for f in range(FT):
            r = dve.tensor_scalar(self.y[:, c, f, :], self.psT[:, f, :], self.mod[:, f, 1:2], self.mod[:, f, 0:1],
                                  ALU.mult, ALU.add)
        r.then_inc(self.s_y, 1)

    def deviation(self, act, i):
        act.wait_ge(self.s_mv, i + 1)
        act.activation(self.std[:, :], self.mv[:, :, 1], ACT.Sqrt, bias=self.k["eps"][:, 0:1]).then_inc(self.s_std, 1)

    def high(self, act, i, c, XH, X8):
        act.wait_ge(self.s_y, i * CPB + c + 2)
        act.activation(XH, self.y[:, c, 0:2, :], ACT.Copy)
        act.activation(X8, self.y[:, c, 2, :], ACT.Copy).then_inc(self.s_h, 1)

    def low(self, pool, i, c, XH, XL, X8):
        pool.wait_ge(self.s_h, i * CPB + c + 1)
        pool.wait_ge(self.s_l, i * CPB + c + CPB)
        pool.tensor_tensor(XL, self.y[:, c, 0:2, :], XH.bitcast(F32), ALU.subtract).then_inc(self.s_xl, 1)
        pool.wait_ge(self.s_xl, i * CPB + c + 1)
        pool.tensor_tensor(X8[64:P], self.y[64:P, c, 2, :], X8[64:P].bitcast(F32), ALU.subtract).then_inc(self.s_l, 1)

    def transpose(self, pe, i, c):
        pe.wait_ge(self.s_xn, i * CPB + c + 1)
        pe.wait_ge(self.s_y, i * CPB + c + 1)
        for f in range(FT):
            for t in range(TPC):
                r = pe.transpose(self.psT[:, f, t * P:(t + 1) * P], self.xn[:, c, t, f * P:(f + 1) * P], self.k["ident"][:, :])
        r.then_inc(self.s_T, 1)


def project_qkv(nc, d, k, l, x, qk_scr, v_scr):
    norm = l == 1
    RING = 2 if norm else 4
    NQK = 2 * QUADS
    NM, NV = CPB * NQK, CPB * TPC
    MM0 = NM + NV
    with ExitStack() as ph:
        tag = f"q{l}_"
        sb = lambda n, s, dt=F32: ph.enter_context(nc.sbuf_tensor(tag + n, s, dt))
        sem = ph.enter_context(signals(nc, tag))
        prep = Prep(nc, ph, sem, k, l, 0, x, tag)
        NW = NQK * P + QUADS * P
        raw = sb("raw", [P, FT, NW])
        WH = sb("WH", [P, 2, NW], F32R)
        WL = sb("WL", [P, 2, NW], F32R)
        W8 = sb("W8", [P, NW], F32R)
        XH = sb("XH", [P, CPB, 2, CH], F32R)
        XL = sb("XL", [P, CPB, 2, CH], F32R)
        X8 = sb("X8", [P, CPB, CH], F32R)
        bqk = sb("bqk", [P, NQK])
        bv = sb("bv", [P, CH])
        hst = sb("hst", [P, 4, CH], F32R)
        lst = sb("lst", [P, 4, CH], F32R)
        vst = sb("vst", [P, 2, CH])
        ps = ph.enter_context(nc.psum_tensor(tag + "ps", [P, RING, CH], F32))
        if norm:
            psC = ph.enter_context(nc.psum_tensor(tag + "psC", [P, 2, CH], F32))
            psV = ph.enter_context(nc.psum_tensor(tag + "psV", [P, CH], F32))
            gb = sb("gb", [P, 4])
            praw = sb("praw", [P, 2, CH])
            sq = sb("sq", [P, CH])
            sdev = sb("sdev", [P, CH])
            rdev = sb("rdev", [P, CH])
            qn = sb("qn", [P, 2, CH])
            qy = sb("qy", [P, 2, CH])
            p_raw, p_cen, p_sq, p_var, p_dev, p_rdev, p_qn, p_y = (
                sem("p_raw"), sem("p_cen"), sem("p_sq"), sem("p_var"), sem("p_dev"), sem("p_rdev"),
                sem("p_qn"), sem("p_y"))
        small, w_in, w_h, w_l, mm, out_h, out_l, freed = (
            sem("small"), sem("w_in"), sem("w_h"), sem("w_l"), sem("mm"), sem("out_h"), sem("out_l"),
            sem("freed"))
        sent = [sem(f"sent{n}") for n in range(4)]
        vsent = [sem(f"vsent{n}") for n in range(2)]
        block = ph.enter_context(nc.Block())

        use = lambda i, c, w: i * (NM + NV) + c * (NQK + TPC) + w
        tile = lambda i, c, n: i * NM + c * NQK + n

        def slot_free(eng, i, c, n):
            g = c * NQK + n
            eng.wait_ge(sent[g % 4], (i * (NM // 4) + g // 4 + 1) * 32)

        @block.sync
        def _(sp):
            sp.dma_start(raw[:, :, :], d[f"wqkv{l}"]).then_inc(w_in, 16)
            sp.dma_start(bqk[:, :], d[f"bqk{l}"]).then_inc(small, 16)
            sp.dma_start(bv[:, :], d[f"bv{l}"].partition_broadcast(P)).then_inc(small, 16)
            if norm:
                sp.dma_start(gb[:, :], d["qkn"]).then_inc(small, 16)
            for s in sent:
                sp.sem_inc(s, 32)
            for s in vsent:
                sp.sem_inc(s, 16)
            with sp.Fori(0, NB) as i:
                for c in range(CPB):
                    for t in range(TPC):
                        sp.wait_ge(freed, use(i, c, t) + RING + 1)
                        sp.dma_start(v_scr[bass.ds(i * QUADS, QUADS), c * TPC + t, :, :].rearrange("q p c -> p q c"),
                                     vst[:, t % 2, :].rearrange("p (q c) -> p q c", q=QUADS)).then_inc(vsent[t % 2], 16)
                    for n in range(NQK):
                        if norm:
                            sp.wait_ge(out_l, tile(i, c, n) + 3)
                        else:
                            sp.wait_ge(freed, use(i, c, TPC + n) + RING + 1)
                        for part, st in ((0, hst), (1, lst)):
                            dst = qk_scr[part, n // QUADS, bass.ds(i * QUADS + n % QUADS, 1), :, c * CH:(c + 1) * CH]
                            sp.dma_start(dst.rearrange("o p c -> p (o c)"),
                                         st[:, n % 4, :].bitcast(F32)).then_inc(sent[n % 4], 16)
            for s in sent:
                sp.wait_ge(s, 32 * (NB * NM // 4 + 1))
            for s in vsent:
                sp.wait_ge(s, 16 * (NB * NV // 2 + 1))

        @block.gpsimd
        def _(pool):
            pool.sem_inc(prep.s_l, CPB)
            pool.wait_ge(w_h, 1)
            pool.tensor_tensor(WL[:, :, :], raw[:, 0:2, :], WH[:, :, :].bitcast(F32), ALU.subtract).then_inc(w_l, 1)
            for n, b in enumerate((1, 3)):
                pool.wait_ge(w_l, n + 1)
                pool.tensor_tensor(W8[32 * b:32 * b + 32, :], raw[32 * b:32 * b + 32, 2, :],
                                   W8[32 * b:32 * b + 32, :].bitcast(F32), ALU.subtract).then_inc(w_l, 1)
            pool.wait_ge(w_l, 3)
            with pool.Fori(0, NB) as i:
                for c in range(CPB):
                    prep.low(pool, i, c, XH[:, c, :, :], XL[:, c, :, :], X8[:, c, :])

        @block.scalar
        def _(act):
            act.sem_inc(out_h, 2)
            if norm:
                act.sem_inc(p_dev, 1)
            act.wait_ge(w_in, 16)
            act.activation(WH[:, :, :], raw[:, 0:2, :], ACT.Copy)
            act.activation(W8[:, :], raw[:, 2, :], ACT.Copy).then_inc(w_h, 1)
            act.wait_ge(small, 48 if norm else 32)
            with act.Fori(0, NB) as i:
                prep.deviation(act, i)
                for c in range(CPB):
                    act.wait_ge(mm, use(i, c + 1, 0))
                    prep.high(act, i, c, XH[:, c, :, :], X8[:, c, :])
                for c in range(CPB):
                    for n in range(NQK if not norm else NQK + 3):
                        if not norm:
                            act.wait_ge(mm, use(i, c, TPC + n) + 1 + MM0)
                            slot_free(act, i, c, n)
                            act.activation(hst[:, n % 4, :], ps[:, (TPC + n) % RING, :], ACT.Identity,
                                           bias=bqk[:, n:n + 1]).then_inc(out_h, 1)
                            continue
                        if 1 <= n <= NQK:
                            g = tile(i, c, n - 1)
                            act.wait_ge(p_cen, g + 3)
                            act.wait_ge(p_var, g + 1)
                            act.activation(sq[:, :], psC[:, (n - 1) % 2, :], ACT.Square).then_inc(p_sq, 1)
                        if 2 <= n <= NQK + 1:
                            g = tile(i, c, n - 2)
                            act.wait_ge(p_var, g + 2)
                            act.wait_ge(p_rdev, g + 1)
                            act.activation(sdev[:, :], psV[:, :], ACT.Sqrt, bias=k["eps"][:, 1:2]).then_inc(p_dev, 1)
                        if n >= 3:
                            g, m = tile(i, c, n - 3), n - 3
                            w = 2 * (m // QUADS)
                            act.wait_ge(p_qn, g + 3)
                            slot_free(act, i, c, m)
                            act.activation(hst[:, m % 4, :], qn[:, m % 2, :], ACT.Identity,
                                           bias=gb[:, w + 1:w + 2], scale=gb[:, w:w + 1]).then_inc(out_h, 1)

        @block.vector
        def _(dve):
            dve.sem_inc(prep.s_y, 1)
            dve.sem_inc(freed, RING)
            if norm:
                dve.sem_inc(out_l, 2)
                dve.sem_inc(p_rdev, 1)
                dve.sem_inc(p_qn, 2)
            dve.wait_ge(small, 48 if norm else 32)
            with dve.Fori(0, NB) as i:
                prep.normalise(dve, i)
                for c in range(CPB):
                    prep.modulate(dve, i, c)
                for c in range(CPB):
                    for t in range(TPC):
                        dve.wait_ge(mm, use(i, c, t) + 1 + MM0)
                        dve.wait_ge(vsent[t % 2], (i * (NV // 2) + (c * TPC + t) // 2 + 1) * 16)
                        dve.tensor_tensor(vst[:, t % 2, :], ps[:, t % RING, :], bv[:, :], ALU.add).then_inc(freed, 1)
                    for n in range(NQK if not norm else NQK + 3):
                        if not norm:
                            dve.wait_ge(out_h, tile(i, c, n) + 3)
                            dve.wait_ge(mm, use(i, c, TPC + n) + 1 + MM0)
                            slot_free(dve, i, c, n)
                            dve.scalar_tensor_tensor(out=lst[:, n % 4, :], in0=ps[:, (TPC + n) % RING, :],
                                                     scalar=bqk[:, n:n + 1], in1=hst[:, n % 4, :].bitcast(F32),
                                                     op0=ALU.add, op1=ALU.subtract).then_inc(freed, 1)
                            continue
                        if n < NQK:
                            dve.wait_ge(mm, use(i, c, TPC + n) + 1 + MM0)
                            dve.wait_ge(p_cen, tile(i, c, n) + 1)
                            dve.tensor_scalar(praw[:, n % 2, :], ps[:, (TPC + n) % RING, :], bqk[:, n:n + 1], None,
                                              ALU.add).then_inc(freed, 1)
                        if 2 <= n <= NQK + 1:
                            g, m = tile(i, c, n - 2), n - 2
                            w = 2 * (m // QUADS)
                            dve.wait_ge(p_dev, g + 2)
                            dve.wait_ge(p_qn, g + 2)
                            dve.reciprocal(rdev[:, :], sdev[:, :]).then_inc(p_rdev, 1)
                            dve.wait_ge(p_rdev, g + 2)
                            dve.wait_ge(out_h, g + 1)
                            dve.tensor_tensor(qn[:, m % 2, :], psC[:, m % 2, :], rdev[:, :], ALU.mult).then_inc(p_qn, 1)
                            dve.wait_ge(p_qn, g + 3)
                            dve.wait_ge(out_l, g + 1)
                            dve.tensor_scalar(qy[:, m % 2, :], qn[:, m % 2, :], gb[:, w:w + 1], gb[:, w + 1:w + 2],
                                              ALU.mult, ALU.add).then_inc(p_y, 1)
                        if n >= 3:
                            g, m = tile(i, c, n - 3), n - 3
                            dve.wait_ge(out_h, g + 3)
                            dve.wait_ge(p_y, g + 1)
                            slot_free(dve, i, c, m)
                            dve.tensor_tensor(lst[:, m % 4, :], qy[:, m % 2, :], hst[:, m % 4, :].bitcast(F32),
                                              ALU.subtract).then_inc(out_l, 1)

        @block.tensor
        def _(pe):
            pe.sem_inc(mm, MM0)
            if norm:
                pe.sem_inc(p_cen, 2)
                pe.sem_inc(p_var, 1)
            pe.wait_ge(w_h, 1)
            pe.wait_ge(w_l, 3)
            with pe.Fori(0, NB) as i:
                for c in range(CPB):
                    prep.transpose(pe, i, c)
                for c in range(CPB):
                    pe.wait_ge(prep.s_l, i * CPB + c + 1 + CPB)
                    pe.wait_ge(prep.s_h, i * CPB + c + 1)
                    for t in range(TPC):
                        pe.wait_ge(freed, use(i, c, t) + 1)
                        cols = slice(t * P, (t + 1) * P)
                        vw = slice(NQK * P, NW)
                        terms = [(x_[:, c, f, cols], w_[:, f, vw]) for x_, w_ in ((XH, WH), (XL, WH), (XH, WL)) for f in range(2)]
                        terms.append((X8[:, c, cols], W8[:, vw]))
                        for a, (lhs, rhs) in enumerate(terms):
                            r = pe.matmul(ps[:, t % RING, :], lhs, rhs, start=(a == 0), stop=(a == 6))
                        r.then_inc(mm, 1)
                    for n in range(NQK if not norm else NQK + 2):
                        if n < NQK:
                            pe.wait_ge(freed, use(i, c, TPC + n) + 1)
                            cols = slice(n * P, (n + 1) * P)
                            terms = [(w_[:, f, cols], x_[:, c, f, :]) for x_, w_ in ((XH, WH), (XL, WH), (XH, WL)) for f in range(2)]
                            terms.append((W8[:, cols], X8[:, c, :]))
                            for a, (lhs, rhs) in enumerate(terms):
                                r = pe.matmul(ps[:, (TPC + n) % RING, :], lhs, rhs, start=(a == 0), stop=(a == 6))
                            r.then_inc(mm, 1)
                        if norm and 1 <= n <= NQK:
                            g = tile(i, c, n - 1)
                            pe.wait_ge(freed, use(i, c, TPC + n - 1) + 1 + RING)
                            pe.wait_ge(p_qn, g + 1)
                            pe.matmul(psC[:, (n - 1) % 2, :], k["center"][:, :], praw[:, (n - 1) % 2, :],
                                      start=True, stop=True).then_inc(p_cen, 1)
                        if norm and n >= 2:
                            g = tile(i, c, n - 2)
                            pe.wait_ge(p_sq, g + 1)
                            pe.wait_ge(p_dev, g + 1)
                            pe.matmul(psV[:, :], k["blocks"][:, :], sq[:, :], start=True, stop=True).then_inc(p_var, 1)


def attend(nc, d, k, l, qk_scr, v_scr, oT):
    NS = 2 * TPB
    NMX = 4 * TPB * 2
    USES = NMX + 2
    TURN = (40, USES - 1)
    RING = 3
    with ExitStack() as ph:
        tag = f"a{l}_"
        sb = lambda n, s, dt=F32: ph.enter_context(nc.sbuf_tensor(tag + n, s, dt))
        sem = ph.enter_context(signals(nc, tag))
        qd = [sb(f"qd{p}", [P, 4, SEQ], F32R) for p in range(2)]
        kd = [sb(f"kd{p}", [P, SEQ], F32R) for p in range(2)]
        qr = [sb(f"qr{p}", [P, 4, SEQ], F32R) for p in range(2)]
        kr = [sb(f"kr{p}", [P, 4, SEQ], F32R) for p in range(2)]
        vq = [sb(f"vq{p}", [P, TPB, P]) for p in range(2)]
        probs = [sb(f"probs{p}", [P, 4, CH]) for p in range(2)]
        mx = sb("mx", [P, 4 * TPB, 2])
        mm_ = sb("mm", [P, 4 * TPB])
        mh = [sb(f"mh{p}", [2 * TPB, P], F32R) for p in range(2)]
        ml = [sb(f"ml{p}", [2 * TPB, P], F32R) for p in range(2)]
        u = sb("u", [P, CH])
        rs = sb("rs", [P, CH])
        psS = ph.enter_context(nc.psum_tensor(tag + "psS", [P, 4, CH], F32))
        psO = ph.enter_context(nc.psum_tensor(tag + "psO", [P, CH], F32))
        psM = ph.enter_context(nc.psum_tensor(tag + "psM", [P, RING, CH], F32))
        zeroed, mx_ready, mx_free, comb, mh_ok, sc, ex, pv, u_ok, bc, rec, o_ok = (
            sem("zeroed"), sem("mx_ready"), sem("mx_free"), sem("comb"), sem("mh_ok"), sem("sc"),
            sem("ex"), sem("pv"), sem("u_ok"), sem("bc"), sem("rec"), sem("o_ok"))
        d_in = [sem(f"d_in{p}") for p in range(2)]
        r_in = [sem(f"r_in{p}") for p in range(2)]
        v_in = [sem(f"v_in{p}") for p in range(2)]
        m_in = [sem(f"m_in{p}") for p in range(2)]
        block = ph.enter_context(nc.Block())
        f = lambda ap: ap.bitcast(F32)

        def unit(scr, n):
            return scr[bass.ds(n, 1)].rearrange("o p c -> p (o c)")

        def load_d(eng, n, p):
            q, kk = qk_scr[0, 0], qk_scr[0, 1]
            for h in range(4):
                r = slice(HP * h, HP * h + HD)
                eng.dma_start(f(qd[p][r, h, :]), unit(q[:, r, :], n)).then_inc(d_in[p], 16)
            eng.dma_start(f(kd[p][:, :]), unit(kk, n)).then_inc(d_in[p], 16)

        def load_r(eng, n, p):
            for b in range(4):
                q = qk_scr[b // 2, 0, bass.ds(n, 1)].rearrange("o (h e) c -> e (o h) c", h=4)
                kk = qk_scr[b % 2, 1, bass.ds(n, 1)].rearrange("o (h e) c -> e (o h) c", h=4)
                eng.dma_start(f(qr[p][HP * b:HP * b + HD, :, :]), q[0:HD]).then_inc(r_in[p], 16)
                eng.dma_start(f(kr[p][HP * b:HP * b + HD + 1, :, :]), kk[0:HD + 1]).then_inc(r_in[p], 16)

        def load_v(eng, n, p):
            eng.dma_start(vq[p][:, :, :], v_scr[bass.ds(n, 1)].rearrange("o t p c -> p (o t) c")).then_inc(v_in[p], 16)

        def load_m(eng, n, p, half):
            eng.wait_ge(mx_free, RING + USES * n + TURN[half] + 1)
            for b in range(4):
                src = (mh if b < 2 else ml)[half]
                row = HP * b + HD
                eng.dma_start(f(qr[p][row:row + 1, 2 * half:2 * half + 2, :]).rearrange("o h (t c) -> o (h t) c", c=P),
                              f(src[:, :])).then_inc(m_in[p], 16)

        def iterations(eng, body):
            with eng.Fori(0, NQ // 2 - 1) as i:
                for p in range(2):
                    body(i * 2 + p, i, p, True, True)
            for p in range(2):
                body(NQ - 2 + p, NQ // 2 - 1, p, False, p == 0)

        @block.sync
        def _(sp):
            sp.wait_ge(zeroed, 1)
            for p in range(2):
                load_d(sp, p, p)
            load_r(sp, 0, 0)
            load_v(sp, 0, 0)
            load_r(sp, 1, 1)
            load_v(sp, 1, 1)
            for half in range(2):
                load_m(sp, 0, 0, half)

            def body(n, i, p, load, find):
                if load:
                    sp.wait_ge(mx_ready, USES * (n + 1))
                    load_d(sp, n + 2, p)
                if find:
                    for half in range(2):
                        load_m(sp, n + 1, 1 - p, half)
                if load:
                    sp.wait_ge(sc, 2 * NS * (n + 1))
                    load_r(sp, n + 2, p)
                    sp.wait_ge(pv, 2 + NS * (n + 1))
                    load_v(sp, n + 2, p)

            iterations(sp, body)

        @block.gpsimd
        def _(pool):
            for t in (*qd, *qr, *kr):
                r = pool.memset(t[:, :, :].bitcast(F32), 0.0)
            r.then_inc(zeroed, 1)
            pool.sem_inc(o_ok, 1)

            def body(n, i, p, load, find):
                for half in range(2):
                    pool.wait_ge(rec, 2 * n + half + 2)
                    pool.tensor_tensor(oT[:, bass.ds(n, 1), half * CH:(half + 1) * CH].rearrange("p o c -> p (o c)"),
                                       u[:, :], rs[:, :], ALU.mult).then_inc(o_ok, 1)

            iterations(pool, body)

        @block.scalar
        def _(act):
            act.sem_inc(ex, 2)

            def body(n, i, p, load, find):
                for s in range(NS):
                    for pr in range(2):
                        act.wait_ge(sc, 2 * NS * n + 2 * s + pr + 1)
                        act.wait_ge(pv, NS * n + s + 1)
                        act.activation(probs[s % 2][:, 2 * pr:2 * pr + 2, :], psS[:, 2 * pr:2 * pr + 2, :],
                                       ACT.Exp, scale=SCALE).then_inc(ex, 1)
                    if s in (TPB, NS - 1):
                        half = s // (NS - 1)
                        act.wait_ge(pv, 2 + NS * n + TPB * (half + 1))
                        act.wait_ge(o_ok, 2 * n + half + 1)
                        act.activation(u[:, :], psO[:, :], ACT.Copy).then_inc(u_ok, 1)

            iterations(act, body)

        @block.vector
        def _(dve):
            dve.sem_inc(mx_free, RING)
            dve.sem_inc(rec, 1)

            def find_max(m, j0, j1, sent=None):
                for j in range(j0, j1):
                    dve.wait_ge(mx_ready, USES * m + j + 1)
                    if j in TURN:
                        half = TURN.index(j)
                        src = psM[0:2 * TPB, j % RING, 0:P]
                        if half == 0 and sent:
                            sent()
                        dve.tensor_scalar(mh[half][:, :], src, -1.0, None, ALU.mult).then_inc(mh_ok, 1)
                        dve.wait_ge(mh_ok, 2 * m + half + 1)
                        dve.scalar_tensor_tensor(out=ml[half][:, :], in0=src, scalar=-1.0, in1=f(mh[half][:, :]),
                                                 op0=ALU.mult, op1=ALU.subtract).then_inc(mx_free, 1)
                        continue
                    e = j - (j > TURN[0])
                    if e == 0 and sent:
                        dve.wait_ge(comb, 2 * m)
                    dve.tensor_reduce(mx[:, e // 2, e % 2:e % 2 + 1], psM[:, j % RING, :], AX, ALU.max).then_inc(mx_free, 1)
                    if (e + 1) % (NMX // 2) == 0:
                        half = e // (NMX // 2)
                        cols = slice(half * 2 * TPB, (half + 1) * 2 * TPB)
                        dve.wait_ge(mx_free, RING + USES * m + j + 1)
                        dve.tensor_tensor(mm_[:, cols], mx[:, cols, 0], mx[:, cols, 1], ALU.max).then_inc(comb, 1)

            def invert(n, half):
                dve.wait_ge(bc, 2 * n + half + 1)
                dve.wait_ge(o_ok, 2 * n + half + 1)
                dve.reciprocal(rs[:, :], psO[:, :]).then_inc(rec, 1)

            find_max(0, 0, USES)

            def body(n, i, p, load, find):
                sent = lambda: dve.wait_ge(m_in[p], 128 * (i + 1))
                mid = 50
                if find:
                    find_max(n + 1, 0, mid, sent)
                invert(n, 0)
                if find:
                    find_max(n + 1, mid, USES, sent)
                invert(n, 1)

            iterations(dve, body)

        @block.tensor
        def _(pe):
            pe.sem_inc(pv, 2)

            def find_max(m, pm, j0, j1):
                for j in range(j0, min(j1, USES)):
                    pe.wait_ge(mx_free, USES * m + j + 1)
                    if j in TURN:
                        half = TURN.index(j)
                        pe.wait_ge(comb, 2 * m + half + 1)
                        pe.transpose(psM[0:2 * TPB, j % RING, 0:P], mm_[:, half * 2 * TPB:(half + 1) * 2 * TPB],
                                     k["ident"][:, :]).then_inc(mx_ready, 1)
                        continue
                    e = j - (j > TURN[0])
                    h, t, kh = e // (2 * TPB), e // 2 % TPB, e % 2
                    pe.matmul(psM[:, j % RING, :], qd[pm][:, h, t * P:(t + 1) * P], kd[pm][:, kh * CH:(kh + 1) * CH],
                              start=True, stop=True).then_inc(mx_ready, 1)

            def pv_step(n, i, p, s):
                half, kt = s // TPB, s % TPB
                if s == 0:
                    pe.wait_ge(v_in[p], 16 * (i + 1))
                if kt == 0:
                    pe.wait_ge(rec, 2 * n + half + 1)
                pe.wait_ge(ex, 2 + 2 * NS * n + 2 * s + 2)
                for h in range(4):
                    r = pe.matmul(psO[HP * h:HP * (h + 1), :], vq[p][:, kt, HP * h:HP * (h + 1)], probs[s % 2][:, h, :],
                                  start=(kt == 0), stop=(kt == TPB - 1))
                r.then_inc(pv, 1)

            def spread(n, half):
                pe.wait_ge(u_ok, 2 * n + half + 1)
                pe.matmul(psO[:, :], k["sumsel"][:, :], u[:, :], start=True, stop=True).then_inc(bc, 1)

            pe.wait_ge(d_in[0], 80)
            find_max(0, 0, 0, USES)

            def body(n, i, p, load, find):
                pe.wait_ge(r_in[p], 128 * (i + 1))
                pe.wait_ge(m_in[p], 128 * (i + 1))
                if find:
                    pe.wait_ge(d_in[1 - p], 80 * (i + 1 + p))
                for s in range(NS):
                    half, kt = s // TPB, s % TPB
                    for pr in range(2):
                        pe.wait_ge(ex, 2 * NS * n + 2 * s + pr + 1)
                        for h in (2 * pr, 2 * pr + 1):
                            r = pe.matmul(psS[:, h, :], kr[p][:, h, kt * P:(kt + 1) * P],
                                          qr[p][:, h, half * CH:(half + 1) * CH], start=True, stop=True)
                        r.then_inc(sc, 1)
                        if find:
                            find_max(n + 1, 1 - p, 5 * s + 2 * pr, 5 * s + 2 + 3 * pr)
                    if s == TPB + 1:
                        spread(n, 0)
                    if s:
                        pv_step(n, i, p, s - 1)
                pv_step(n, i, p, NS - 1)
                spread(n, 1)

            iterations(pe, body)


def project_out(nc, d, k, l, x, oT):
    with ExitStack() as ph:
        tag = f"p{l}_"
        sb = lambda n, s, dt=F32: ph.enter_context(nc.sbuf_tensor(tag + n, s, dt))
        sem = ph.enter_context(signals(nc, tag))
        wp = sb("wp", [P, QUADS, C])
        bp = sb("bp", [P, C])
        gate = sb("gate", [P, NB, C])
        t = sb("t", [P, 2, C])
        t2 = sb("t2", [P, 2, C])
        ps = ph.enter_context(nc.psum_tensor(tag + "ps", [P, 4, CH], F32))
        w_in, mm, freed, biased, gated, added = (
            sem("w_in"), sem("mm"), sem("freed"), sem("biased"), sem("gated"), sem("added"))
        block = ph.enter_context(nc.Block())

        @block.sync
        def _(sp):
            sp.dma_start(wp[:, :, :], d[f"wp{l}"]).then_inc(w_in, 16)
            sp.dma_start(bp[:, :], d[f"bp{l}"].partition_broadcast(P)).then_inc(w_in, 16)
            sp.dma_start(gate[:, :, :], k["gate_scr"][l, 0]).then_inc(w_in, 16)

        @block.tensor
        def _(pe):
            pe.wait_ge(w_in, 48)
            for n in range(TILES):
                if n >= 4:
                    pe.wait_ge(freed, n - 3)
                for q in range(QUADS):
                    o = oT[:, n // TPB * QUADS + q, n % TPB * P:(n % TPB + 1) * P]
                    r = pe.matmul(ps[:, n % 4, 0:C], o, wp[:, q, :], start=(q == 0), stop=(q == QUADS - 1))
                r.then_inc(mm, 1)

        @block.vector
        def _(dve):
            dve.wait_ge(w_in, 48)
            for n in range(TILES):
                dve.wait_ge(mm, n + 1)
                if n >= 2:
                    dve.wait_ge(gated, n - 1)
                dve.tensor_tensor(t[:, n % 2, :], ps[:, n % 4, 0:C], bp[:, :], ALU.add).then_inc(freed, 1)

        @block.gpsimd
        def _(pool):
            pool.wait_ge(w_in, 48)
            for n in range(TILES):
                pool.wait_ge(freed, n + 1)
                if n >= 2:
                    pool.wait_ge(added, n - 1)
                pool.tensor_tensor(t2[:, n % 2, :], t[:, n % 2, :], gate[:, n // TPB, :], ALU.mult).then_inc(gated, 1)
                pool.wait_ge(gated, n + 1)
                pool.tensor_tensor(x[:, n, :], x[:, n, :], t2[:, n % 2, :], ALU.add).then_inc(added, 1)


def feed_forward(nc, d, k, l, x):
    moe = l == 0
    n_exp = NE if moe else 1
    func = ACT.Gelu if l == 1 else ACT.Gelu_apprx_tanh
    CHUNKS = NB * CPB
    M = CHUNKS * KT
    DN0 = 2 * M
    with ExitStack() as outer:
        tag = f"f{l}_"
        osb = lambda n, s, dt=F32: outer.enter_context(nc.sbuf_tensor(tag + n, s, dt))
        osem = outer.enter_context(signals(nc, tag))
        XH = osb("XH", [P, 2, TOK], F32R)
        XL = osb("XL", [P, 2, TOK], F32R)
        X8 = osb("X8", [P, TOK], F32R)
        b1 = osb("b1", [P, n_exp, KT])
        b2 = osb("b2", [P, n_exp, C])
        gate = osb("gate", [P, NB, C])
        cw = osb("cw", [P, TILES, NE]) if moe else None
        raw1 = osb("raw1", [P, FT, FF])
        raw2 = osb("raw2", [P, KT, C])
        b_in, raw_in, split = osem("b_in"), osem("raw_in"), osem("split")

        with ExitStack() as ph:
            sb = lambda n, s, dt=F32: ph.enter_context(nc.sbuf_tensor(tag + n, s, dt))
            sem = ph.enter_context(signals(nc, tag))
            prep = Prep(nc, ph, sem, k, l, 1, x, tag)
            if moe:
                wg = sb("wg", [P, FT, NE])
                lg = sb("lg", [P, TILES, NE])
                cmp = sb("cmp", [P, TILES, NE, NE - 1])
                top = sb("top", [P, TILES])
                ee = sb("ee", [P, TILES, NE])
                psG = ph.enter_context(nc.psum_tensor(tag + "psG", [P, TPB, NE], F32))
                g_in, g_mm, g_got, g_dve, g_exp = sem("g_in"), sem("g_mm"), sem("g_got"), sem("g_dve"), sem("g_exp")
            block = ph.enter_context(nc.Block())

            @block.sync
            def _(sp):
                if moe:
                    sp.dma_start(wg[:, :, :], d["wg"]).then_inc(g_in, 16)
                sp.dma_start(raw1[:, :, :], d[f"w1_{l}"][0]).then_inc(raw_in, 16)
                sp.dma_start(raw2[:, :, :], d[f"w2_{l}"][0]).then_inc(raw_in, 16)
                sp.dma_start(b1[:, :, :], d[f"b1_{l}"]).then_inc(b_in, 16)
                sp.dma_start(gate[:, :, :], k["gate_scr"][l, 1]).then_inc(b_in, 16)
                for e in range(n_exp):
                    sp.dma_start(b2[:, e, :], d[f"b2_{l}"][e].partition_broadcast(P)).then_inc(b_in, 16)

            def stack(i, c):
                at = bass.ds(i * SEQ + c * CH, CH)
                return XH[:, :, at], XL[:, :, at], X8[:, at]

            @block.gpsimd
            def _(pool):
                pool.sem_inc(prep.s_l, CPB)
                with pool.Fori(0, NB) as i:
                    for c in range(CPB):
                        h, lo, e8 = stack(i, c)
                        prep.low(pool, i, c, h, lo, e8)

            @block.scalar
            def _(act):
                with act.Fori(0, NB) as i:
                    prep.deviation(act, i)
                    for c in range(CPB):
                        h, lo, e8 = stack(i, c)
                        prep.high(act, i, c, h, e8)
                if moe:
                    act.wait_ge(g_dve, 2)
                    act.activation(ee[:, :, :], ee[:, :, :], ACT.Exp).then_inc(g_exp, 1)

            @block.vector
            def _(dve):
                dve.sem_inc(prep.s_y, 1)
                with dve.Fori(0, NB) as i:
                    prep.normalise(dve, i)
                    for c in range(CPB):
                        prep.modulate(dve, i, c)
                    if moe:
                        dve.wait_ge(g_mm, i + 1)
                        dve.tensor_copy(lg[:, bass.ds(i * TPB, TPB), :], psG[:, :, :]).then_inc(g_got, 1)
                if moe:
                    done = count(1)

                    dve.wait_ge(g_got, NB)
                    dve.tensor_reduce(top[:, :], lg[:, :, :], AX, ALU.max).then_inc(g_dve, 1)
                    dve.wait_ge(g_dve, next(done))
                    dve.tensor_tensor(ee[:, :, :], lg[:, :, :], top[:, :].unsqueeze(2).broadcast_to([P, TILES, NE]), ALU.subtract).then_inc(g_dve, 1)
                    dve.wait_ge(g_dve, next(done))
                    for e in range(NE):
                        for a, j in enumerate(j for j in range(NE) if j != e):
                            r = dve.tensor_tensor(cmp[:, :, e, a], lg[:, :, j], lg[:, :, e], ALU.is_ge if j < e else ALU.is_gt)
                    r.then_inc(g_dve, 1)
                    dve.wait_ge(g_dve, next(done))
                    dve.tensor_reduce(cw[:, :, :], cmp[:, :, :, :], AX, ALU.add).then_inc(g_dve, 1)
                    dve.wait_ge(g_dve, next(done))
                    dve.tensor_scalar(cw[:, :, :], cw[:, :, :], 2.0, None, ALU.is_lt).then_inc(g_dve, 1)
                    dve.wait_ge(g_dve, next(done))
                    dve.wait_ge(g_exp, 1)
                    dve.tensor_tensor(cw[:, :, :], cw[:, :, :], ee[:, :, :], ALU.mult).then_inc(g_dve, 1)
                    dve.wait_ge(g_dve, next(done))
                    dve.tensor_reduce(top[:, :], cw[:, :, :], AX, ALU.add).then_inc(g_dve, 1)
                    dve.wait_ge(g_dve, next(done))
                    dve.reciprocal(top[:, :], top[:, :]).then_inc(g_dve, 1)
                    dve.wait_ge(g_dve, next(done))
                    dve.tensor_tensor(cw[:, :, :], cw[:, :, :], top[:, :].unsqueeze(2).broadcast_to([P, TILES, NE]), ALU.mult).then_inc(g_dve, 1)
                    dve.wait_ge(g_dve, next(done))

            @block.tensor
            def _(pe):
                if moe:
                    pe.wait_ge(g_in, 16)
                with pe.Fori(0, NB) as i:
                    for c in range(CPB):
                        prep.transpose(pe, i, c)
                        if moe:
                            pe.wait_ge(prep.s_y, i * CPB + c + 2)
                            for t in range(TPC):
                                cols = slice(t * P, (t + 1) * P)
                                for f, rows in enumerate((P, P, TAIL)):
                                    r = pe.matmul(psG[:, c * TPC + t, :], prep.y[0:rows, c, f, cols], wg[0:rows, f, :],
                                                  start=(f == 0), stop=(f == FT - 1))
                    if moe:
                        r.then_inc(g_mm, 1)

        with ExitStack() as ph:
            sb = lambda n, s, dt=F32: ph.enter_context(nc.sbuf_tensor(tag + n, s, dt))
            sem = ph.enter_context(signals(nc, tag))
            SLOTS = min(2, n_exp)
            W1H = [sb(f"W1H{p}", [P, 2, FF], F32R) for p in range(SLOTS)]
            W1L = [sb(f"W1L{p}", [P, 2, FF], F32R) for p in range(SLOTS)]
            W18 = [sb(f"W18{p}", [P, FF], F32R) for p in range(SLOTS)]
            W2H = [sb(f"W2H{p}", [P, KT, C], F32R) for p in range(SLOTS)]
            W2L = [sb(f"W2L{p}", [P, KT, C], F32R) for p in range(SLOTS)]
            b1e = [sb(f"b1e{p}", [P, KT]) for p in range(SLOTS)]
            cwe = sb("cwe", [P, TILES])
            GS = 3
            g32 = sb("g32", [P, GS, CH])
            gh = sb("gh", [P, GS, CH], F32R)
            gl = sb("gl", [P, GS, CH], F32R)
            tb = sb("tb", [P, TPC, C])
            psU = ph.enter_context(nc.psum_tensor(tag + "psU", [P, GS, CH], F32))
            psA = ph.enter_context(nc.psum_tensor(tag + "psA", [P, TPC, CH], F32))
            up, acted, glow, dn, taken, me, h_ok = sem("up"), sem("acted"), sem("glow"), sem("dn"), sem("taken"), sem("self"), sem("h_ok")
            block = ph.enter_context(nc.Block())

            def experts(eng, body):
                if n_exp == 1:
                    body(0, 0)
                    return
                with eng.Fori(0, n_exp // 2) as i:
                    for p in range(2):
                        body(i * 2 + p, p)

            @block.sync
            def _(sp):
                if moe:
                    with sp.Fori(1, NE) as e:
                        sp.wait_ge(split, e)
                        sp.dma_start(raw1[:, :, :], d[f"w1_{l}"][bass.ds(e, 1)].rearrange("o p f n -> p (o f) n")).then_inc(raw_in, 16)
                        sp.dma_start(raw2[:, :, :], d[f"w2_{l}"][bass.ds(e, 1)].rearrange("o p f n -> p (o f) n")).then_inc(raw_in, 16)

            @block.gpsimd
            def _(pool):
                def body(e, p):
                    pool.wait_ge(raw_in, 32 * (e + 1))
                    pool.wait_ge(dn, DN0 + M * (e - 1))
                    pool.wait_ge(b_in, 16 * (2 + n_exp))
                    pool.tensor_copy(b1e[p][:, :], b1[:, bass.ds(e, 1), :].rearrange("p o n -> p (o n)"))
                    pool.tensor_copy(W1H[p][:, :, :], raw1[:, 0:2, :])
                    pool.tensor_copy(W18[p][:, :], raw1[:, 2, :])
                    pool.tensor_copy(W2H[p][:, :, :], raw2[:, :, :]).then_inc(h_ok, 1)
                    pool.wait_ge(h_ok, 4 * e + 1)
                    pool.tensor_tensor(W1L[p][:, :, :], raw1[:, 0:2, :], W1H[p][:, :, :].bitcast(F32), ALU.subtract).then_inc(h_ok, 1)
                    for n, b in enumerate((1, 3)):
                        pool.wait_ge(h_ok, 4 * e + 2 + n)
                        rows = slice(32 * b, 32 * b + 32)
                        pool.tensor_tensor(W18[p][rows, :], raw1[rows, 2, :], W18[p][rows, :].bitcast(F32), ALU.subtract).then_inc(h_ok, 1)
                    pool.wait_ge(h_ok, 4 * e + 4)
                    pool.tensor_tensor(W2L[p][:, :, :], raw2[:, :, :], W2H[p][:, :, :].bitcast(F32), ALU.subtract).then_inc(split, 1)

                experts(pool, body)

            @block.scalar
            def _(act):
                act.sem_inc(acted, GS)

                def body(e, p):
                    act.wait_ge(split, e + 1)
                    for m in range(M):
                        g = M * e + m
                        act.wait_ge(up, g + 1)
                        act.wait_ge(dn, DN0 + g - GS + 1)
                        act.wait_ge(glow, g + 1)
                        bias = b1e[p][:, m % KT:m % KT + 1]
                        act.activation(gh[:, m % GS, :], psU[:, m % GS, :], func, bias=bias)
                        act.activation(g32[:, m % GS, :], psU[:, m % GS, :], func, bias=bias).then_inc(acted, 1)

                experts(act, body)

            @block.vector
            def _(dve):
                dve.sem_inc(glow, GS)
                dve.sem_inc(taken, TPC)
                dve.wait_ge(b_in, 16 * (2 + n_exp))
                per = (1 if moe else 0) + CHUNKS * TPC * 2

                def body(e, p):
                    before = e * per + (1 if moe else 0)
                    if moe:
                        dve.tensor_copy(cwe[:, :], cw[:, :, bass.ds(e, 1)].rearrange("p t o -> p (t o)")).then_inc(me, 1)

                    def take(c):
                        dve.wait_ge(dn, DN0 + M * e + KT * (c + 1))
                        for t in range(TPC):
                            dve.tensor_tensor(tb[:, t, :], psA[:, t, 0:C], b2[:, bass.ds(e, 1), :].rearrange("p o n -> p (o n)"),
                                              ALU.add).then_inc(taken, 1)

                    def add(c, t):
                        n = c * TPC + t
                        dve.wait_ge(taken, TPC + CHUNKS * TPC * e + TPC * c + t + 1)
                        if moe and n == 0:
                            dve.wait_ge(me, before)
                        dve.scalar_tensor_tensor(
                            out=tb[:, t, :], in0=tb[:, t, :], scalar=cwe[:, n:n + 1] if moe else 1.0,
                            in1=gate[:, n // TPB, :], op0=ALU.mult, op1=ALU.mult).then_inc(me, 1)
                        dve.wait_ge(me, before + 2 * n + 1)
                        dve.tensor_tensor(x[:, n, :], x[:, n, :], tb[:, t, :], ALU.add).then_inc(me, 1)
                        dve.wait_ge(me, before + 2 * n + 2)

                    for m in range(M + 2):
                        g = M * e + m
                        if m < M:
                            dve.wait_ge(acted, g + 1 + GS)
                            dve.wait_ge(dn, DN0 + g - GS + 1)
                            dve.tensor_tensor(gl[:, m % GS, :], g32[:, m % GS, :], gh[:, m % GS, :].bitcast(F32),
                                              ALU.subtract).then_inc(glow, 1)
                        c, r = divmod(m - 2 - (KT - 1), KT)
                        if c >= 0 and r == 0:
                            take(c)
                        if c >= 0 and 1 <= r <= TPC:
                            add(c, r - 1)
                    for t in range(TPC):
                        add(CHUNKS - 1, t)

                experts(dve, body)

            @block.tensor
            def _(pe):
                pe.sem_inc(dn, DN0)

                def down(e, p, m):
                    g, c, kt = M * e + m, m // KT, m % KT
                    pe.wait_ge(glow, g + 1 + GS)
                    for t in range(TPC):
                        if kt == 0:
                            pe.wait_ge(taken, CHUNKS * TPC * e + TPC * c + t + 1)
                        cols = slice(t * P, (t + 1) * P)
                        for a, (lhs, rhs) in enumerate(((gh, W2H), (gl, W2H), (gh, W2L))):
                            r = pe.matmul(psA[:, t, 0:C], lhs[:, m % GS, cols], rhs[p][:, kt, :],
                                          start=(kt == 0 and a == 0), stop=(kt == KT - 1 and a == 2))
                    r.then_inc(dn, 1)

                def body(e, p):
                    pe.wait_ge(split, e + 1)
                    for m in range(M + 2):
                        if m < M:
                            g, c, kt = M * e + m, m // KT, m % KT
                            cols = slice(kt * P, (kt + 1) * P)
                            at = slice(c * CH, (c + 1) * CH)
                            pe.wait_ge(acted, g + 1)
                            terms = [(w_[p][:, f, cols], x_[:, f, at]) for x_, w_ in ((XH, W1H), (XL, W1H), (XH, W1L)) for f in range(2)]
                            terms.append((W18[p][:, cols], X8[:, at]))
                            for a, (lhs, rhs) in enumerate(terms):
                                r = pe.matmul(psU[:, m % GS, :], lhs, rhs, start=(a == 0), stop=(a == 6))
                            r.then_inc(up, 1)
                        if m >= 2:
                            down(e, p, m - 2)

                experts(pe, body)


def build(nc, d, out):
    with ExitStack() as ctx:
        k = {}
        consts(nc, ctx, k)
        x = ctx.enter_context(nc.sbuf_tensor("x", [P, TILES, C], F32))
        qk_scr = nc.dram_tensor("qk_scr", (2, 2, NQ, P, SEQ), F32, kind="Internal").ap()
        v_scr = nc.dram_tensor("v_scr", (NQ, TPB, P, P), F32, kind="Internal").ap()
        condition(nc, ctx, d, k)
        rotate(nc, d, k, x)
        for l in range(3):
            project_qkv(nc, d, k, l, x, qk_scr, v_scr)
            with ExitStack() as att:
                oT = att.enter_context(nc.sbuf_tensor(f"oT{l}", [P, NQ, SEQ], F32))
                attend(nc, d, k, l, qk_scr, v_scr, oT)
                project_out(nc, d, k, l, x, oT)
            feed_forward(nc, d, k, l, x)
        stored = ctx.enter_context(nc.semaphore("stored"))
        with nc.Block() as block:

            @block.sync
            def _(sp):
                sp.dma_start(out.rearrange("b s c -> (b s) c").rearrange("(t p) c -> p t c", p=P), x[:, :, :]).then_inc(stored, 16)
                sp.wait_ge(stored, 16)


_OUT = ((NB, SEQ, C), "float32")


def _layout(a):
    import numpy as np

    z = lambda *s: np.zeros(s, np.float32)
    d = {}

    def stack(w):
        tail = np.concatenate([w[2 * P:]] * 4, 0)
        return np.ascontiguousarray(np.stack([w[0:P], w[P:2 * P], tail], 1))

    def heads(w, one=None):
        p = z(*w.shape[:-1], NH, HP)
        p[..., :HD] = w.reshape(*w.shape[:-1], NH, HD)
        if one:
            p[..., SUMCOL] = 1.0
        return p.reshape(*w.shape[:-1], NH * HP)

    d["x"] = a["x"].reshape(TOK, C)
    d["xT"] = np.ascontiguousarray(d["x"].T)
    d["condT"] = np.ascontiguousarray(a["cond_1152"].T)
    d["PT"] = np.ascontiguousarray(a["L0_cond_P"].T)
    iu, ju = np.triu_indices(RD, k=1)
    w = z(RD, RD, C)
    w[iu, ju] = a["L0_cond_W"]
    d["rot_w"] = np.ascontiguousarray(w.reshape(RD * RD, C).T)
    b = z(RD, RD)
    b[iu, ju] = a["L0_cond_b"]
    d["rot_b"] = b.reshape(1, RD * RD)
    names = [
        dict(ada="L1_cond_w_adaln", bada="L1_cond_b_adaln", qkv="L1_cond_w_qkv", bqkv="L1_cond_b_qkv",
             p="L1_cond_w_proj", bp="L1_cond_b_proj", w1="L1_cond_w1", b1="L1_cond_b1", w2="L1_cond_w2", b2="L1_cond_b2"),
        dict(ada="L2_cond_w_ada", bada="L2_cond_b_ada", qkv="L2_cond_w_qkv", bqkv="L2_cond_b_qkv",
             p="L2_cond_w_proj", bp="L2_cond_b_proj", w1="L2_cond_w1", b1="L2_cond_b1", w2="L2_cond_w2", b2="L2_cond_b2"),
        dict(ada="L3_cond_W_ada", bada="L3_cond_b_ada", qkv="L3_cond_W_qkv", bqkv="L3_cond_b_qkv",
             p="L3_cond_W_proj", bp="L3_cond_b_proj", w1="L3_cond_W_fc1", b1="L3_cond_b_fc1", w2="L3_cond_W_fc2", b2="L3_cond_b_fc2"),
    ]
    for l, nm in enumerate(names):
        ada, bada = a[nm["ada"]].reshape(C, 6, C), a[nm["bada"]].reshape(6, C)
        rep = lambda v: np.concatenate([v] + [v[..., 2 * P:]] * 3, -1)
        d[f"wfm{l}"] = np.ascontiguousarray(rep(ada[:, [0, 1, 3, 4]]).reshape(C, 4 * CP))
        d[f"bfm{l}"] = np.ascontiguousarray(rep(bada[[0, 1, 3, 4]]).reshape(4, FT, P).transpose(2, 1, 0))
        d[f"wga{l}"] = np.ascontiguousarray(ada[:, [2, 5]].reshape(C, 2 * C))
        d[f"bga{l}"] = np.ascontiguousarray(bada[[2, 5]])
        qkv, bqkv = a[nm["qkv"]].reshape(C, 3, C), a[nm["bqkv"]].reshape(3, C)
        d[f"wqkv{l}"] = stack(np.concatenate([heads(qkv[:, j]) for j in range(3)], 1))
        bq, bk = heads(bqkv[0]), heads(bqkv[1], True)
        d[f"bqk{l}"] = np.ascontiguousarray(np.concatenate([bq, bk]).reshape(2 * QUADS, P).T)
        d[f"bv{l}"] = heads(bqkv[2], True)
        wp = z(NH, HP, C)
        wp[:, :HD] = a[nm["p"]].reshape(NH, HD, C)
        d[f"wp{l}"] = np.ascontiguousarray(wp.reshape(QUADS, P, C).transpose(1, 0, 2))
        d[f"bp{l}"] = a[nm["bp"]]
        n = NE if l == 0 else 1
        w1, b1 = a[nm["w1"]].reshape(n, C, FF), a[nm["b1"]].reshape(n, KT, P)
        w2, b2 = a[nm["w2"]].reshape(n, KT, P, C), a[nm["b2"]].reshape(n, C)
        d[f"w1_{l}"] = np.stack([stack(w1[e]) for e in range(n)])
        d[f"b1_{l}"] = np.ascontiguousarray(b1.transpose(2, 0, 1))
        d[f"w2_{l}"] = np.ascontiguousarray(w2.transpose(0, 2, 1, 3))
        d[f"b2_{l}"] = b2
    d["wg"] = stack(a["L1_cond_w_gate"])
    g = z(4, 4, HP)
    for j, nm in enumerate(("L2_cond_qn_g", "L2_cond_qn_b", "L2_cond_kn_g", "L2_cond_kn_b")):
        g[j, :, :HD] = a[nm]
    g[3, :, SUMCOL] = 1.0
    d["qkn"] = np.ascontiguousarray(g.reshape(4, P).T)
    return d


def kernel(**inputs):
    import numpy as np
    from concourse import bacc
    from concourse.bass_utils import run_bass_kernel_spmd

    laid = _layout({n: np.asarray(v) for n, v in inputs.items()})
    nc = bacc.Bacc("TRN2", target_bir_lowering=False, num_devices=1)
    arrays, d = {}, {}
    for n, v in laid.items():
        arrays["in_" + n] = v
        d[n] = nc.dram_tensor("in_" + n, v.shape, mybir.dt.from_np(v.dtype), kind="ExternalInput").ap()
    out = nc.dram_tensor("out_0", _OUT[0], F32, kind="ExternalOutput").ap()
    build(nc, d, out)
    r = run_bass_kernel_spmd(nc, [arrays], core_ids=[0])
    return r.results[0]["out_0"]
```

```python
from contextlib import ExitStack, contextmanager
from itertools import count

import concourse.bass as bass
from concourse import mybir

F32 = mybir.dt.float32
F32R = mybir.dt.float32r
ACT = mybir.ActivationFunctionType
ALU = mybir.AluOpType
AX = mybir.AxisListType.X

P = 128
NB, SEQ, C = 2, 1024, 288
TOK = NB * SEQ
TILES = TOK // P
TPB = SEQ // P
NH, HD = 16, 18
HP = 32
QUADS = NH // 4
NQ = NB * QUADS
CH = 512
CPB = SEQ // CH
TPC = CH // P
FT = 3
CP = FT * P
TAIL = C - 2 * P
FF = 4 * C
KT = FF // P
NE = 4
RD = 64
SCALE = float(HD) ** -0.5
LN_EPS = 1e-6
QK_EPS = 1e-5
SCALINGS, TERMS = 5, 12
SUMCOL = HD


@contextmanager
def signals(nc, tag):
    made = []

    def make(name):
        made.append(nc.alloc_semaphore(tag + name))
        return made[-1]

    yield make
    nc.clear_and_free_semaphores(made)
    nc.all_engine_barrier()


def consts(nc, ctx, out):
    ident = ctx.enter_context(nc.sbuf_tensor("ident", [P, P], F32))
    blocks = ctx.enter_context(nc.sbuf_tensor("blocks", [P, P], F32))
    sumrow = ctx.enter_context(nc.sbuf_tensor("sumrow", [P, 4], F32))
    eps = ctx.enter_context(nc.sbuf_tensor("eps", [P, 2], F32))
    made = ctx.enter_context(nc.semaphore("const_made"))
    with nc.Block() as block:

        @block.gpsimd
        def _(pool):
            pool.memset(ident[:, :], 0.0)
            pool.memset(sumrow[:, :], 0.0)
            pool.memset(eps[:, 0:1], LN_EPS)
            pool.memset(eps[:, 1:2], QK_EPS)
            pool.memset(blocks[:, :], 1.0 / HD).then_inc(made, 1)
            pool.wait_ge(made, 1)
            pool.affine_select(out=ident[:, :], in_=ident[:, :], compare_op=ALU.not_equal, fill=1.0,
                               base=0, pattern=[[-1, P]], channel_multiplier=1)
            pool.affine_select(out=sumrow[:, :], in_=sumrow[:, :], compare_op=ALU.not_equal, fill=1.0,
                               base=-SUMCOL, pattern=[[-HP, 4]], channel_multiplier=1)
            b = blocks[:, :].rearrange("p (a m) -> p a m", a=4)
            pool.affine_select(out=b, in_=b, compare_op=ALU.is_ge, fill=0.0,
                               base=0, pattern=[[-HP, 4], [0, HP]], channel_multiplier=1).then_inc(made, 1)
            pool.wait_ge(made, 2)
            pool.affine_select(out=b, in_=b, compare_op=ALU.is_ge, fill=0.0,
                               base=HD - 1, pattern=[[HP, 4], [0, HP]], channel_multiplier=-1).then_inc(made, 1)
            pool.wait_ge(made, 3)
            pool.affine_select(out=b, in_=b, compare_op=ALU.is_ge, fill=0.0,
                               base=HD - 1, pattern=[[0, 4], [-1, HP]], channel_multiplier=0).then_inc(made, 1)
            pool.wait_ge(made, 4)

    center = ctx.enter_context(nc.sbuf_tensor("center", [P, P], F32))
    with nc.Block() as block:

        @block.vector
        def _(dve):
            dve.tensor_tensor(center[:, :], ident[:, :], blocks[:, :], ALU.subtract)

    out.update(ident=ident, blocks=blocks, sumrow=sumrow, eps=eps, center=center)


def condition(nc, ctx, d, k):
    silu = ctx.enter_context(nc.sbuf_tensor("siluT", [96, 3, NB], F32))
    fm = [ctx.enter_context(nc.sbuf_tensor(f"fm{l}", [P, FT, 4, NB], F32)) for l in range(3)]
    gate_scr = nc.dram_tensor("gate_scr", (3, 2, P, NB, C), F32, kind="Internal").ap()
    rot = ctx.enter_context(nc.sbuf_tensor("rot", [RD, NB, RD], F32))
    k.update(fm=fm, gate_scr=gate_scr, rot=rot)
    with ExitStack() as ph:
        sb = lambda n, s, dt=F32: ph.enter_context(nc.sbuf_tensor("c_" + n, s, dt))
        sem = ph.enter_context(signals(nc, "c_"))
        condT = sb("condT", [96, 3, NB])
        sig = sb("sig", [96, 3, NB])
        rep = sb("rep", [96, 3, NB, P])
        wfm = sb("wfm", [96, 2, 3, 4 * CP])
        wga = sb("wga", [96, 2, 3, 2 * C])
        bfm = sb("bfm", [P, 3, FT, 4])
        bga = sb("bga", [P, 3, 2, C])
        gates = [sb(f"gates{l}", [P, 2, NB, C]) for l in range(3)]
        wrot = sb("wrot", [96, 3, 2, 512])
        vrow = sb("vrow", [NB, RD * RD])
        brow = sb("brow", [NB, RD * RD])
        psf = ph.enter_context(nc.psum_tensor("c_psf", [P, 2, 512], F32))
        psg = ph.enter_context(nc.psum_tensor("c_psg", [P, 4, 512], F32))
        psv = ph.enter_context(nc.psum_tensor("c_psv", [P, 2, 512], F32))
        small, silu_done, sig_done, rep_done = sem("small"), sem("silu"), sem("sig"), sem("rep")
        ada = [sem(f"ada{p}") for p in range(2)]
        rw = [sem(f"rw{p}") for p in range(2)]
        mm_f, mm_g, mm_v, got_f, got_g, got_v, sent = (
            sem("mm_f"), sem("mm_g"), sem("mm_v"), sem("got_f"), sem("got_g"), sem("got_v"), sem("sent"))
        block = ph.enter_context(nc.Block())

        @block.sync
        def _(sp):
            sp.dma_start(condT[:, :, :], d["condT"].rearrange("(a p) b -> p a b", p=96)).then_inc(small, 16)
            sp.dma_start(brow[0:1, :], d["rot_b"]).then_inc(small, 16)
            sp.dma_start(brow[1:2, :], d["rot_b"]).then_inc(small, 16)
            for l in range(3):
                sp.dma_start(bfm[:, l, :, :], d[f"bfm{l}"]).then_inc(small, 16)
                sp.dma_start(bga[:, l, :, :], d[f"bga{l}"].partition_broadcast(P)).then_inc(small, 16)
            for l in range(3):
                if l == 2:
                    sp.wait_ge(mm_f, 1)
                    sp.wait_ge(mm_g, 4)
                sp.dma_start(wfm[:, l % 2, :, :], d[f"wfm{l}"].rearrange("(a p) n -> p a n", p=96)).then_inc(ada[l % 2], 16)
                sp.dma_start(wga[:, l % 2, :, :], d[f"wga{l}"].rearrange("(a p) n -> p a n", p=96)).then_inc(ada[l % 2], 16)
            sp.wait_ge(got_v, 8)
            for b in range(NB):
                sp.dma_start(rot[:, b, :], vrow[b:b + 1, :].rearrange("o (i j) -> o i j", i=RD)).then_inc(sent, 16)
            for l in range(3):
                sp.wait_ge(got_g, 4 * (l + 1))
                for g in range(2):
                    sp.dma_start(gate_scr[l, g], gates[l][:, g, :, :]).then_inc(sent, 16)
            sp.wait_ge(sent, 32 + 96)

        @block.gpsimd
        def _(pool):
            for j in range(8):
                if j >= 2:
                    pool.wait_ge(mm_v, j - 1)
                pool.dma_start(wrot[:, :, j % 2, :],
                               d["rot_w"][:, 512 * j:512 * j + 512].rearrange("(a p) n -> p a n", p=96)).then_inc(rw[j % 2], 16)

        @block.scalar
        def _(act):
            act.wait_ge(small, 16 * 9)
            act.activation(sig[:, :, :], condT[:, :, :], ACT.Sigmoid).then_inc(sig_done, 1)

        @block.vector
        def _(dve):
            dve.wait_ge(small, 16 * 9)
            dve.wait_ge(sig_done, 1)
            dve.tensor_tensor(silu[:, :, :], condT[:, :, :], sig[:, :, :], ALU.mult).then_inc(silu_done, 1)
            dve.wait_ge(silu_done, 1)
            dve.tensor_copy(rep[:, :, :, :], silu[:, :, :].unsqueeze(3).broadcast_to([96, 3, NB, P])).then_inc(rep_done, 1)
            for j in range(8):
                dve.wait_ge(mm_v, j + 1)
                dve.tensor_tensor(vrow[:, 512 * j:512 * j + 512], psv[0:NB, j % 2, :], brow[:, 512 * j:512 * j + 512],
                                  ALU.add).then_inc(got_v, 1)
            for l in range(3):
                dve.wait_ge(mm_f, l + 1)
                dve.tensor_tensor(fm[l][:, :, :, :], psf[:, l % 2, 0:FT * 4 * NB].rearrange("p (f m b) -> p f m b", f=FT, m=4),
                                  bfm[:, l, :, :].unsqueeze(3).broadcast_to([P, FT, 4, NB]), ALU.add).then_inc(got_f, 1)
                dve.wait_ge(got_f, 2 * l + 1)
                dve.tensor_scalar(fm[l][:, :, 1:4:2, :], fm[l][:, :, 1:4:2, :], 1.0, None, ALU.add).then_inc(got_f, 1)
                for g in range(2):
                    for b in range(NB):
                        n = 4 * l + 2 * g + b
                        dve.wait_ge(mm_g, n + 1)
                        dve.tensor_tensor(gates[l][:, g, b, :], psg[:, n % 4, 0:C], bga[:, l, g, :], ALU.add).then_inc(got_g, 1)

        @block.tensor
        def _(pe):
            pe.wait_ge(silu_done, 1)
            pe.wait_ge(rep_done, 1)
            for j in range(8):
                pe.wait_ge(rw[j % 2], 16 * (j // 2 + 1))
                if j >= 2:
                    pe.wait_ge(got_v, j - 1)
                for a in range(3):
                    mm = pe.matmul(psv[0:NB, j % 2, :], silu[:, a, :], wrot[:, a, j % 2, :], start=(a == 0), stop=(a == 2))
                mm.then_inc(mm_v, 1)
            for l in range(3):
                pe.wait_ge(ada[l % 2], 32 * (l // 2 + 1))
                if l >= 2:
                    pe.wait_ge(got_f, 1)
                for f in range(FT):
                    for m in range(4):
                        o = (f * 4 + m) * NB
                        for a in range(3):
                            mm = pe.matmul(psf[:, l % 2, o:o + NB], wfm[:, l % 2, a, m * CP + f * P:m * CP + f * P + P],
                                           silu[:, a, :], start=(a == 0), stop=(a == 2))
                mm.then_inc(mm_f, 1)
                for g in range(2):
                    for b in range(NB):
                        n = 4 * l + 2 * g + b
                        if n >= 4:
                            pe.wait_ge(got_g, n - 3)
                        for a in range(3):
                            mm = pe.matmul(psg[:, n % 4, 0:C], rep[:, a, b, :], wga[:, l % 2, a, g * C:g * C + C],
                                           start=(a == 0), stop=(a == 2))
                        mm.then_inc(mm_g, 1)


QR_UNROLL = 8


def rotate(nc, d, k, x):
    ident, rot = k["ident"], k["rot"]
    W = C
    with ExitStack() as ph:
        sb = lambda n, s, dt=F32: ph.enter_context(nc.sbuf_tensor("r_" + n, s, dt))
        sem = ph.enter_context(signals(nc, "r_"))
        pT = sb("pT", [RD, C])
        A = sb("A", [P, C + RD])
        sel = sb("sel", [P, P])
        scr = sb("scr", [P, C])
        scr2 = sb("scr2", [P, C])
        sc = sb("sc", [P, 16])
        xT = sb("xT", [96, 3, TOK])
        skew = sb("skew", [RD, 4, RD])
        ex = sb("ex", [RD, 2, 4, RD])
        N1 = sb("N1", [RD, 2, RD])
        N1T = sb("N1T", [RD, 2, RD])
        ZT = sb("ZT", [RD, 2, RD])
        rinv = sb("rinv", [RD, RD])
        U = sb("U", [96, 3, RD])
        UT = sb("UT", [RD, C])
        RmI = sb("RmI", [RD, NB, RD])
        W2 = sb("W2", [RD, NB, C])
        zT = sb("zT", [RD, TOK])
        psR = ph.enter_context(nc.psum_tensor("r_psR", [P, 512], F32))
        psQ = ph.enter_context(nc.psum_tensor("r_psQ", [P, 512], F32))
        psE = ph.enter_context(nc.psum_tensor("r_psE", [P, 512], F32))
        psN = ph.enter_context(nc.psum_tensor("r_psN", [P, 3, 512], F32))
        psZ = ph.enter_context(nc.psum_tensor("r_psZ", [P, 2, 512], F32))
        loaded, xloaded, dv, row, row2, sel_ok, nsq_ok, nrm_ok, upd, mm, dd, xo = (
            sem("loaded"), sem("xloaded"), sem("dve_self"), sem("row"), sem("row2"), sem("sel"), sem("nsq"), sem("nrm"),
            sem("updated"), sem("mm"), sem("dve_done"), sem("x_out"))
        block = ph.enter_context(nc.Block())

        @block.sync
        def _(sp):
            sp.dma_start(pT[:, :], d["PT"]).then_inc(loaded, 16)
            sp.dma_start(x[:, :, :], d["x"].rearrange("(t p) c -> p t c", p=P)).then_inc(xloaded, 16)
            sp.dma_start(xT[:, :, :], d["xT"].rearrange("(a p) n -> p a n", p=96)).then_inc(xloaded, 16)

        SELF = 9

        @block.gpsimd
        def _(pool):
            pool.memset(sel[:, :], 1.0).then_inc(sel_ok, 1)
            pool.wait_ge(sel_ok, 1)
            with pool.Fori(0, RD) as s:
                pool.wait_ge(row2, s + 1)
                pool.tensor_copy(sel[:, :], ident[:, bass.ds(s, 1)].broadcast_to([P, P])).then_inc(sel_ok, 1)
            pool.wait_ge(upd, RD + 1)
            pool.wait_ge(dv, 1 + SELF * RD)
            pool.affine_select(out=N1[:, 0, :], in_=A[0:RD, 0:RD], compare_op=ALU.is_gt, fill=0.0,
                               base=0, pattern=[[-1, RD]], channel_multiplier=1).then_inc(xo, 1)

        @block.scalar
        def _(act):
            with act.Fori(0, RD // QR_UNROLL) as i:
                for u in range(QR_UNROLL):
                    s = i * QR_UNROLL + u
                    act.wait_ge(row2, s + 2)
                    act.activation(scr2[:, :], psQ[:, 0:W], ACT.Square, accum_out=sc[:, 0:1]).then_inc(nsq_ok, 1)
                    act.wait_ge(nsq_ok, s + 1)
                    act.activation(sc[:, 1:2], sc[:, 0:1], ACT.Sqrt).then_inc(nrm_ok, 1)

        @block.vector
        def _(dve):
            dve.memset(A[:, :], 0.0).then_inc(dv, 1)
            dve.wait_ge(loaded, 16)
            dve.wait_ge(dv, 1)
            dve.tensor_copy(A[0:RD, 0:C], pT[:, :]).then_inc(upd, 1)
            with dve.Fori(0, RD // QR_UNROLL) as i:
                for u in range(QR_UNROLL):
                    s = i * QR_UNROLL + u
                    before = s * SELF + 1
                    a = A[:, bass.ds(s, W)]
                    akk = A[:, bass.ds(s, 1)]
                    dve.wait_ge(row, s + 1)
                    dve.scalar_tensor_tensor(out=scr[:, :], in0=psR[:, 0:W], scalar=1.0, in1=a,
                                             op0=ALU.mult, op1=ALU.mult, accum_out=sc[:, 2:3]).then_inc(dv, 1)
                    dve.tensor_copy(sc[:, 3:4], psR[:, 0:1]).then_inc(dv, 1)
                    dve.tensor_scalar(sc[:, 4:5], psR[:, 0:1], 0.0, 2.0, ALU.is_ge, ALU.mult).then_inc(dv, 1)
                    dve.wait_ge(nrm_ok, s + 1)
                    dve.wait_ge(dv, before + 3)
                    dve.tensor_scalar(sc[:, 5:6], sc[:, 4:5], 1.0, sc[:, 1:2], ALU.subtract, ALU.mult).then_inc(dv, 1)
                    dve.wait_ge(dv, before + 4)
                    dve.tensor_scalar(sc[:, 6:7], sc[:, 3:4], sc[:, 5:6], sc[:, 0:1], ALU.mult, ALU.add).then_inc(dv, 1)
                    dve.tensor_scalar(sc[:, 7:8], akk, sc[:, 5:6], sc[:, 2:3], ALU.mult, ALU.add).then_inc(dv, 1)
                    dve.wait_ge(dv, before + 6)
                    dve.reciprocal(sc[:, 8:9], sc[:, 6:7]).then_inc(dv, 1)
                    dve.wait_ge(dv, before + 7)
                    dve.tensor_scalar(sc[:, 9:10], sc[:, 7:8], sc[:, 8:9], -1.0, ALU.mult, ALU.mult).then_inc(dv, 1)
                    dve.wait_ge(dv, before + 8)
                    dve.scalar_tensor_tensor(out=a, in0=psR[:, 0:W], scalar=sc[:, 9:10], in1=a,
                                             op0=ALU.mult, op1=ALU.add).then_inc(upd, 1)
                    dve.wait_ge(upd, s + 2)
                    dve.tensor_scalar(akk, sc[:, 9:10], sc[:, 5:6], akk, ALU.mult, ALU.add).then_inc(dv, 1)
                    dve.wait_ge(dv, before + 9)

            done = count(1)

            f = 1.0 / 2 ** SCALINGS
            dve.wait_ge(mm, 1)
            for b in range(NB):
                dve.tensor_tensor(skew[:, 2 * b, :], rot[:, b, :], psE[0:RD, b * RD:(b + 1) * RD], ALU.subtract).then_inc(dd, 1)
                dve.wait_ge(dd, next(done))
                dve.tensor_scalar(skew[:, 2 * b + 1, :], skew[:, 2 * b, :], -f, None, ALU.mult).then_inc(dd, 1)
                dve.wait_ge(dd, next(done))
                dve.tensor_scalar(skew[:, 2 * b, :], skew[:, 2 * b, :], f, None, ALU.mult).then_inc(dd, 1)
                dve.wait_ge(dd, next(done))
                for j in range(2):
                    dve.tensor_copy(ex[:, 0, 2 * b + j, :], ident[0:RD, 0:RD]).then_inc(dd, 1)
                    dve.wait_ge(dd, next(done))
            q = 0
            idb = ident[0:RD, 0:RD].unsqueeze(1).broadcast_to([RD, 4, RD])
            for t in range(TERMS, 0, -1):
                dve.wait_ge(mm, 2 + q)
                dve.scalar_tensor_tensor(out=ex[:, 1 - q % 2, :, :], in0=psE[0:RD, 0:4 * RD].rearrange("p (a n) -> p a n", a=4),
                                         scalar=1.0 / t, in1=idb, op0=ALU.mult, op1=ALU.add).then_inc(dd, 1)
                dve.wait_ge(dd, next(done))
                q += 1
            for t in range(SCALINGS):
                dve.wait_ge(mm, 2 + q)
                dve.tensor_copy(ex[:, 1 - q % 2, :, :], psE[0:RD, 0:4 * RD].rearrange("p (a n) -> p a n", a=4)).then_inc(dd, 1)
                dve.wait_ge(dd, next(done))
                q += 1
            for b in range(NB):
                dve.tensor_tensor(RmI[:, b, :], ex[:, q % 2, 2 * b + 1, :], ident[0:RD, 0:RD], ALU.subtract).then_inc(dd, 1)
                dve.wait_ge(dd, next(done))
            dve.tensor_tensor(scr[0:RD, 0:RD], A[0:RD, 0:RD], ident[0:RD, 0:RD], ALU.mult).then_inc(dd, 1)
            dve.wait_ge(dd, next(done))
            dve.tensor_reduce(sc[0:RD, 10:11], scr[0:RD, 0:RD], AX, ALU.add).then_inc(dd, 1)
            dve.wait_ge(dd, next(done))
            dve.reciprocal(sc[0:RD, 11:12], sc[0:RD, 10:11]).then_inc(dd, 1)
            dve.wait_ge(dd, next(done))
            dve.wait_ge(xo, 1)
            dve.tensor_scalar(N1[:, 0, :], N1[:, 0, :], sc[0:RD, 11:12], -1.0, ALU.mult, ALU.mult).then_inc(dd, 1)
            dve.wait_ge(dd, next(done))
            m0 = 2 + q
            dve.wait_ge(mm, m0)
            dve.tensor_copy(N1T[:, 0, :], psN[0:RD, 0, 0:RD]).then_inc(dd, 1)
            dve.wait_ge(dd, next(done))
            dve.tensor_tensor(ZT[:, 0, :], N1T[:, 0, :], ident[0:RD, 0:RD], ALU.add).then_inc(dd, 1)
            dve.wait_ge(dd, next(done))
            for s in range(1, 6):
                c, o = s % 2, 1 - s % 2
                dve.wait_ge(mm, m0 + 2 * s - 1)
                dve.tensor_copy(N1[:, c, :], psN[0:RD, 0, 0:RD]).then_inc(dd, 1)
                dve.wait_ge(dd, next(done))
                dve.tensor_copy(N1T[:, c, :], psN[0:RD, 1, 0:RD]).then_inc(dd, 1)
                dve.wait_ge(dd, next(done))
                dve.wait_ge(mm, m0 + 2 * s)
                dve.tensor_tensor(ZT[:, c, :], ZT[:, o, :], psN[0:RD, 2, 0:RD], ALU.add).then_inc(dd, 1)
                dve.wait_ge(dd, next(done))
            dve.tensor_scalar(rinv[:, :], ZT[:, 1, :], sc[0:RD, 11:12], None, ALU.mult).then_inc(dd, 1)
            dve.wait_ge(dd, next(done))
            m1 = m0 + 11
            dve.wait_ge(mm, m1)
            dve.tensor_copy(U[:, :, :], psN[0:96, 0, 0:3 * RD].rearrange("p (a n) -> p a n", a=3)).then_inc(dd, 1)
            dve.wait_ge(dd, next(done))
            dve.tensor_copy(UT[:, :], psN[0:RD, 1, 0:C]).then_inc(dd, 1)
            dve.wait_ge(dd, next(done))
            dve.wait_ge(mm, m1 + 1)
            dve.tensor_copy(W2[:, :, :], psN[0:RD, 1:3, 0:C]).then_inc(dd, 1)
            dve.wait_ge(dd, next(done))
            for c in range(TOK // CH):
                dve.wait_ge(mm, m1 + 2 + c)
                dve.tensor_copy(zT[:, c * CH:(c + 1) * CH], psZ[0:RD, c % 2, :]).then_inc(dd, 1)
                dve.wait_ge(dd, next(done))
            dve.wait_ge(xloaded, 32)
            for t in range(TILES):
                dve.wait_ge(mm, m1 + 6 + t)
                dve.tensor_tensor(x[:, t, :], x[:, t, :], psZ[:, t % 2, 0:C], ALU.add).then_inc(dd, 1)
                dve.wait_ge(dd, next(done))

        @block.tensor
        def _(pe):
            pe.wait_ge(sel_ok, 1)
            pe.sem_inc(row2, 1)
            with pe.Fori(0, RD) as s:
                pe.wait_ge(sel_ok, s + 2)
                pe.wait_ge(upd, s + 1)
                pe.matmul(psR[:, 0:W], sel[:, :], A[:, bass.ds(s, W)], start=True, stop=True).then_inc(row, 1)
                pe.matmul(psQ[:, 0:W], sel[:, :], A[:, bass.ds(s, W)], start=True, stop=True).then_inc(row2, 1)
            for b in range(NB):
                t = pe.transpose(psE[0:RD, b * RD:(b + 1) * RD], rot[:, b, :], ident[0:RD, 0:RD])
            t.then_inc(mm, 1)
            after = 5 * NB
            q = 0
            for t in range(TERMS):
                pe.wait_ge(dd, after + q)
                for j in range(4):
                    m = pe.matmul(psE[0:RD, j * RD:(j + 1) * RD], skew[:, j ^ 1, :], ex[:, q % 2, j, :], start=True, stop=True)
                m.then_inc(mm, 1)
                q += 1
            for t in range(SCALINGS):
                pe.wait_ge(dd, after + q)
                for j in range(4):
                    m = pe.matmul(psE[0:RD, j * RD:(j + 1) * RD], ex[:, q % 2, j ^ 1, :], ex[:, q % 2, j, :], start=True, stop=True)
                m.then_inc(mm, 1)
                q += 1
            after += q + NB + 3 + 1
            pe.wait_ge(dd, after)
            pe.transpose(psN[0:RD, 0, 0:RD], N1[:, 0, :], ident[0:RD, 0:RD]).then_inc(mm, 1)
            after += 2
            for s in range(1, 6):
                c, o = s % 2, 1 - s % 2
                pe.wait_ge(dd, after)
                pe.matmul(psN[0:RD, 0, 0:RD], N1T[:, o, :], N1[:, o, :], start=True, stop=True)
                pe.matmul(psN[0:RD, 1, 0:RD], N1[:, o, :], N1T[:, o, :], start=True, stop=True).then_inc(mm, 1)
                pe.wait_ge(dd, after + 2)
                pe.matmul(psN[0:RD, 2, 0:RD], N1[:, c, :], ZT[:, o, :], start=True, stop=True).then_inc(mm, 1)
                after += 3
            after += 1
            pe.wait_ge(dd, after)
            for a in range(3):
                pe.matmul(psN[0:96, 0, a * RD:(a + 1) * RD], pT[:, a * 96:(a + 1) * 96], rinv[:, :], start=True, stop=True)
            pe.matmul(psN[0:RD, 1, 0:C], rinv[:, :], pT[:, :], start=True, stop=True).then_inc(mm, 1)
            after += 2
            pe.wait_ge(dd, after)
            for b in range(NB):
                m = pe.matmul(psN[0:RD, 1 + b, 0:C], RmI[:, b, :], UT[:, :], start=True, stop=True)
            m.then_inc(mm, 1)
            after += 1
            pe.wait_ge(xloaded, 32)
            for c in range(TOK // CH):
                if c >= 2:
                    pe.wait_ge(dd, after + c - 1)
                for a in range(3):
                    m = pe.matmul(psZ[0:RD, c % 2, :], U[:, a, :], xT[:, a, c * CH:(c + 1) * CH], start=(a == 0), stop=(a == 2))
                m.then_inc(mm, 1)
            after += TOK // CH
            pe.wait_ge(dd, after)
            for t in range(TILES):
                if t >= 2:
                    pe.wait_ge(dd, after + t - 1)
                pe.matmul(psZ[:, t % 2, 0:C], zT[:, t * P:(t + 1) * P], W2[:, t // TPB, :], start=True, stop=True).then_inc(mm, 1)


class Prep:

    def __init__(self, nc, ph, sem, k, l, which, x, tag):
        sb = lambda n, s, dt=F32: ph.enter_context(nc.sbuf_tensor(tag + n, s, dt))
        self.k, self.x, self.which, self.l = k, x, which, l
        self.stats = sb("stats", [P, TPB, 6])
        self.mv = sb("mv", [P, TPB, 2])
        self.std = sb("std", [P, TPB])
        self.rstd = sb("rstd", [P, TPB])
        self.mod = sb("mod", [P, FT, 2])
        self.xn = sb("xn", [P, CPB, TPC, CP])
        self.y = sb("y", [P, CPB, FT, CH])
        self.psT = ph.enter_context(nc.psum_tensor(tag + "psT", [P, FT, CH], F32))
        self.s_mv, self.s_std, self.s_self, self.s_xn, self.s_T, self.s_y, self.s_h, self.s_l, self.s_xl = (
            sem("mv"), sem("std"), sem("norm_self"), sem("xn"), sem("T"), sem("y"), sem("h"), sem("l"), sem("xl"))

    SELF = 3

    def normalise(self, dve, i):
        dve.wait_ge(self.s_y, i * CPB + 1)
        for t in range(TPB):
            r = dve.bn_stats(self.stats[:, t, :], self.x[:, bass.ds(i * TPB + t, 1), :].rearrange("p o c -> p (o c)"))
        r.then_inc(self.s_self, 1)
        dve.wait_ge(self.s_self, i * self.SELF + 1)
        b = 2 * self.which
        dve.tensor_copy(self.mod[:, :, :],
                        self.k["fm"][self.l][:, :, b:b + 2, bass.ds(i, 1)].rearrange("p f m o -> p f (m o)")).then_inc(self.s_self, 1)
        for t in range(TPB):
            r = dve.bn_aggr(self.mv[:, t, :], self.stats[:, t, :])
        r.then_inc(self.s_mv, 1)
        dve.wait_ge(self.s_std, i + 1)
        dve.reciprocal(self.rstd[:, :], self.std[:, :]).then_inc(self.s_self, 1)
        dve.wait_ge(self.s_self, i * self.SELF + 3)
        for c in range(CPB):
            for t in range(TPC):
                g = c * TPC + t
                xs = self.x[:, bass.ds(i * TPB + g, 1), :].rearrange("p o c -> p (o c)")
                dve.tensor_scalar(self.xn[:, c, t, 0:C], xs, self.mv[:, g, 0:1], self.rstd[:, g:g + 1],
                                  ALU.subtract, ALU.mult)
                r = dve.tensor_scalar(self.xn[:, c, t, C:CP].rearrange("p (a m) -> p a m", a=3),
                                      xs[:, 2 * P:C].unsqueeze(1).broadcast_to([P, 3, TAIL]),
                                      self.mv[:, g, 0:1], self.rstd[:, g:g + 1], ALU.subtract, ALU.mult)
            r.then_inc(self.s_xn, 1)

    def modulate(self, dve, i, c):
        dve.wait_ge(self.s_T, i * CPB + c + 1)
        dve.wait_ge(self.s_l, i * CPB + c + 1)
        for f in range(FT):
            r = dve.tensor_scalar(self.y[:, c, f, :], self.psT[:, f, :], self.mod[:, f, 1:2], self.mod[:, f, 0:1],
                                  ALU.mult, ALU.add)
        r.then_inc(self.s_y, 1)

    def deviation(self, act, i):
        act.wait_ge(self.s_mv, i + 1)
        act.activation(self.std[:, :], self.mv[:, :, 1], ACT.Sqrt, bias=self.k["eps"][:, 0:1]).then_inc(self.s_std, 1)

    def high(self, act, i, c, XH, X8):
        act.wait_ge(self.s_y, i * CPB + c + 2)
        act.activation(XH, self.y[:, c, 0:2, :], ACT.Copy)
        act.activation(X8, self.y[:, c, 2, :], ACT.Copy).then_inc(self.s_h, 1)

    def low(self, pool, i, c, XH, XL, X8):
        pool.wait_ge(self.s_h, i * CPB + c + 1)
        pool.wait_ge(self.s_l, i * CPB + c + CPB)
        pool.tensor_tensor(XL, self.y[:, c, 0:2, :], XH.bitcast(F32), ALU.subtract).then_inc(self.s_xl, 1)
        pool.wait_ge(self.s_xl, i * CPB + c + 1)
        pool.tensor_tensor(X8[64:P], self.y[64:P, c, 2, :], X8[64:P].bitcast(F32), ALU.subtract).then_inc(self.s_l, 1)

    def transpose(self, pe, i, c):
        pe.wait_ge(self.s_xn, i * CPB + c + 1)
        pe.wait_ge(self.s_y, i * CPB + c + 1)
        for f in range(FT):
            for t in range(TPC):
                r = pe.transpose(self.psT[:, f, t * P:(t + 1) * P], self.xn[:, c, t, f * P:(f + 1) * P], self.k["ident"][:, :])
        r.then_inc(self.s_T, 1)


def project_qkv(nc, d, k, l, x, qk_scr, v_scr):
    norm = l == 1
    RING = 3 if norm else 4
    NQK = 2 * QUADS
    NM, NV = CPB * NQK, CPB * TPC
    MM0 = NM + NV
    with ExitStack() as ph:
        tag = f"q{l}_"
        sb = lambda n, s, dt=F32: ph.enter_context(nc.sbuf_tensor(tag + n, s, dt))
        sem = ph.enter_context(signals(nc, tag))
        prep = Prep(nc, ph, sem, k, l, 0, x, tag)
        NW = NQK * P + QUADS * P
        raw = sb("raw", [P, FT, NW])
        WH = sb("WH", [P, 2, NW], F32R)
        WL = sb("WL", [P, 2, NW], F32R)
        W8 = sb("W8", [P, NW], F32R)
        XH = sb("XH", [P, CPB, 2, CH], F32R)
        XL = sb("XL", [P, CPB, 2, CH], F32R)
        X8 = sb("X8", [P, CPB, CH], F32R)
        bqk = sb("bqk", [P, NQK])
        bv = sb("bv", [P, CH])
        hst = sb("hst", [P, 4, CH], F32R)
        lst = sb("lst", [P, 4, CH], F32R)
        vst = sb("vst", [P, 2, CH])
        ps = ph.enter_context(nc.psum_tensor(tag + "ps", [P, RING, CH], F32))
        if norm:
            psV = ph.enter_context(nc.psum_tensor(tag + "psV", [P, CH], F32))
            psI = ph.enter_context(nc.psum_tensor(tag + "psI", [P, CH], F32))
            gb = sb("gb", [P, 4])
            wmean = sb("wmean", [P, FT, 2 * NH])
            bcen = sb("bcen", [P, NQK])
            sq = sb("sq", [P, 2, CH])
            sdev = sb("sdev", [P, 2, TPC, 4])
            rdev = sb("rdev", [P, 2, TPC, 4])
            rg = sb("rg", [P, 2, CH])
            qn = sb("qn", [P, 2, CH])
            wcen, bc_mm, bc_ok, n_sq, n_var, n_dev, n_rdev, n_spread, n_rg, n_qn = (
                sem("wcen"), sem("bc_mm"), sem("bc_ok"), sem("n_sq"), sem("n_var"), sem("n_dev"), sem("n_rdev"),
                sem("n_spread"), sem("n_rg"), sem("n_qn"))
        small, w_in, w_h, w_l, mm, out_h, out_l, freed = (
            sem("small"), sem("w_in"), sem("w_h"), sem("w_l"), sem("mm"), sem("out_h"), sem("out_l"),
            sem("freed"))
        sent = [sem(f"sent{n}") for n in range(4)]
        vsent = [sem(f"vsent{n}") for n in range(2)]
        block = ph.enter_context(nc.Block())

        use = lambda i, c, w: i * (NM + NV) + c * (NQK + TPC) + w
        tile = lambda i, c, n: i * NM + c * NQK + n
        heads = lambda t: t.rearrange("p (t h) -> p t h", h=4)

        def slot_free(eng, i, c, n):
            g = c * NQK + n
            eng.wait_ge(sent[g % 4], (i * (NM // 4) + g // 4 + 1) * 32)

        @block.sync
        def _(sp):
            sp.dma_start(bqk[:, :], d[f"bqk{l}"]).then_inc(small, 16)
            sp.dma_start(bv[:, :], d[f"bv{l}"].partition_broadcast(P)).then_inc(small, 16)
            if norm:
                sp.dma_start(gb[:, :], d["qkn"]).then_inc(small, 16)
            sp.dma_start(raw[:, :, :], d[f"wqkv{l}"]).then_inc(w_in, 16)
            for s in sent:
                sp.sem_inc(s, 32)
            for s in vsent:
                sp.sem_inc(s, 16)
            with sp.Fori(0, NB) as i:
                for c in range(CPB):
                    for t in range(TPC):
                        sp.wait_ge(freed, use(i, c, t) + RING + 1)
                        sp.dma_start(v_scr[bass.ds(i * QUADS, QUADS), c * TPC + t, :, :].rearrange("q p c -> p q c"),
                                     vst[:, t % 2, :].rearrange("p (q c) -> p q c", q=QUADS)).then_inc(vsent[t % 2], 16)
                    for n in range(NQK):
                        sp.wait_ge(out_l, tile(i, c, n) + 3)
                        for part, st in ((0, hst), (1, lst)):
                            dst = qk_scr[part, n // QUADS, bass.ds(i * QUADS + n % QUADS, 1), :, c * CH:(c + 1) * CH]
                            sp.dma_start(dst.rearrange("o p c -> p (o c)"),
                                         st[:, n % 4, :].bitcast(F32)).then_inc(sent[n % 4], 16)
            for s in sent:
                sp.wait_ge(s, 32 * (NB * NM // 4 + 1))
            for s in vsent:
                sp.wait_ge(s, 16 * (NB * NV // 2 + 1))

        @block.gpsimd
        def _(pool):
            pool.sem_inc(prep.s_l, CPB)
            pool.wait_ge(w_h, 1)
            pool.tensor_tensor(WL[:, :, :], raw[:, 0:2, :], WH[:, :, :].bitcast(F32), ALU.subtract).then_inc(w_l, 1)
            for n, b in enumerate((1, 3)):
                pool.wait_ge(w_l, n + 1)
                pool.tensor_tensor(W8[32 * b:32 * b + 32, :], raw[32 * b:32 * b + 32, 2, :],
                                   W8[32 * b:32 * b + 32, :].bitcast(F32), ALU.subtract).then_inc(w_l, 1)
            pool.wait_ge(w_l, 3)
            with pool.Fori(0, NB) as i:
                for c in range(CPB):
                    prep.low(pool, i, c, XH[:, c, :, :], XL[:, c, :, :], X8[:, c, :])

        @block.scalar
        def _(act):
            act.wait_ge(w_in, 16)
            if norm:
                act.wait_ge(wcen, 3)
            act.activation(WH[:, :, :], raw[:, 0:2, :], ACT.Copy)
            act.activation(W8[:, :], raw[:, 2, :], ACT.Copy).then_inc(w_h, 1)
            act.wait_ge(small, 48 if norm else 32)
            if norm:
                act.wait_ge(bc_mm, 1)
                act.activation(bcen[:, :], psV[:, 0:NQK], ACT.Copy).then_inc(bc_ok, 1)
                act.wait_ge(bc_ok, 1)
                act.sem_inc(n_dev, 2)
                act.sem_inc(n_rg, 2)
                act.sem_inc(n_sq, 2)
            with act.Fori(0, NB) as i:
                prep.deviation(act, i)
                for c in range(CPB):
                    act.wait_ge(mm, use(i, c + 1, 0))
                    prep.high(act, i, c, XH[:, c, :, :], X8[:, c, :])
                for c in range(CPB):
                    for n in range(NQK if not norm else NQK + 3):
                        if not norm:
                            act.wait_ge(mm, use(i, c, TPC + n) + 1 + MM0)
                            slot_free(act, i, c, n)
                            act.activation(hst[:, n % 4, :], ps[:, (TPC + n) % RING, :], ACT.Identity,
                                           bias=bqk[:, n:n + 1]).then_inc(out_h, 1)
                            continue
                        if n >= 3:
                            g, m = tile(i, c, n - 3), n - 3
                            w = 2 * (m // QUADS)
                            act.wait_ge(n_qn, g + 3)
                            slot_free(act, i, c, m)
                            act.activation(hst[:, m % 4, :], qn[:, m % 2, :], ACT.Identity,
                                           bias=gb[:, w + 1:w + 2]).then_inc(out_h, 1)
                        if 2 <= n <= NQK + 1:
                            g, w = tile(i, c, n - 2), 2 * ((n - 2) // QUADS)
                            act.wait_ge(n_qn, g + 1)
                            act.wait_ge(n_spread, g + 3)
                            act.activation(rg[:, n % 2, :], psI[:, :], ACT.Identity, scale=gb[:, w:w + 1]).then_inc(n_rg, 1)
                        if 1 <= n <= NQK:
                            g = tile(i, c, n - 1)
                            act.wait_ge(n_rdev, g + 1)
                            act.wait_ge(n_var, g + 3)
                            act.activation(sdev[:, (n - 1) % 2, :, :], heads(psV[:, 0:4 * TPC]), ACT.Sqrt,
                                           bias=k["eps"][:, 1:2]).then_inc(n_dev, 1)
                        if n < NQK:
                            g = tile(i, c, n)
                            act.wait_ge(mm, use(i, c, TPC + n) + 1 + MM0)
                            act.wait_ge(n_var, g + 1)
                            act.activation(sq[:, n % 2, :], ps[:, (TPC + n) % RING, :], ACT.Square,
                                           bias=bcen[:, n:n + 1]).then_inc(n_sq, 1)

        @block.vector
        def _(dve):
            dve.sem_inc(prep.s_y, 1)
            dve.sem_inc(freed, RING)
            dve.sem_inc(out_l, 2)
            if norm:
                dve.sem_inc(n_rdev, 2)
                dve.sem_inc(n_qn, 2)
                dve.wait_ge(w_in, 16)
                w = raw[:, :, 0:NQK * P].rearrange("p f (h e) -> p f h e", e=HP)[:, :, :, 0:HD]
                dve.tensor_reduce(wmean[:, :, :], w, AX, ALU.add).then_inc(wcen, 1)
                dve.wait_ge(wcen, 1)
                dve.tensor_scalar(wmean[:, :, :], wmean[:, :, :], 1.0 / HD, None, ALU.mult).then_inc(wcen, 1)
                dve.wait_ge(wcen, 2)
                dve.tensor_tensor(w, w, wmean[:, :, :].unsqueeze(3).broadcast_to([P, FT, 2 * NH, HD]), ALU.subtract).then_inc(wcen, 1)
            dve.wait_ge(small, 48 if norm else 32)
            with dve.Fori(0, NB) as i:
                prep.normalise(dve, i)
                for c in range(CPB):
                    prep.modulate(dve, i, c)
                for c in range(CPB):
                    for t in range(TPC):
                        dve.wait_ge(mm, use(i, c, t) + 1 + MM0)
                        dve.wait_ge(vsent[t % 2], (i * (NV // 2) + (c * TPC + t) // 2 + 1) * 16)
                        dve.tensor_tensor(vst[:, t % 2, :], ps[:, t % RING, :], bv[:, :], ALU.add).then_inc(freed, 1)
                    for n in range(NQK if not norm else NQK + 3):
                        if not norm:
                            dve.wait_ge(out_h, tile(i, c, n) + 1)
                            slot_free(dve, i, c, n)
                            dve.scalar_tensor_tensor(out=lst[:, n % 4, :], in0=ps[:, (TPC + n) % RING, :],
                                                     scalar=bqk[:, n:n + 1], in1=hst[:, n % 4, :].bitcast(F32),
                                                     op0=ALU.add, op1=ALU.subtract).then_inc(out_l, 1)
                            dve.wait_ge(out_l, tile(i, c, n) + 3)
                            dve.sem_inc(freed, 1)
                            continue
                        if 2 <= n <= NQK + 1:
                            g, m = tile(i, c, n - 2), n - 2
                            dve.wait_ge(out_l, g + 1)
                            dve.wait_ge(n_rg, g + 3)
                            dve.wait_ge(n_sq, g + 3)
                            dve.scalar_tensor_tensor(out=qn[:, m % 2, :], in0=ps[:, (TPC + m) % RING, :],
                                                     scalar=bcen[:, m:m + 1], in1=rg[:, m % 2, :],
                                                     op0=ALU.add, op1=ALU.mult).then_inc(n_qn, 1)
                            dve.wait_ge(n_qn, g + 3)
                            dve.sem_inc(freed, 1)
                        if 1 <= n <= NQK:
                            g = tile(i, c, n - 1)
                            dve.wait_ge(n_spread, g + 1)
                            dve.wait_ge(n_dev, g + 3)
                            dve.reciprocal(rdev[:, (n - 1) % 2, :, :], sdev[:, (n - 1) % 2, :, :]).then_inc(n_rdev, 1)
                        if n >= 3:
                            g, m = tile(i, c, n - 3), n - 3
                            w = 2 * (m // QUADS)
                            dve.wait_ge(out_h, g + 1)
                            slot_free(dve, i, c, m)
                            dve.scalar_tensor_tensor(out=lst[:, m % 4, :], in0=qn[:, m % 2, :], scalar=gb[:, w + 1:w + 2],
                                                     in1=hst[:, m % 4, :].bitcast(F32),
                                                     op0=ALU.add, op1=ALU.subtract).then_inc(out_l, 1)

        @block.tensor
        def _(pe):
            pe.sem_inc(mm, MM0)
            if norm:
                pe.sem_inc(n_var, 2)
                pe.sem_inc(n_spread, 2)
                pe.wait_ge(small, 48)
                pe.matmul(psV[:, 0:NQK], k["center"][:, :], bqk[:, :], start=True, stop=True).then_inc(bc_mm, 1)
                pe.wait_ge(bc_ok, 1)
            with pe.Fori(0, NB) as i:
                for c in range(CPB):
                    prep.transpose(pe, i, c)
                pe.wait_ge(w_h, 1)
                pe.wait_ge(w_l, 3)
                for c in range(CPB):
                    pe.wait_ge(prep.s_l, i * CPB + c + 1 + CPB)
                    pe.wait_ge(prep.s_h, i * CPB + c + 1)
                    for t in range(TPC):
                        pe.wait_ge(freed, use(i, c, t) + 1)
                        cols = slice(t * P, (t + 1) * P)
                        vw = slice(NQK * P, NW)
                        terms = [(x_[:, c, f, cols], w_[:, f, vw]) for x_, w_ in ((XH, WH), (XL, WH), (XH, WL)) for f in range(2)]
                        terms.append((X8[:, c, cols], W8[:, vw]))
                        for a, (lhs, rhs) in enumerate(terms):
                            r = pe.matmul(ps[:, t % RING, :], lhs, rhs, start=(a == 0), stop=(a == 6))
                        r.then_inc(mm, 1)
                    for n in range(NQK if not norm else NQK + 2):
                        if norm and n >= 2:
                            g, m = tile(i, c, n - 2), n - 2
                            pe.wait_ge(n_rdev, g + 3)
                            pe.wait_ge(n_rg, g + 2)
                            for t in range(TPC):
                                for h in range(4):
                                    r = pe.matmul(psI[HP * h:HP * (h + 1), t * P:(t + 1) * P],
                                                  rdev[:, m % 2, t, h:h + 1].broadcast_to([P, HP]), k["ident"][:, :],
                                                  start=True, stop=True)
                            r.then_inc(n_spread, 1)
                        if norm and 1 <= n <= NQK:
                            g, m = tile(i, c, n - 1), n - 1
                            pe.wait_ge(n_sq, g + 3)
                            pe.wait_ge(n_dev, g + 2)
                            for t in range(TPC):
                                r = pe.matmul(psV[:, 4 * t:4 * t + 4], sq[:, m % 2, t * P:(t + 1) * P],
                                              k["blocks"][:, 0:P:HP], start=True, stop=True)
                            r.then_inc(n_var, 1)
                        if n < NQK:
                            pe.wait_ge(freed, use(i, c, TPC + n) + 1)
                            cols = slice(n * P, (n + 1) * P)
                            terms = [(w_[:, f, cols], x_[:, c, f, :]) for x_, w_ in ((XH, WH), (XL, WH), (XH, WL)) for f in range(2)]
                            terms.append((W8[:, cols], X8[:, c, :]))
                            for a, (lhs, rhs) in enumerate(terms):
                                r = pe.matmul(ps[:, (TPC + n) % RING, :], lhs, rhs, start=(a == 0), stop=(a == 6))
                            r.then_inc(mm, 1)


RING = 3
EARLY = 18


def ring_plan(find, ahead):
    seq = []
    if find:
        seq += [("max", e) for e in range(EARLY, NMX)]
        seq.insert(NMX // 2 + 4 - EARLY, ("turn", 0))
        early = [("max2", e) for e in range(EARLY if ahead else 0)]
        early.insert(4, ("turn", 1))
        seq += early
    span = NS if ahead else NS - 4
    steps = [seq[len(seq) * s // span:len(seq) * (s + 1) // span] for s in range(NS)]
    for half, s in ((1, 1), (0, TPB + 1)):
        steps[s].append(("sums", half))
        steps[s + 1].append(("spread", half))
    return steps


NS = 2 * TPB
NMX = 4 * TPB * 2
WIDTH = lambda kind: 2 if kind == "turn" else 1
UNIT_USES = NMX + 2 * 2 + 4
FIRST_USES = NMX + 2 * 2 + EARLY
assert UNIT_USES % RING == 0 and EARLY % RING == 0


def attend(nc, d, k, l, qk_scr, v_scr, oT):
    with ExitStack() as ph:
        tag = f"a{l}_"
        sb = lambda n, s, dt=F32: ph.enter_context(nc.sbuf_tensor(tag + n, s, dt))
        sem = ph.enter_context(signals(nc, tag))
        qd = [sb(f"qd{p}", [P, 4, SEQ], F32R) for p in range(2)]
        kd = [sb(f"kd{p}", [P, SEQ], F32R) for p in range(2)]
        qr = [sb(f"qr{p}", [P, 4, SEQ], F32R) for p in range(2)]
        kr = [sb(f"kr{p}", [P, 4, SEQ], F32R) for p in range(2)]
        vq = [sb(f"vq{p}", [P, TPB, P]) for p in range(2)]
        probs = [sb(f"probs{p}", [P, 4, CH]) for p in range(2)]
        mx = sb("mx", [P, 4 * TPB, 2])
        mm_ = sb("mm", [P, 4 * TPB])
        mh = [sb(f"mh{p}", [2 * TPB, P], F32R) for p in range(2)]
        ml = [sb(f"ml{p}", [2 * TPB, P], F32R) for p in range(2)]
        u = sb("u", [P, CH])
        inv = sb("inv", [P, TPC, 4])
        psS = ph.enter_context(nc.psum_tensor(tag + "psS", [P, 4, CH], F32))
        psO = ph.enter_context(nc.psum_tensor(tag + "psO", [P, CH], F32))
        psM = ph.enter_context(nc.psum_tensor(tag + "psM", [P, RING, CH], F32))
        zero_d, zeroed, ring_ready, ring_free, comb, mh_ok, sc, ex, pv, u_ok, inv_ok, o_ok = (
            sem("zero_d"), sem("zeroed"), sem("ring_ready"), sem("ring_free"), sem("comb"), sem("mh_ok"), sem("sc"),
            sem("ex"), sem("pv"), sem("u_ok"), sem("inv_ok"), sem("o_ok"))
        d_in = [sem(f"d_in{p}") for p in range(2)]
        r_in = [sem(f"r_in{p}") for p in range(2)]
        v_in = [sem(f"v_in{p}") for p in range(2)]
        m_in = [sem(f"m_in{p}") for p in range(2)]
        block = ph.enter_context(nc.Block())
        f = lambda ap: ap.bitcast(F32)

        def unit(scr, n):
            return scr[bass.ds(n, 1)].rearrange("o p c -> p (o c)")

        def load_d(eng, n, p):
            q, kk = qk_scr[0, 0], qk_scr[0, 1]
            eng.dma_start(f(kd[p][:, :]), unit(kk, n)).then_inc(d_in[p], 16)
            for h in range(4):
                r = slice(HP * h, HP * h + HD)
                eng.dma_start(f(qd[p][r, h, :]), unit(q[:, r, :], n)).then_inc(d_in[p], 16)

        def load_r(eng, n, p):
            for b in range(4):
                q = qk_scr[b // 2, 0, bass.ds(n, 1)].rearrange("o (h e) c -> e (o h) c", h=4)
                kk = qk_scr[b % 2, 1, bass.ds(n, 1)].rearrange("o (h e) c -> e (o h) c", h=4)
                eng.dma_start(f(qr[p][HP * b:HP * b + HD, :, :]), q[0:HD]).then_inc(r_in[p], 16)
                eng.dma_start(f(kr[p][HP * b:HP * b + HD + 1, :, :]), kk[0:HD + 1]).then_inc(r_in[p], 16)

        def load_v(eng, n, p):
            eng.dma_start(vq[p][:, :, :], v_scr[bass.ds(n, 1)].rearrange("o t p c -> p (o t) c")).then_inc(v_in[p], 16)

        def load_m(eng, p, half):
            for b in range(4):
                src = (mh if b < 2 else ml)[half]
                row = HP * b + HD
                eng.dma_start(f(qr[p][row:row + 1, 2 * half:2 * half + 2, :]).rearrange("o h (t c) -> o (h t) c", c=P),
                              f(src[:, :])).then_inc(m_in[p], 16)

        def iterations(eng, body):
            with eng.Fori(0, NQ // 2 - 1) as i:
                for p in range(2):
                    body(i * 2 + p, i, p, FIRST_USES + (i * 2 + p) * UNIT_USES, True, True)
            start = FIRST_USES + (NQ - 2) * UNIT_USES
            body(NQ - 2, NQ // 2 - 1, 0, start, True, False)
            body(NQ - 1, NQ // 2 - 1, 1, start + UNIT_USES - EARLY, False, False)

        def uses(find, ahead):
            at, steps = 0, []
            for step in ring_plan(find, ahead):
                steps.append([])
                for kind, e in step:
                    steps[-1].append((kind, e, at, (FIRST_USES + at) % RING))
                    at += WIDTH(kind)
            return steps

        first = [("max", e) for e in range(NMX)]
        first.insert(NMX // 2 + 4, ("turn", 0))
        first += [("max2", e) for e in range(EARLY)]
        first.insert(NMX + 1 + 4, ("turn", 1))
        opening, at = [], 0
        for kind, e in first:
            opening.append((kind, e, at, at % RING))
            at += WIDTH(kind)
        assert at == FIRST_USES
        opening_turn = [a for kind, e, a, b in opening if kind == "turn"]
        END = FIRST_USES + (NQ - 1) * UNIT_USES - EARLY + 4

        @block.sync
        def _(sp):
            sp.wait_ge(zero_d, 1)
            load_d(sp, 0, 0)
            sp.wait_ge(zeroed, 1)
            load_d(sp, 1, 1)
            sp.wait_ge(zeroed, 3)
            load_r(sp, 0, 0)
            load_v(sp, 0, 0)
            sp.wait_ge(zeroed, 5)
            load_r(sp, 1, 1)
            load_v(sp, 1, 1)
            for half in range(2):
                sp.wait_ge(ring_free, RING + opening_turn[half] + 2)
                load_m(sp, 0, half)

            def body(n, i, p, start, find, ahead):
                if ahead:
                    sp.wait_ge(ring_ready, start)
                    load_d(sp, n + 2, p)
                turns = {e: a for step in uses(find, ahead) for kind, e, a, b in step if kind == "turn"}
                for half in turns:
                    sp.wait_ge(ring_free, RING + start + turns[half] + 2)
                    load_m(sp, 1 - p, half)
                if ahead:
                    sp.wait_ge(sc, 2 * NS * (n + 1))
                    load_r(sp, n + 2, p)
                    sp.wait_ge(pv, 2 + NS * (n + 1))
                    load_v(sp, n + 2, p)

            iterations(sp, body)

        @block.gpsimd
        def _(pool):
            pool.memset(u[:, :], 1.0).then_inc(u_ok, 1)
            pool.memset(f(qd[1][:, :, :]), 0.0).then_inc(zeroed, 1)
            for p in range(2):
                pool.memset(f(qr[p][:, :, :]), 0.0).then_inc(zeroed, 1)
                pool.memset(f(kr[p][:, :, :]), 0.0).then_inc(zeroed, 1)

        @block.scalar
        def _(act):
            act.sem_inc(ex, 2)

            def exps(n, s):
                for pr in range(2):
                    act.wait_ge(sc, 2 * NS * n + 2 * s + pr + 1)
                    act.wait_ge(pv, NS * n + s + 1)
                    act.activation(probs[s % 2][:, 2 * pr:2 * pr + 2, :], psS[:, 2 * pr:2 * pr + 2, :],
                                   ACT.Exp, scale=SCALE).then_inc(ex, 1)

            def take(n, half):
                act.wait_ge(pv, 2 + NS * n + TPB * (half + 1))
                act.wait_ge(o_ok, 2 * n + half + 1)
                act.activation(u[:, :], psO[:, :], ACT.Copy).then_inc(u_ok, 1)

            exps(0, 0)

            def body(n, i, p, start, find, ahead):
                for s in range(1, NS):
                    exps(n, s)
                    if s == TPB:
                        take(n, 0)
                if find:
                    exps(n + 1, 0)
                take(n, 1)

            iterations(act, body)

        @block.vector
        def _(dve):
            dve.memset(f(qd[0][:, :, :]), 0.0).then_inc(zero_d, 1)
            dve.sem_inc(ring_free, RING)

            def serve(kind, e, use, bank, m, n, sent=None):
                dve.wait_ge(ring_ready, use + WIDTH(kind))
                if kind == "max":
                    dve.tensor_reduce(mx[:, e // 2, e % 2:e % 2 + 1], psM[:, bank, :], AX, ALU.max).then_inc(ring_free, 1)
                    if (e + 1) % (NMX // 2) == 0:
                        half = e // (NMX // 2)
                        cols = slice(half * 2 * TPB, (half + 1) * 2 * TPB)
                        dve.wait_ge(ring_free, RING + use + 1)
                        dve.tensor_tensor(mm_[:, cols], mx[:, cols, 0], mx[:, cols, 1], ALU.max).then_inc(comb, 1)
                elif kind == "turn":
                    src = psM[0:2 * TPB, bank, 0:P]
                    if sent and e == 0:
                        sent()
                    dve.tensor_scalar(mh[e][:, :], src, -1.0, None, ALU.mult).then_inc(mh_ok, 1)
                    dve.wait_ge(mh_ok, 2 * m + e + 1)
                    dve.scalar_tensor_tensor(out=ml[e][:, :], in0=src, scalar=-1.0, in1=f(mh[e][:, :]),
                                             op0=ALU.mult, op1=ALU.subtract).then_inc(ring_free, 2)
                elif kind == "sums":
                    dve.reciprocal(inv[:, :, :], psM[:, bank, 0:TPC * 4].rearrange("p (t h) -> p t h", h=4)).then_inc(inv_ok, 1)
                    dve.wait_ge(inv_ok, 2 * n + 2 - e)
                    dve.sem_inc(ring_free, 1)
                else:
                    dve.wait_ge(u_ok, 2 * n + 2 - e)
                    dve.tensor_tensor(oT[:, bass.ds(n + 1 - e, 1), e * CH:(e + 1) * CH].rearrange("p o c -> p (o c)"),
                                      u[:, :], psM[:, bank, :], ALU.mult).then_inc(o_ok, 1)
                    dve.wait_ge(o_ok, 2 * n + 2 - e)
                    dve.sem_inc(ring_free, 1)

            for kind, e, use, bank in opening:
                if kind == "max2" and e == 0:
                    dve.wait_ge(comb, 2)
                serve("max" if kind == "max2" else kind, e, use, bank, 0, 0)

            def body(n, i, p, start, find, ahead):
                sent = lambda: dve.wait_ge(m_in[p], 128 * (i + 1))
                for step in uses(find, ahead):
                    for kind, e, at, bank in step:
                        if kind == "max2" and e == 0:
                            dve.wait_ge(comb, 2 * (n + 2))
                        serve("max" if kind == "max2" else kind, e, start + at, bank, n + 1, n, sent)

            iterations(dve, body)
            serve("sums", 1, END, END % RING, None, NQ)
            serve("spread", 1, END + 1, (END + 1) % RING, None, NQ)

        @block.tensor
        def _(pe):
            pe.sem_inc(pv, 2)

            def fill(kind, e, use, bank, m, pm, n):
                pe.wait_ge(ring_free, use + 1)
                if kind == "max":
                    h, t, kh = e // (2 * TPB), e // 2 % TPB, e % 2
                    pe.matmul(psM[:, bank, :], qd[pm][:, h, t * P:(t + 1) * P], kd[pm][:, kh * CH:(kh + 1) * CH],
                              start=True, stop=True).then_inc(ring_ready, 1)
                elif kind == "turn":
                    pe.wait_ge(comb, 2 * m + e + 1)
                    pe.transpose(psM[0:2 * TPB, bank, 0:P], mm_[:, e * 2 * TPB:(e + 1) * 2 * TPB],
                                 k["ident"][:, :]).then_inc(ring_ready, 2)
                elif kind == "sums":
                    pe.wait_ge(u_ok, 2 * n + 2 - e)
                    for t in range(TPC):
                        r = pe.matmul(psM[:, bank, 4 * t:4 * t + 4], u[:, t * P:(t + 1) * P], k["sumrow"][:, :],
                                      start=True, stop=True)
                    r.then_inc(ring_ready, 1)
                else:
                    pe.wait_ge(inv_ok, 2 * n + 2 - e)
                    for t in range(TPC):
                        for h in range(4):
                            r = pe.matmul(psM[HP * h:HP * (h + 1), bank, t * P:(t + 1) * P],
                                          inv[:, t, h:h + 1].broadcast_to([P, HP]), k["ident"][:, :], start=True, stop=True)
                    r.then_inc(ring_ready, 1)

            def scores(n, p, s, pr):
                half, kt = s // TPB, s % TPB
                pe.wait_ge(ex, 2 * NS * n + 2 * s + pr + 1)
                for h in (2 * pr, 2 * pr + 1):
                    r = pe.matmul(psS[:, h, :], kr[p][:, h, kt * P:(kt + 1) * P],
                                  qr[p][:, h, half * CH:(half + 1) * CH], start=True, stop=True)
                r.then_inc(sc, 1)

            def pv_step(n, i, p, s):
                half, kt = s // TPB, s % TPB
                if s == 0:
                    pe.wait_ge(v_in[p], 16 * (i + 1))
                if kt == 0:
                    pe.wait_ge(u_ok, 2 * n + half + 1)
                pe.wait_ge(ex, 2 + 2 * NS * n + 2 * s + 2)
                for h in range(4):
                    r = pe.matmul(psO[HP * h:HP * (h + 1), :], vq[p][:, kt, HP * h:HP * (h + 1)], probs[s % 2][:, h, :],
                                  start=(kt == 0), stop=(kt == TPB - 1))
                r.then_inc(pv, 1)

            def loaded(n, i, p):
                pe.wait_ge(r_in[p], 128 * (i + 1))
                pe.wait_ge(m_in[p], 128 * (i + 1))

            pe.wait_ge(d_in[0], 80)
            for kind, e, use, bank in opening:
                if kind == "max2" and e == 0:
                    pe.wait_ge(d_in[1], 80)
                fill("max" if kind == "max2" else kind, e, use, bank, 0, int(kind == "max2"), 0)
            loaded(0, 0, 0)
            for pr in range(2):
                scores(0, 0, 0, pr)

            def body(n, i, p, start, find, ahead):
                plan = uses(find, ahead)
                for s in range(NS):
                    if s == NS - 1 and find:
                        loaded(n + 1, i + p, 1 - p)
                    cut = len(plan[s]) // 2
                    for pr in range(2):
                        if s < NS - 1:
                            scores(n, p, s + 1, pr)
                        elif find:
                            scores(n + 1, 1 - p, 0, pr)
                        for kind, e, at, bank in plan[s][cut * pr:cut if pr == 0 else None]:
                            if kind == "max2" and e == 0:
                                pe.wait_ge(d_in[p], 80 * (i + 2))
                            fill("max" if kind == "max2" else kind, e, start + at, bank, n + 1,
                                 p if kind == "max2" else 1 - p, n)
                    pv_step(n, i, p, s)

            iterations(pe, body)
            fill("sums", 1, END, END % RING, None, None, NQ)
            fill("spread", 1, END + 1, (END + 1) % RING, None, None, NQ)


class FeedTensors:

    def __init__(self, nc, ctx, l):
        tag = f"f{l}_"
        sb = lambda n, s, dt=F32: ctx.enter_context(nc.sbuf_tensor(tag + n, s, dt))
        sem = ctx.enter_context(signals(nc, tag))
        self.moe = l == 0
        self.n_exp = n = NE if self.moe else 1
        self.XH = sb("XH", [P, 2, TOK], F32R)
        self.XL = sb("XL", [P, 2, TOK], F32R)
        self.X8 = sb("X8", [P, TOK], F32R)
        self.b1 = sb("b1", [P, n, KT])
        self.b2 = sb("b2", [P, n, C])
        self.gate = sb("gate", [P, NB, C])
        self.b_in, self.raw_in, self.split, self.h_ok = sem("b_in"), sem("raw_in"), sem("split"), sem("h_ok")
        self.slots = [self.slot(sb, 0)]

    @staticmethod
    def slot(sb, p):
        return (sb(f"W1H{p}", [P, 2, FF], F32R), sb(f"W1L{p}", [P, 2, FF], F32R), sb(f"W18{p}", [P, FF], F32R),
                sb(f"W2H{p}", [P, KT, C], F32R), sb(f"W2L{p}", [P, KT, C], F32R), sb(f"b1e{p}", [P, KT]))


def low_parts(pool, ff, raw1, raw2, e, slot):
    W1H, W1L, W18, W2H, W2L, b1e = slot
    pool.tensor_tensor(W1L[:, :, :], raw1[:, 0:2, :], W1H[:, :, :].bitcast(F32), ALU.subtract).then_inc(ff.h_ok, 1)
    for n, b in enumerate((1, 3)):
        pool.wait_ge(ff.h_ok, 4 * e + 2 + n)
        rows = slice(32 * b, 32 * b + 32)
        pool.tensor_tensor(W18[rows, :], raw1[rows, 2, :], W18[rows, :].bitcast(F32), ALU.subtract).then_inc(ff.h_ok, 1)
    pool.wait_ge(ff.h_ok, 4 * e + 4)
    pool.tensor_tensor(W2L[:, :, :], raw2[:, :, :], W2H[:, :, :].bitcast(F32), ALU.subtract).then_inc(ff.split, 1)


def project_out(nc, d, k, l, x, oT, ff):
    with ExitStack() as ph:
        tag = f"p{l}_"
        sb = lambda n, s, dt=F32: ph.enter_context(nc.sbuf_tensor(tag + n, s, dt))
        sem = ph.enter_context(signals(nc, tag))
        raw1 = sb("raw1", [P, FT, FF])
        raw2 = sb("raw2", [P, KT, C])
        wp = sb("wp", [P, QUADS, C])
        bp = sb("bp", [P, C])
        gate = sb("gate", [P, NB, C])
        t = sb("t", [P, 2, C])
        t2 = sb("t2", [P, 2, C])
        ps = ph.enter_context(nc.psum_tensor(tag + "ps", [P, 4, CH], F32))
        w_in, mm, freed, gated, added = sem("w_in"), sem("mm"), sem("freed"), sem("gated"), sem("added")
        block = ph.enter_context(nc.Block())

        @block.sync
        def _(sp):
            sp.dma_start(wp[:, :, :], d[f"wp{l}"]).then_inc(w_in, 16)
            sp.dma_start(bp[:, :], d[f"bp{l}"].partition_broadcast(P)).then_inc(w_in, 16)
            sp.dma_start(gate[:, :, :], k["gate_scr"][l, 0]).then_inc(w_in, 16)
            sp.dma_start(ff.b1[:, :, :], d[f"b1_{l}"]).then_inc(ff.b_in, 16)
            sp.dma_start(raw1[:, :, :], d[f"w1_{l}"][0]).then_inc(ff.raw_in, 16)
            sp.dma_start(raw2[:, :, :], d[f"w2_{l}"][0]).then_inc(ff.raw_in, 16)
            sp.dma_start(ff.gate[:, :, :], k["gate_scr"][l, 1]).then_inc(ff.b_in, 16)
            for e in range(ff.n_exp):
                sp.dma_start(ff.b2[:, e, :], d[f"b2_{l}"][e].partition_broadcast(P)).then_inc(ff.b_in, 16)

        @block.tensor
        def _(pe):
            pe.wait_ge(w_in, 48)
            for n in range(TILES):
                if n >= 4:
                    pe.wait_ge(freed, n - 3)
                for q in range(QUADS):
                    o = oT[:, 1 + n // TPB * QUADS + q, n % TPB * P:(n % TPB + 1) * P]
                    r = pe.matmul(ps[:, n % 4, 0:C], o, wp[:, q, :], start=(q == 0), stop=(q == QUADS - 1))
                r.then_inc(mm, 1)

        @block.scalar
        def _(act):
            W1H, W1L, W18, W2H, W2L, b1e = ff.slots[0]
            act.wait_ge(ff.b_in, 16 * (2 + ff.n_exp))
            act.activation(b1e[:, :], ff.b1[:, 0, :], ACT.Copy)
            act.wait_ge(ff.raw_in, 32)
            act.activation(W1H[:, :, :], raw1[:, 0:2, :], ACT.Copy)
            act.activation(W18[:, :], raw1[:, 2, :], ACT.Copy)
            act.activation(W2H[:, :, :], raw2[:, :, :], ACT.Copy).then_inc(ff.h_ok, 1)

        @block.gpsimd
        def _(pool):
            pool.wait_ge(ff.h_ok, 1)
            low_parts(pool, ff, raw1, raw2, 0, ff.slots[0])

        @block.vector
        def _(dve):
            dve.wait_ge(w_in, 48)
            for n in range(TILES):
                dve.wait_ge(mm, n + 1)
                if n >= 2:
                    dve.wait_ge(gated, n - 1)
                dve.tensor_tensor(t[:, n % 2, :], ps[:, n % 4, 0:C], bp[:, :], ALU.add).then_inc(freed, 1)
                dve.wait_ge(freed, n + 1)
                if n >= 2:
                    dve.wait_ge(added, n - 1)
                dve.tensor_tensor(t2[:, n % 2, :], t[:, n % 2, :], gate[:, n // TPB, :], ALU.mult).then_inc(gated, 1)
                dve.wait_ge(gated, n + 1)
                dve.tensor_tensor(x[:, n, :], x[:, n, :], t2[:, n % 2, :], ALU.add).then_inc(added, 1)


def feed_forward(nc, d, k, l, x, oT, ff):
    moe, n_exp = ff.moe, ff.n_exp
    func = ACT.Gelu if l == 1 else ACT.Gelu_apprx_tanh
    CHUNKS = NB * CPB
    M = CHUNKS * KT
    DN0 = 2 * M
    XH, XL, X8, b1, b2, gate = ff.XH, ff.XL, ff.X8, ff.b1, ff.b2, ff.gate
    b_in, raw_in, split, h_ok = ff.b_in, ff.raw_in, ff.split, ff.h_ok
    tag = f"g{l}_"
    with ExitStack() as outer:
        cw = outer.enter_context(nc.sbuf_tensor(tag + "cw", [P, TILES, NE], F32)) if moe else None

        with ExitStack() as ph:
            sb = lambda n, s, dt=F32: ph.enter_context(nc.sbuf_tensor(tag + n, s, dt))
            sem = ph.enter_context(signals(nc, tag))
            prep = Prep(nc, ph, sem, k, l, 1, x, tag)
            if moe:
                wg = sb("wg", [P, FT, NE])
                lg = sb("lg", [P, TILES, NE])
                cmp = sb("cmp", [P, TILES, NE, NE - 1])
                top = sb("top", [P, TILES])
                ee = sb("ee", [P, TILES, NE])
                psG = ph.enter_context(nc.psum_tensor(tag + "psG", [P, TPB, NE], F32))
                g_in, g_mm, g_got, g_dve, g_exp = sem("g_in"), sem("g_mm"), sem("g_got"), sem("g_dve"), sem("g_exp")
            block = ph.enter_context(nc.Block())

            if moe:
                @block.sync
                def _(sp):
                    sp.dma_start(wg[:, :, :], d["wg"]).then_inc(g_in, 16)

            def stack(i, c):
                at = bass.ds(i * SEQ + c * CH, CH)
                return XH[:, :, at], XL[:, :, at], X8[:, at]

            @block.gpsimd
            def _(pool):
                pool.sem_inc(prep.s_l, CPB)
                with pool.Fori(0, NB) as i:
                    for c in range(CPB):
                        h, lo, e8 = stack(i, c)
                        prep.low(pool, i, c, h, lo, e8)

            @block.scalar
            def _(act):
                with act.Fori(0, NB) as i:
                    prep.deviation(act, i)
                    for c in range(CPB):
                        h, lo, e8 = stack(i, c)
                        prep.high(act, i, c, h, e8)
                if moe:
                    act.wait_ge(g_dve, 2)
                    act.activation(ee[:, :, :], ee[:, :, :], ACT.Exp).then_inc(g_exp, 1)

            @block.vector
            def _(dve):
                dve.sem_inc(prep.s_y, 1)
                with dve.Fori(0, NB) as i:
                    prep.normalise(dve, i)
                    for c in range(CPB):
                        prep.modulate(dve, i, c)
                    if moe:
                        dve.wait_ge(g_mm, i + 1)
                        dve.tensor_copy(lg[:, bass.ds(i * TPB, TPB), :], psG[:, :, :]).then_inc(g_got, 1)
                if moe:
                    done = count(1)

                    dve.wait_ge(g_got, NB)
                    dve.tensor_reduce(top[:, :], lg[:, :, :], AX, ALU.max).then_inc(g_dve, 1)
                    dve.wait_ge(g_dve, next(done))
                    dve.tensor_tensor(ee[:, :, :], lg[:, :, :], top[:, :].unsqueeze(2).broadcast_to([P, TILES, NE]), ALU.subtract).then_inc(g_dve, 1)
                    dve.wait_ge(g_dve, next(done))
                    for e in range(NE):
                        for a, j in enumerate(j for j in range(NE) if j != e):
                            r = dve.tensor_tensor(cmp[:, :, e, a], lg[:, :, j], lg[:, :, e], ALU.is_ge if j < e else ALU.is_gt)
                    r.then_inc(g_dve, 1)
                    dve.wait_ge(g_dve, next(done))
                    dve.tensor_reduce(cw[:, :, :], cmp[:, :, :, :], AX, ALU.add).then_inc(g_dve, 1)
                    dve.wait_ge(g_dve, next(done))
                    dve.tensor_scalar(cw[:, :, :], cw[:, :, :], 2.0, None, ALU.is_lt).then_inc(g_dve, 1)
                    dve.wait_ge(g_dve, next(done))
                    dve.wait_ge(g_exp, 1)
                    dve.tensor_tensor(cw[:, :, :], cw[:, :, :], ee[:, :, :], ALU.mult).then_inc(g_dve, 1)
                    dve.wait_ge(g_dve, next(done))
                    dve.tensor_reduce(top[:, :], cw[:, :, :], AX, ALU.add).then_inc(g_dve, 1)
                    dve.wait_ge(g_dve, next(done))
                    dve.reciprocal(top[:, :], top[:, :]).then_inc(g_dve, 1)
                    dve.wait_ge(g_dve, next(done))
                    dve.tensor_tensor(cw[:, :, :], cw[:, :, :], top[:, :].unsqueeze(2).broadcast_to([P, TILES, NE]), ALU.mult).then_inc(g_dve, 1)
                    dve.wait_ge(g_dve, next(done))

            @block.tensor
            def _(pe):
                if moe:
                    pe.wait_ge(g_in, 16)
                with pe.Fori(0, NB) as i:
                    for c in range(CPB):
                        prep.transpose(pe, i, c)
                        if moe:
                            pe.wait_ge(prep.s_y, i * CPB + c + 2)
                            for t in range(TPC):
                                cols = slice(t * P, (t + 1) * P)
                                for f, rows in enumerate((P, P, TAIL)):
                                    r = pe.matmul(psG[:, c * TPC + t, :], prep.y[0:rows, c, f, cols], wg[0:rows, f, :],
                                                  start=(f == 0), stop=(f == FT - 1))
                    if moe:
                        r.then_inc(g_mm, 1)

        with ExitStack() as ph:
            sb = lambda n, s, dt=F32: ph.enter_context(nc.sbuf_tensor(tag + n, s, dt))
            sem = ph.enter_context(signals(nc, tag))
            slots = ff.slots + ([ff.slot(sb, 1)] if moe else [])
            W1H, W1L, W18, W2H, W2L, b1e = zip(*slots)
            cwe = sb("cwe", [P, TILES])
            GS = 3
            room, at = oT[:, :, :].rearrange("p n c -> p (n c)"), 0
            views = []
            for shape in ((FT, FF), (KT, C), (GS, CH), (TPC, C)):
                size = shape[0] * shape[1]
                views.append(room[:, at:at + size].rearrange("p (a c) -> p a c", c=shape[1]))
                at += size
            raw1, raw2, g32, tb = views
            gh = sb("gh", [P, GS, CH], F32R)
            gl = sb("gl", [P, GS, CH], F32R)
            psU = ph.enter_context(nc.psum_tensor(tag + "psU", [P, GS, CH], F32))
            psA = ph.enter_context(nc.psum_tensor(tag + "psA", [P, TPC, CH], F32))
            up, acted, glow, dn, taken, me = (
                sem("up"), sem("acted"), sem("glow"), sem("dn"), sem("taken"), sem("self"))
            block = ph.enter_context(nc.Block())

            def experts(eng, body):
                if n_exp == 1:
                    body(0, 0)
                    return
                with eng.Fori(0, n_exp // 2) as i:
                    for p in range(2):
                        body(i * 2 + p, p)

            @block.sync
            def _(sp):
                if moe:
                    with sp.Fori(1, NE) as e:
                        sp.wait_ge(split, e)
                        sp.dma_start(raw1[:, :, :], d[f"w1_{l}"][bass.ds(e, 1)].rearrange("o p f n -> p (o f) n")).then_inc(raw_in, 16)
                        sp.dma_start(raw2[:, :, :], d[f"w2_{l}"][bass.ds(e, 1)].rearrange("o p f n -> p (o f) n")).then_inc(raw_in, 16)

            @block.gpsimd
            def _(pool):
                for e in range(1, n_exp):
                    p = e % 2
                    pool.wait_ge(raw_in, 32 * (e + 1))
                    pool.wait_ge(dn, DN0 + M * (e - 1))
                    pool.tensor_copy(b1e[p][:, :], b1[:, e, :])
                    pool.tensor_copy(W1H[p][:, :, :], raw1[:, 0:2, :])
                    pool.tensor_copy(W18[p][:, :], raw1[:, 2, :])
                    pool.tensor_copy(W2H[p][:, :, :], raw2[:, :, :]).then_inc(h_ok, 1)
                    pool.wait_ge(h_ok, 4 * e + 1)
                    low_parts(pool, ff, raw1, raw2, e, slots[p])

            @block.scalar
            def _(act):
                act.sem_inc(acted, GS)

                def body(e, p):
                    act.wait_ge(split, e + 1)
                    for m in range(M):
                        g = M * e + m
                        act.wait_ge(up, g + 1)
                        act.wait_ge(dn, DN0 + g - GS + 1)
                        act.wait_ge(glow, g + 1)
                        bias = b1e[p][:, m % KT:m % KT + 1]
                        act.activation(gh[:, m % GS, :], psU[:, m % GS, :], func, bias=bias)
                        act.activation(g32[:, m % GS, :], psU[:, m % GS, :], func, bias=bias).then_inc(acted, 1)

                experts(act, body)

            @block.vector
            def _(dve):
                dve.sem_inc(glow, GS)
                dve.sem_inc(taken, TPC)
                dve.wait_ge(b_in, 16 * (2 + n_exp))
                per = (1 if moe else 0) + CHUNKS * TPC * 2

                def body(e, p):
                    before = e * per + (1 if moe else 0)
                    if moe:
                        dve.tensor_copy(cwe[:, :], cw[:, :, bass.ds(e, 1)].rearrange("p t o -> p (t o)")).then_inc(me, 1)

                    def take(c):
                        dve.wait_ge(dn, DN0 + M * e + KT * (c + 1))
                        for t in range(TPC):
                            dve.tensor_tensor(tb[:, t, :], psA[:, t, 0:C], b2[:, bass.ds(e, 1), :].rearrange("p o n -> p (o n)"),
                                              ALU.add).then_inc(taken, 1)

                    def add(c, t):
                        n = c * TPC + t
                        dve.wait_ge(taken, TPC + CHUNKS * TPC * e + TPC * c + t + 1)
                        if moe and n == 0:
                            dve.wait_ge(me, before)
                        dve.scalar_tensor_tensor(
                            out=tb[:, t, :], in0=tb[:, t, :], scalar=cwe[:, n:n + 1] if moe else 1.0,
                            in1=gate[:, n // TPB, :], op0=ALU.mult, op1=ALU.mult).then_inc(me, 1)
                        dve.wait_ge(me, before + 2 * n + 1)
                        dve.tensor_tensor(x[:, n, :], x[:, n, :], tb[:, t, :], ALU.add).then_inc(me, 1)
                        dve.wait_ge(me, before + 2 * n + 2)

                    for m in range(M + 2):
                        g = M * e + m
                        if m < M:
                            dve.wait_ge(acted, g + 1 + GS)
                            dve.wait_ge(dn, DN0 + g - GS + 1)
                            dve.tensor_tensor(gl[:, m % GS, :], g32[:, m % GS, :], gh[:, m % GS, :].bitcast(F32),
                                              ALU.subtract).then_inc(glow, 1)
                        c, r = divmod(m - 2 - (KT - 1), KT)
                        if c >= 0 and r == 0:
                            take(c)
                        if c >= 0 and 1 <= r <= TPC:
                            add(c, r - 1)
                    for t in range(TPC):
                        add(CHUNKS - 1, t)

                experts(dve, body)

            @block.tensor
            def _(pe):
                pe.sem_inc(dn, DN0)

                def down(e, p, m):
                    g, c, kt = M * e + m, m // KT, m % KT
                    pe.wait_ge(glow, g + 1 + GS)
                    for t in range(TPC):
                        if kt == 0:
                            pe.wait_ge(taken, CHUNKS * TPC * e + TPC * c + t + 1)
                        cols = slice(t * P, (t + 1) * P)
                        for a, (lhs, rhs) in enumerate(((gh, W2H), (gl, W2H), (gh, W2L))):
                            r = pe.matmul(psA[:, t, 0:C], lhs[:, m % GS, cols], rhs[p][:, kt, :],
                                          start=(kt == 0 and a == 0), stop=(kt == KT - 1 and a == 2))
                    r.then_inc(dn, 1)

                def body(e, p):
                    pe.wait_ge(split, e + 1)
                    for m in range(M + 2):
                        if m < M:
                            g, c, kt = M * e + m, m // KT, m % KT
                            cols = slice(kt * P, (kt + 1) * P)
                            at = slice(c * CH, (c + 1) * CH)
                            pe.wait_ge(acted, g + 1)
                            terms = [(w_[p][:, f, cols], x_[:, f, at]) for x_, w_ in ((XH, W1H), (XL, W1H), (XH, W1L)) for f in range(2)]
                            terms.append((W18[p][:, cols], X8[:, at]))
                            for a, (lhs, rhs) in enumerate(terms):
                                r = pe.matmul(psU[:, m % GS, :], lhs, rhs, start=(a == 0), stop=(a == 6))
                            r.then_inc(up, 1)
                        if m >= 2:
                            down(e, p, m - 2)

                experts(pe, body)


def build(nc, d, out):
    with ExitStack() as ctx:
        k = {}
        consts(nc, ctx, k)
        x = ctx.enter_context(nc.sbuf_tensor("x", [P, TILES, C], F32))
        qk_scr = nc.dram_tensor("qk_scr", (2, 2, NQ, P, SEQ), F32, kind="Internal").ap()
        v_scr = nc.dram_tensor("v_scr", (NQ, TPB, P, P), F32, kind="Internal").ap()
        condition(nc, ctx, d, k)
        rotate(nc, d, k, x)
        oT = ctx.enter_context(nc.sbuf_tensor("oT", [P, NQ + 1, SEQ], F32))
        for l in range(3):
            project_qkv(nc, d, k, l, x, qk_scr, v_scr)
            attend(nc, d, k, l, qk_scr, v_scr, oT)
            with ExitStack() as fed:
                ff = FeedTensors(nc, fed, l)
                project_out(nc, d, k, l, x, oT, ff)
                feed_forward(nc, d, k, l, x, oT, ff)
        stored = ctx.enter_context(nc.semaphore("stored"))
        with nc.Block() as block:

            @block.sync
            def _(sp):
                sp.dma_start(out.rearrange("b s c -> (b s) c").rearrange("(t p) c -> p t c", p=P), x[:, :, :]).then_inc(stored, 16)
                sp.wait_ge(stored, 16)


_OUT = ((NB, SEQ, C), "float32")


def _layout(a):
    import numpy as np

    z = lambda *s: np.zeros(s, np.float32)
    d = {}

    def stack(w):
        tail = np.concatenate([w[2 * P:]] * 4, 0)
        return np.ascontiguousarray(np.stack([w[0:P], w[P:2 * P], tail], 1))

    def heads(w, one=None):
        p = z(*w.shape[:-1], NH, HP)
        p[..., :HD] = w.reshape(*w.shape[:-1], NH, HD)
        if one:
            p[..., SUMCOL] = 1.0
        return p.reshape(*w.shape[:-1], NH * HP)

    d["x"] = a["x"].reshape(TOK, C)
    d["xT"] = np.ascontiguousarray(d["x"].T)
    d["condT"] = np.ascontiguousarray(a["cond_1152"].T)
    d["PT"] = np.ascontiguousarray(a["L0_cond_P"].T)
    iu, ju = np.triu_indices(RD, k=1)
    w = z(RD, RD, C)
    w[iu, ju] = a["L0_cond_W"]
    d["rot_w"] = np.ascontiguousarray(w.reshape(RD * RD, C).T)
    b = z(RD, RD)
    b[iu, ju] = a["L0_cond_b"]
    d["rot_b"] = b.reshape(1, RD * RD)
    names = [
        dict(ada="L1_cond_w_adaln", bada="L1_cond_b_adaln", qkv="L1_cond_w_qkv", bqkv="L1_cond_b_qkv",
             p="L1_cond_w_proj", bp="L1_cond_b_proj", w1="L1_cond_w1", b1="L1_cond_b1", w2="L1_cond_w2", b2="L1_cond_b2"),
        dict(ada="L2_cond_w_ada", bada="L2_cond_b_ada", qkv="L2_cond_w_qkv", bqkv="L2_cond_b_qkv",
             p="L2_cond_w_proj", bp="L2_cond_b_proj", w1="L2_cond_w1", b1="L2_cond_b1", w2="L2_cond_w2", b2="L2_cond_b2"),
        dict(ada="L3_cond_W_ada", bada="L3_cond_b_ada", qkv="L3_cond_W_qkv", bqkv="L3_cond_b_qkv",
             p="L3_cond_W_proj", bp="L3_cond_b_proj", w1="L3_cond_W_fc1", b1="L3_cond_b_fc1", w2="L3_cond_W_fc2", b2="L3_cond_b_fc2"),
    ]
    for l, nm in enumerate(names):
        ada, bada = a[nm["ada"]].reshape(C, 6, C), a[nm["bada"]].reshape(6, C)
        rep = lambda v: np.concatenate([v] + [v[..., 2 * P:]] * 3, -1)
        d[f"wfm{l}"] = np.ascontiguousarray(rep(ada[:, [0, 1, 3, 4]]).reshape(C, 4 * CP))
        d[f"bfm{l}"] = np.ascontiguousarray(rep(bada[[0, 1, 3, 4]]).reshape(4, FT, P).transpose(2, 1, 0))
        d[f"wga{l}"] = np.ascontiguousarray(ada[:, [2, 5]].reshape(C, 2 * C))
        d[f"bga{l}"] = np.ascontiguousarray(bada[[2, 5]])
        qkv, bqkv = a[nm["qkv"]].reshape(C, 3, C), a[nm["bqkv"]].reshape(3, C)
        d[f"wqkv{l}"] = stack(np.concatenate([heads(qkv[:, j]) for j in range(3)], 1))
        bq, bk = heads(bqkv[0]), heads(bqkv[1], True)
        d[f"bqk{l}"] = np.ascontiguousarray(np.concatenate([bq, bk]).reshape(2 * QUADS, P).T)
        d[f"bv{l}"] = heads(bqkv[2], True)
        wp = z(NH, HP, C)
        wp[:, :HD] = a[nm["p"]].reshape(NH, HD, C)
        d[f"wp{l}"] = np.ascontiguousarray(wp.reshape(QUADS, P, C).transpose(1, 0, 2))
        d[f"bp{l}"] = a[nm["bp"]]
        n = NE if l == 0 else 1
        w1, b1 = a[nm["w1"]].reshape(n, C, FF), a[nm["b1"]].reshape(n, KT, P)
        w2, b2 = a[nm["w2"]].reshape(n, KT, P, C), a[nm["b2"]].reshape(n, C)
        d[f"w1_{l}"] = np.stack([stack(w1[e]) for e in range(n)])
        d[f"b1_{l}"] = np.ascontiguousarray(b1.transpose(2, 0, 1))
        d[f"w2_{l}"] = np.ascontiguousarray(w2.transpose(0, 2, 1, 3))
        d[f"b2_{l}"] = b2
    d["wg"] = stack(a["L1_cond_w_gate"])
    g = z(4, 4, HP)
    for j, nm in enumerate(("L2_cond_qn_g", "L2_cond_qn_b", "L2_cond_kn_g", "L2_cond_kn_b")):
        g[j, :, :HD] = a[nm]
    g[3, :, SUMCOL] = 1.0
    d["qkn"] = np.ascontiguousarray(g.reshape(4, P).T)
    return d


def kernel(**inputs):
    import numpy as np
    from concourse import bacc
    from concourse.bass_utils import run_bass_kernel_spmd

    laid = _layout({n: np.asarray(v) for n, v in inputs.items()})
    nc = bacc.Bacc("TRN2", target_bir_lowering=False, num_devices=1)
    arrays, d = {}, {}
    for n, v in laid.items():
        arrays["in_" + n] = v
        d[n] = nc.dram_tensor("in_" + n, v.shape, mybir.dt.from_np(v.dtype), kind="ExternalInput").ap()
    out = nc.dram_tensor("out_0", _OUT[0], F32, kind="ExternalOutput").ap()
    build(nc, d, out)
    r = run_bass_kernel_spmd(nc, [arrays], core_ids=[0])
    return r.results[0]["out_0"]
```

```python
from contextlib import ExitStack, contextmanager
from itertools import count

import concourse.bass as bass
from concourse import mybir

F32 = mybir.dt.float32
F32R = mybir.dt.float32r
ACT = mybir.ActivationFunctionType
ALU = mybir.AluOpType
AX = mybir.AxisListType.X

P = 128
NB, SEQ, C = 2, 1024, 288
TOK = NB * SEQ
TILES = TOK // P
TPB = SEQ // P
NH, HD = 16, 18
HP = 32
QUADS = NH // 4
NQ = NB * QUADS
CH = 512
CPB = SEQ // CH
TPC = CH // P
FT = 3
CP = FT * P
TAIL = C - 2 * P
FF = 4 * C
KT = FF // P
NE = 4
RD = 64
SCALE = float(HD) ** -0.5
LN_EPS = 1e-6
QK_EPS = 1e-5
SCALINGS, TERMS = 10, 8
SQUARES = (RD - 1).bit_length() - 1
SUMCOL = HD


@contextmanager
def signals(nc, tag):
    made = []

    def make(name):
        made.append(nc.alloc_semaphore(tag + name))
        return made[-1]

    yield make
    nc.clear_and_free_semaphores(made)
    nc.all_engine_barrier()


def consts(nc, ctx, out):
    ident = ctx.enter_context(nc.sbuf_tensor("ident", [P, P], F32))
    blocks = ctx.enter_context(nc.sbuf_tensor("blocks", [P, P], F32))
    sumrow = ctx.enter_context(nc.sbuf_tensor("sumrow", [P, 4], F32))
    eps = ctx.enter_context(nc.sbuf_tensor("eps", [P, 2], F32))
    made = ctx.enter_context(nc.semaphore("const_made"))
    with nc.Block() as block:

        @block.gpsimd
        def _(pool):
            pool.memset(ident[:, :], 0.0)
            pool.memset(sumrow[:, :], 0.0)
            pool.memset(eps[:, 0:1], LN_EPS)
            pool.memset(eps[:, 1:2], QK_EPS)
            pool.memset(blocks[:, :], 1.0 / HD).then_inc(made, 1)
            pool.wait_ge(made, 1)
            pool.affine_select(out=ident[:, :], in_=ident[:, :], compare_op=ALU.not_equal, fill=1.0,
                               base=0, pattern=[[-1, P]], channel_multiplier=1)
            pool.affine_select(out=sumrow[:, :], in_=sumrow[:, :], compare_op=ALU.not_equal, fill=1.0,
                               base=-SUMCOL, pattern=[[-HP, 4]], channel_multiplier=1)
            b = blocks[:, :].rearrange("p (a m) -> p a m", a=4)
            pool.affine_select(out=b, in_=b, compare_op=ALU.is_ge, fill=0.0,
                               base=0, pattern=[[-HP, 4], [0, HP]], channel_multiplier=1).then_inc(made, 1)
            pool.wait_ge(made, 2)
            pool.affine_select(out=b, in_=b, compare_op=ALU.is_ge, fill=0.0,
                               base=HD - 1, pattern=[[HP, 4], [0, HP]], channel_multiplier=-1).then_inc(made, 1)
            pool.wait_ge(made, 3)
            pool.affine_select(out=b, in_=b, compare_op=ALU.is_ge, fill=0.0,
                               base=HD - 1, pattern=[[0, 4], [-1, HP]], channel_multiplier=0).then_inc(made, 1)
            pool.wait_ge(made, 4)

    center = ctx.enter_context(nc.sbuf_tensor("center", [P, P], F32))
    with nc.Block() as block:

        @block.vector
        def _(dve):
            dve.tensor_tensor(center[:, :], ident[:, :], blocks[:, :], ALU.subtract)

    out.update(ident=ident, blocks=blocks, sumrow=sumrow, eps=eps, center=center)


MODS = 3 * 6 * C
NCOND = 8
CC = -(-(RD * RD + MODS) // (3 * NCOND))
CW = 3 * CC
QR_UNROLL = 16


def rotate(nc, ctx, d, k, x):
    fm = [ctx.enter_context(nc.sbuf_tensor(f"fm{l}", [P, FT, 4, NB], F32)) for l in range(3)]
    mod_scr = nc.dram_tensor("mod_scr", (NB, NCOND * CW), F32, kind="Internal").ap()
    mods = mod_scr[:, RD * RD:RD * RD + MODS].rearrange("b (l g c) -> b l g c", g=6, c=C)
    k.update(fm=fm, mods=mods)
    ident = k["ident"]
    W = C
    with ExitStack() as ph:
        sb = lambda n, s, dt=F32: ph.enter_context(nc.sbuf_tensor("r_" + n, s, dt))
        sem = ph.enter_context(signals(nc, "r_"))
        condT = sb("condT", [96, 3, NB])
        sig = sb("sig", [96, 3, NB])
        silu = sb("silu", [96, 3, NB])
        wc = sb("wc", [96, 2, 3, CW])
        bc = sb("bc", [NB, 2, CW])
        rows = sb("rows", [NB, 2, CW])
        rot = sb("rot", [RD, NB, RD])
        modr = sb("modr", [2 * FT * 12, P])
        pT = sb("pT", [RD, C])
        A = sb("A", [P, C + RD])
        sel = sb("sel", [P, P])
        scr = sb("scr", [P, C])
        scr2 = sb("scr2", [P, C])
        sc = sb("sc", [P, 16])
        xT = sb("xT", [96, 3, TOK])
        skew = sb("skew", [RD, 4, RD])
        ex = sb("ex", [RD, 2, 4, RD])
        N1 = sb("N1", [RD, 2, RD])
        N1T = sb("N1T", [RD, 2, RD])
        ZT = sb("ZT", [RD, 2, RD])
        rinv = sb("rinv", [RD, RD])
        U = sb("U", [96, 3, RD])
        UT = sb("UT", [RD, C])
        W2 = sb("W2", [RD, NB, C])
        zT = sb("zT", [RD, TOK])
        psR = ph.enter_context(nc.psum_tensor("r_psR", [P, 512], F32))
        psQ = ph.enter_context(nc.psum_tensor("r_psQ", [P, 512], F32))
        psE = ph.enter_context(nc.psum_tensor("r_psE", [P, 512], F32))
        psN = ph.enter_context(nc.psum_tensor("r_psN", [P, 3, 512], F32))
        psZ = ph.enter_context(nc.psum_tensor("r_psZ", [P, 2, 512], F32))
        last = [psZ[:, 0, :], psZ[:, 1, :], psN[:, 0, :], psN[:, 1, :], psN[:, 2, :]]
        loaded, xloaded, dv, row, row2, sel_ok, nsq_ok, nrm_ok, upd, mm, dd, xo = (
            sem("loaded"), sem("xloaded"), sem("dve_self"), sem("row"), sem("row2"), sem("sel"), sem("nsq"), sem("nrm"),
            sem("updated"), sem("mm"), sem("dve_done"), sem("x_out"))
        nd, nm, fixed, c_in, sig_ok, silu_ok, c_mm, c_got, rot_in, mod_in = (
            sem("nd"), sem("nm"), sem("fixed"), sem("c_in"), sem("sig_ok"), sem("silu_ok"), sem("c_mm"), sem("c_got"), sem("rot_in"), sem("mod_in"))
        w_in = [sem(f"w_in{p}") for p in range(2)]
        sent = [sem(f"sent{p}") for p in range(2)]
        block = ph.enter_context(nc.Block())

        @block.sync
        def _(sp):
            def load(j, p):
                cols = bass.ds(j * CW, CW)
                sp.dma_start(wc[:, p, :, :], d["w_cond"][:, cols].rearrange("(a p) n -> p a n", p=96)).then_inc(w_in[p], 16)
                for b in range(NB):
                    sp.dma_start(bc[b:b + 1, p, :], d["b_cond"][:, cols]).then_inc(w_in[p], 16)

            def send(j, p):
                sp.wait_ge(c_got, 3 * (j + 1) + 2)
                sp.dma_start(mod_scr[:, bass.ds(j * CW, CW)], rows[:, p, :]).then_inc(sent[p], 16)

            sp.dma_start(pT[:, :], d["PT"]).then_inc(loaded, 16)
            sp.dma_start(condT[:, :, :], d["condT"].rearrange("(a p) b -> p a b", p=96)).then_inc(c_in, 16)
            for p in range(2):
                load(p, p)
            sp.dma_start(x[:, :, :], d["x"].rearrange("(t p) c -> p t c", p=P)).then_inc(xloaded, 16)
            sp.dma_start(xT[:, :, :], d["xT"].rearrange("(a p) n -> p a n", p=96)).then_inc(xloaded, 16)
            for p in range(2):
                sp.sem_inc(sent[p], 16)
            with sp.Fori(0, NCOND // 2 - 1) as i:
                for p in range(2):
                    send(i * 2 + p, p)
                    load(i * 2 + p + 2, p)
            assert RD * RD <= (NCOND - 2) * CW
            for p in range(2):
                sp.wait_ge(sent[p], 16 * (NCOND // 2))
            for b in range(NB):
                sp.dma_start(rot[:, b, :], mod_scr[b:b + 1, 0:RD * RD].rearrange("o (i j) -> (o i) j", i=RD)).then_inc(rot_in, 16)
            for p in range(2):
                send(NCOND - 2 + p, p)
            for p in range(2):
                sp.wait_ge(sent[p], 16 * (NCOND // 2 + 1))
            for b in range(NB):
                v = mod_scr[b:b + 1, RD * RD:RD * RD + MODS].rearrange("o (lj m c) -> (o lj) m c", m=3, c=C)
                for f in range(FT):
                    at = (b * FT + f) * 12
                    for a in range(4 if f == 2 else 1):
                        cols = slice(HP * a, HP * (a + 1)) if f == 2 else slice(0, P)
                        src = v[:, 0:2, 2 * P:C] if f == 2 else v[:, 0:2, f * P:(f + 1) * P]
                        sp.dma_start(modr[at:at + 12, cols], src).then_inc(mod_in, 16)

        SELF = 9
        CHUNK_END = (3, 6, 7)

        @block.gpsimd
        def _(pool):
            pool.memset(sel[:, :], 1.0).then_inc(sel_ok, 1)
            pool.wait_ge(sel_ok, 1)
            with pool.Fori(0, RD) as s:
                pool.wait_ge(row, s + 1)
                pool.tensor_copy(sel[:, :], ident[:, bass.ds(s, 1)].broadcast_to([P, P])).then_inc(sel_ok, 1)
            pool.wait_ge(upd, RD + 1)
            pool.wait_ge(fixed, RD)
            pool.affine_select(out=N1[:, 0, :], in_=A[0:RD, 0:RD], compare_op=ALU.is_gt, fill=0.0,
                               base=0, pattern=[[-1, RD]], channel_multiplier=1).then_inc(xo, 1)

        @block.scalar
        def _(act):
            act.wait_ge(c_in, 16)
            act.activation(sig[:, :, :], condT[:, :, :], ACT.Sigmoid).then_inc(sig_ok, 1)
            with act.Fori(0, RD // QR_UNROLL) as i:
                for u in range(QR_UNROLL):
                    s = i * QR_UNROLL + u
                    act.wait_ge(row2, s + 1)
                    act.activation(scr2[:, :], psQ[:, 0:W], ACT.Square, accum_out=sc[:, 0:1]).then_inc(nsq_ok, 1)
                    act.wait_ge(nsq_ok, s + 1)
                    act.activation(sc[:, 1:2], sc[:, 0:1], ACT.Sqrt).then_inc(nrm_ok, 1)

        @block.vector
        def _(dve):
            dve.memset(A[:, :], 0.0).then_inc(dv, 1)
            dve.wait_ge(loaded, 16)
            dve.wait_ge(dv, 1)
            dve.tensor_copy(A[0:RD, 0:C], pT[:, :]).then_inc(upd, 1)
            dve.wait_ge(c_in, 16)
            dve.wait_ge(sig_ok, 1)
            dve.tensor_tensor(silu[:, :, :], condT[:, :, :], sig[:, :, :], ALU.mult).then_inc(silu_ok, 1)
            dve.sem_inc(c_got, 2)
            with dve.Fori(0, RD // QR_UNROLL) as i:
                for u in range(QR_UNROLL):
                    s = i * QR_UNROLL + u
                    before = s * SELF + 1
                    a = A[:, bass.ds(s, W)]
                    akk = A[:, bass.ds(s, 1)]
                    dve.wait_ge(row, s + 2)
                    dve.tensor_scalar(sc[:, 4:5], psR[:, 0:1], 0.0, -2.0, ALU.is_ge, ALU.mult).then_inc(dv, 1)
                    dve.scalar_tensor_tensor(out=scr[:, :], in0=psR[:, 0:W], scalar=1.0, in1=a,
                                             op0=ALU.mult, op1=ALU.mult, accum_out=sc[:, 2:3]).then_inc(dv, 1)
                    dve.wait_ge(dv, before + 1)
                    dve.scalar_tensor_tensor(out=sc[:, 3:4], in0=sc[:, 4:5], scalar=1.0, in1=psR[:, 0:1],
                                             op0=ALU.add, op1=ALU.mult).then_inc(dv, 1)
                    dve.wait_ge(nrm_ok, s + 1)
                    dve.wait_ge(dv, before + 3)
                    dve.tensor_scalar(sc[:, 6:7], sc[:, 1:2], sc[:, 3:4], sc[:, 1:2], ALU.subtract, ALU.mult).then_inc(dv, 1)
                    dve.tensor_scalar(sc[:, 5:6], sc[:, 4:5], 1.0, sc[:, 1:2], ALU.add, ALU.mult).then_inc(dv, 1)
                    dve.wait_ge(dv, before + 5)
                    dve.reciprocal(sc[:, 8:9], sc[:, 6:7]).then_inc(dv, 1)
                    dve.tensor_scalar(sc[:, 7:8], akk, sc[:, 5:6], sc[:, 2:3], ALU.mult, ALU.subtract).then_inc(dv, 1)
                    dve.wait_ge(dv, before + 7)
                    dve.tensor_scalar(sc[:, 9:10], sc[:, 7:8], sc[:, 8:9], None, ALU.mult).then_inc(dv, 1)
                    dve.wait_ge(dv, before + 8)
                    dve.scalar_tensor_tensor(out=a, in0=psR[:, 0:W], scalar=sc[:, 9:10], in1=a,
                                             op0=ALU.mult, op1=ALU.add).then_inc(upd, 1)
                    dve.tensor_scalar(sc[:, 10:11], sc[:, 9:10], sc[:, 5:6], -1.0, ALU.mult, ALU.mult).then_inc(dv, 1)
                    dve.wait_ge(upd, s + 2)
                    dve.wait_ge(dv, before + 9)
                    dve.tensor_tensor(akk, akk, sc[:, 10:11], ALU.add).then_inc(fixed, 1)
                    dve.wait_ge(fixed, s + 1)
                    p, v = u // NCOND, u % NCOND
                    if v in CHUNK_END:
                        c, j = CHUNK_END.index(v), i * 2 + p
                        dve.wait_ge(w_in[p], 48 * (i + 1))
                        dve.wait_ge(sent[p], 16 * (i + 1))
                        dve.wait_ge(c_mm, 3 * j + c + 1)
                        cols = slice(c * CC, (c + 1) * CC)
                        dve.tensor_tensor(rows[:, p, cols], psZ[0:NB, (p + c) % 2, 0:CC], bc[:, p, cols],
                                          ALU.add).then_inc(c_got, 1)

            done, ndone = count(1), count(1)

            dve.tensor_tensor(scr[0:RD, 0:RD], A[0:RD, 0:RD], ident[0:RD, 0:RD], ALU.mult).then_inc(nd, 1)
            dve.wait_ge(nd, next(ndone))
            dve.tensor_reduce(sc[0:RD, 12:13], scr[0:RD, 0:RD], AX, ALU.add).then_inc(nd, 1)
            dve.wait_ge(nd, next(ndone))
            dve.reciprocal(sc[0:RD, 11:12], sc[0:RD, 12:13]).then_inc(nd, 1)
            dve.wait_ge(nd, next(ndone))
            dve.wait_ge(xo, 1)
            dve.tensor_scalar(N1[:, 0, :], N1[:, 0, :], sc[0:RD, 11:12], -1.0, ALU.mult, ALU.mult).then_inc(nd, 1)
            dve.wait_ge(nd, next(ndone))
            f = 1.0 / 2 ** SCALINGS
            dve.wait_ge(rot_in, 16 * NB)
            dve.wait_ge(mm, 1)
            for b in range(NB):
                dve.tensor_tensor(skew[:, 2 * b, :], rot[:, b, :], psE[0:RD, b * RD:(b + 1) * RD], ALU.subtract).then_inc(dd, 1)
                dve.wait_ge(dd, next(done))
                dve.tensor_scalar(skew[:, 2 * b + 1, :], skew[:, 2 * b, :], -f, None, ALU.mult).then_inc(dd, 1)
                dve.wait_ge(dd, next(done))
                dve.tensor_scalar(skew[:, 2 * b, :], skew[:, 2 * b, :], f, None, ALU.mult).then_inc(dd, 1)
                dve.wait_ge(dd, next(done))
            idb = ident[0:RD, 0:RD].unsqueeze(1).broadcast_to([RD, 4, RD])
            dve.tensor_copy(ex[:, 0, :, :], idb).then_inc(dd, 1)
            dve.wait_ge(dd, next(done))
            quads = psE[0:RD, 0:4 * RD].rearrange("p (a n) -> p a n", a=4)
            for q in range(TERMS + SCALINGS):
                dve.wait_ge(mm, 2 + q)
                if q < TERMS - 1:
                    dve.scalar_tensor_tensor(out=ex[:, 1 - q % 2, :, :], in0=quads, scalar=1.0 / (TERMS - q), in1=idb,
                                             op0=ALU.mult, op1=ALU.add).then_inc(dd, 1)
                elif q == TERMS - 1:
                    dve.tensor_copy(ex[:, 1 - q % 2, :, :], quads).then_inc(dd, 1)
                else:
                    dve.scalar_tensor_tensor(out=ex[:, 1 - q % 2, :, :], in0=ex[:, q % 2, :, :], scalar=2.0, in1=quads,
                                             op0=ALU.mult, op1=ALU.add).then_inc(dd, 1)
                dve.wait_ge(dd, next(done))
                s, part = divmod(q + 1, 2)
                c, o = s % 2, 1 - s % 2
                if q == 0:
                    dve.wait_ge(nm, 1)
                    dve.tensor_copy(N1T[:, 0, :], psN[0:RD, 0, 0:RD]).then_inc(nd, 1)
                    dve.wait_ge(nd, next(ndone))
                    dve.tensor_tensor(ZT[:, 0, :], N1T[:, 0, :], ident[0:RD, 0:RD], ALU.add).then_inc(nd, 1)
                    dve.wait_ge(nd, next(ndone))
                elif s <= SQUARES and part == 0:
                    dve.wait_ge(nm, 2 * s)
                    dve.tensor_copy(N1[:, c, :], psN[0:RD, 0, 0:RD]).then_inc(nd, 1)
                    dve.wait_ge(nd, next(ndone))
                    dve.tensor_copy(N1T[:, c, :], psN[0:RD, 1, 0:RD]).then_inc(nd, 1)
                    dve.wait_ge(nd, next(ndone))
                elif s <= SQUARES:
                    dve.wait_ge(nm, 2 * s + 1)
                    dve.tensor_tensor(ZT[:, c, :], ZT[:, o, :], psN[0:RD, 2, 0:RD], ALU.add).then_inc(nd, 1)
                    dve.wait_ge(nd, next(ndone))
            m1 = 2 + TERMS + SCALINGS
            dve.tensor_scalar(rinv[:, :], ZT[:, 1, :], sc[0:RD, 11:12], None, ALU.mult).then_inc(dd, 1)
            dve.wait_ge(dd, next(done))
            dve.wait_ge(mm, m1)
            dve.tensor_copy(U[:, :, :], psN[0:96, 0, 0:3 * RD].rearrange("p (a n) -> p a n", a=3)).then_inc(dd, 1)
            dve.wait_ge(dd, next(done))
            dve.tensor_copy(UT[:, :], psN[0:RD, 1, 0:C]).then_inc(dd, 1)
            dve.wait_ge(dd, next(done))
            dve.wait_ge(mm, m1 + 1)
            dve.tensor_copy(W2[:, :, :], psN[0:RD, 1:3, 0:C]).then_inc(dd, 1)
            dve.wait_ge(dd, next(done))
            for c in range(TOK // CH):
                dve.wait_ge(mm, m1 + 2 + c)
                dve.tensor_copy(zT[:, c * CH:(c + 1) * CH], psZ[0:RD, c % 2, :]).then_inc(dd, 1)
                dve.wait_ge(dd, next(done))
            dve.wait_ge(xloaded, 32)
            for t in range(TILES):
                dve.wait_ge(mm, m1 + 6 + t)
                dve.tensor_tensor(x[:, t, :], x[:, t, :], last[t % 5][:, 0:C], ALU.add).then_inc(dd, 1)
                dve.wait_ge(dd, next(done))
            dve.wait_ge(mm, m1 + 6 + TILES)
            v = psE[:, 0:2 * FT * 12].rearrange("p (b f l j k) -> p k l f j b", b=NB, f=FT, l=3, k=2)
            for kk in range(2):
                for l in range(3):
                    for b in range(NB):
                        dve.tensor_scalar(fm[l][:, :, kk:4:2, b], v[:, kk, l, :, :, b], float(kk), None, ALU.add)

        @block.tensor
        def _(pe):
            pe.wait_ge(sel_ok, 1)
            pe.sem_inc(row, 1)
            pe.wait_ge(silu_ok, 1)
            with pe.Fori(0, RD // QR_UNROLL) as i:
                for u in range(QR_UNROLL):
                    s = i * QR_UNROLL + u
                    pe.wait_ge(sel_ok, s + 2)
                    pe.wait_ge(upd, s + 1)
                    pe.matmul(psQ[:, 0:W], sel[:, :], A[:, bass.ds(s, W)], start=True, stop=True).then_inc(row2, 1)
                    pe.matmul(psR[:, 0:W], sel[:, :], A[:, bass.ds(s, W)], start=True, stop=True).then_inc(row, 1)
                    p, v = u // NCOND, u % NCOND
                    j = i * 2 + p
                    for c, f in [divmod(v, 3)] + ([divmod(NCOND, 3)] if v == NCOND - 1 else []):
                        if v == 0:
                            pe.wait_ge(w_in[p], 48 * (i + 1))
                        if f == 0:
                            pe.wait_ge(c_got, 3 * j + c + 1)
                        r = pe.matmul(psZ[0:NB, (p + c) % 2, 0:CC], silu[:, f, :], wc[:, p, f, c * CC:(c + 1) * CC],
                                      start=(f == 0), stop=(f == 2))
                        if f == 2:
                            r.then_inc(c_mm, 1)
                    for _ in range(2):
                        pe.matmul(psE[:, 0:P], ident[:, :], ident[:, :], start=True, stop=True)
            pe.wait_ge(rot_in, 16 * NB)
            for b in range(NB):
                t = pe.transpose(psE[0:RD, b * RD:(b + 1) * RD], rot[:, b, :], ident[0:RD, 0:RD])
            t.then_inc(mm, 1)
            pe.wait_ge(nd, 4)
            pe.transpose(psN[0:RD, 0, 0:RD], N1[:, 0, :], ident[0:RD, 0:RD]).then_inc(nm, 1)
            after = 3 * NB + 1
            for q in range(TERMS + SCALINGS):
                pe.wait_ge(dd, after + q)
                for j in range(4):
                    left = skew[:, j ^ 1, :] if q < TERMS else ex[:, q % 2, j ^ 1, :]
                    m = pe.matmul(psE[0:RD, j * RD:(j + 1) * RD], left, ex[:, q % 2, j, :], start=True, stop=True)
                m.then_inc(mm, 1)
                s, part = divmod(q + 1, 2)
                c, o = s % 2, 1 - s % 2
                if 1 <= s <= SQUARES and part == 0:
                    pe.wait_ge(nd, 6 + 3 * (s - 1))
                    pe.matmul(psN[0:RD, 0, 0:RD], N1T[:, o, :], N1[:, o, :], start=True, stop=True)
                    pe.matmul(psN[0:RD, 1, 0:RD], N1[:, o, :], N1T[:, o, :], start=True, stop=True).then_inc(nm, 1)
                elif 1 <= s <= SQUARES:
                    pe.wait_ge(nd, 6 + 3 * (s - 1) + 2)
                    pe.matmul(psN[0:RD, 2, 0:RD], N1[:, c, :], ZT[:, o, :], start=True, stop=True).then_inc(nm, 1)
            after += TERMS + SCALINGS + 1
            pe.wait_ge(nd, 6 + 3 * SQUARES)
            pe.wait_ge(dd, after)
            for a in range(3):
                pe.matmul(psN[0:96, 0, a * RD:(a + 1) * RD], pT[:, a * 96:(a + 1) * 96], rinv[:, :], start=True, stop=True)
            pe.matmul(psN[0:RD, 1, 0:C], rinv[:, :], pT[:, :], start=True, stop=True).then_inc(mm, 1)
            after += 2
            pe.wait_ge(dd, after)
            for b in range(NB):
                m = pe.matmul(psN[0:RD, 1 + b, 0:C], ex[:, (TERMS + SCALINGS) % 2, 2 * b + 1, :], UT[:, :],
                              start=True, stop=True)
            m.then_inc(mm, 1)
            after += 1
            pe.wait_ge(xloaded, 32)
            for c in range(TOK // CH):
                if c >= 2:
                    pe.wait_ge(dd, after + c - 1)
                for a in range(3):
                    m = pe.matmul(psZ[0:RD, c % 2, :], U[:, a, :], xT[:, a, c * CH:(c + 1) * CH], start=(a == 0), stop=(a == 2))
                m.then_inc(mm, 1)
            after += TOK // CH
            pe.wait_ge(dd, after)
            for t in range(TILES):
                if t >= 5:
                    pe.wait_ge(dd, after + t - 4)
                pe.matmul(last[t % 5][:, 0:C], zT[:, t * P:(t + 1) * P], W2[:, t // TPB, :], start=True, stop=True).then_inc(mm, 1)
            pe.wait_ge(mod_in, 16 * NB * (2 + 4))
            pe.transpose(psE[:, 0:2 * FT * 12], modr[:, :], ident[0:2 * FT * 12, 0:2 * FT * 12]).then_inc(mm, 1)


class Prep:

    def __init__(self, nc, ph, sem, k, l, which, x, tag):
        sb = lambda n, s, dt=F32: ph.enter_context(nc.sbuf_tensor(tag + n, s, dt))
        self.k, self.x, self.which, self.l = k, x, which, l
        self.stats = sb("stats", [P, TPC, 6])
        self.mv = sb("mv", [P, 2, TPC, 2])
        self.std = sb("std", [P, 2, TPC])
        self.rstd = sb("rstd", [P, TPC])
        self.mod = sb("mod", [P, FT, 2])
        self.xn = sb("xn", [P, 2, TPC, CP])
        self.y = sb("y", [P, 2, FT, CH])
        self.psT = ph.enter_context(nc.psum_tensor(tag + "psT", [P, FT, CH], F32))
        self.s_mv, self.s_std, self.s_stats, self.s_self, self.s_mod, self.s_xn, self.s_T, self.s_y, self.s_h, self.s_l, self.s_xl = (
            sem("mv"), sem("std"), sem("stats"), sem("norm_self"), sem("mod"), sem("xn"), sem("T"), sem("y"), sem("h"), sem("l"), sem("xl"))

    def credits(self, dve):
        dve.sem_inc(self.s_y, 2)
        dve.sem_inc(self.s_l, 2)

    def rows(self, g, t):
        return self.x[:, bass.ds(g * TPC + t, 1), :].rearrange("p o c -> p (o c)")

    def statistics(self, dve, g, p):
        for t in range(TPC):
            r = dve.bn_stats(self.stats[:, t, :], self.rows(g, t))
        r.then_inc(self.s_stats, 1)
        dve.wait_ge(self.s_stats, g + 1)
        for t in range(TPC):
            r = dve.bn_aggr(self.mv[:, p, t, :], self.stats[:, t, :])
        r.then_inc(self.s_mv, 1)
        dve.wait_ge(self.s_mv, g + 1)

    def deviation(self, act, g, p):
        act.wait_ge(self.s_mv, g + 1)
        act.activation(self.std[:, p, :], self.mv[:, p, :, 1], ACT.Sqrt, bias=self.k["eps"][:, 0:1]).then_inc(self.s_std, 1)

    def normalise(self, dve, g, p):
        dve.wait_ge(self.s_T, g + 1)
        dve.wait_ge(self.s_std, g + 1)
        dve.reciprocal(self.rstd[:, :], self.std[:, p, :]).then_inc(self.s_self, 1)
        dve.wait_ge(self.s_self, g + 1)
        for t in range(TPC):
            xs = self.rows(g, t)
            dve.tensor_scalar(self.xn[:, p, t, 0:C], xs, self.mv[:, p, t, 0:1], self.rstd[:, t:t + 1],
                              ALU.subtract, ALU.mult)
            r = dve.tensor_scalar(self.xn[:, p, t, C:CP].rearrange("p (a m) -> p a m", a=3),
                                  xs[:, 2 * P:C].unsqueeze(1).broadcast_to([P, 3, TAIL]),
                                  self.mv[:, p, t, 0:1], self.rstd[:, t:t + 1], ALU.subtract, ALU.mult)
        r.then_inc(self.s_xn, 1)
        dve.wait_ge(self.s_xn, g + 1)

    def transpose(self, pe, g, p):
        pe.wait_ge(self.s_xn, g + 1)
        pe.wait_ge(self.s_y, g + 2)
        for f in range(FT):
            for t in range(TPC):
                r = pe.transpose(self.psT[:, f, t * P:(t + 1) * P], self.xn[:, p, t, f * P:(f + 1) * P], self.k["ident"][:, :])
        r.then_inc(self.s_T, 1)

    def modulate(self, dve, i, g, p):
        m = 2 * self.which
        dve.tensor_copy(self.mod[:, :, :],
                        self.k["fm"][self.l][:, :, m:m + 2, bass.ds(i, 1)].rearrange("p f m o -> p f (m o)")).then_inc(self.s_mod, 1)
        dve.wait_ge(self.s_mod, g + 1)
        dve.wait_ge(self.s_T, g + 3)
        dve.wait_ge(self.s_l, g + 1)
        for f in range(FT):
            r = dve.tensor_scalar(self.y[:, p, f, :], self.psT[:, f, :], self.mod[:, f, 1:2], self.mod[:, f, 0:1],
                                  ALU.mult, ALU.add)
        r.then_inc(self.s_y, 1)
        dve.wait_ge(self.s_y, g + 3)

    def high(self, act, g, p, XH, X8):
        act.wait_ge(self.s_y, g + 3)
        act.activation(XH, self.y[:, p, 0:2, :], ACT.Copy)
        act.activation(X8, self.y[:, p, 2, :], ACT.Copy).then_inc(self.s_h, 1)

    def low(self, pool, g, p, XH, XL, X8):
        pool.wait_ge(self.s_h, g + 1)
        pool.wait_ge(self.s_l, g + 2)
        pool.tensor_tensor(XL, self.y[:, p, 0:2, :], XH.bitcast(F32), ALU.subtract).then_inc(self.s_xl, 1)
        pool.wait_ge(self.s_xl, g + 1)
        pool.tensor_tensor(X8[64:P], self.y[64:P, p, 2, :], X8[64:P].bitcast(F32), ALU.subtract).then_inc(self.s_l, 1)


def batches(eng, body):
    with eng.Fori(0, NB - 1) as i:
        for c in range(CPB):
            body(i, c, i * CPB + c, True)
    for c in range(CPB):
        body(NB - 1, c, (NB - 1) * CPB + c, c < CPB - 1)


def project_qkv(nc, d, k, l, x, qk_scr, v_scr):
    norm = l == 1
    RING = 3 if norm else 4
    NQK = 2 * QUADS
    NM, NV = CPB * NQK, CPB * TPC
    MM0 = NM + NV
    with ExitStack() as ph:
        tag = f"q{l}_"
        sb = lambda n, s, dt=F32: ph.enter_context(nc.sbuf_tensor(tag + n, s, dt))
        sem = ph.enter_context(signals(nc, tag))
        prep = Prep(nc, ph, sem, k, l, 0, x, tag)
        QK = NQK * P
        NW = QK + QUADS * P
        raw = sb("raw", [P, FT, NW])
        WH = sb("WH", [P, 2, NW], F32R)
        WL = sb("WL", [P, 2, NW], F32R)
        W8 = sb("W8", [P, NW], F32R)
        XH = sb("XH", [P, CPB, 2, CH], F32R)
        XL = sb("XL", [P, CPB, 2, CH], F32R)
        X8 = sb("X8", [P, CPB, CH], F32R)
        bqk = sb("bqk", [P, NQK])
        bv = sb("bv", [P, CH])
        hst = sb("hst", [P, 4, CH], F32R)
        lst = sb("lst", [P, 4, CH], F32R)
        vst = sb("vst", [P, 2, CH])
        ps = ph.enter_context(nc.psum_tensor(tag + "ps", [P, RING, CH], F32))
        if norm:
            psV = ph.enter_context(nc.psum_tensor(tag + "psV", [P, CH], F32))
            psI = ph.enter_context(nc.psum_tensor(tag + "psI", [P, CH], F32))
            gb = sb("gb", [P, 4])
            wmean = sb("wmean", [P, FT, 2 * NH])
            bcen = sb("bcen", [P, NQK])
            sq = sb("sq", [P, 2, CH])
            sdev = sb("sdev", [P, 2, TPC, 4])
            rdev = sb("rdev", [P, 2, TPC, 4])
            rg = sb("rg", [P, 2, CH])
            qn = sb("qn", [P, 2, CH])
            wcen, bc_mm, bc_ok, n_sq, n_var, n_dev, n_rdev, n_spread, n_rg, n_qn = (
                sem("wcen"), sem("bc_mm"), sem("bc_ok"), sem("n_sq"), sem("n_var"), sem("n_dev"), sem("n_rdev"),
                sem("n_spread"), sem("n_rg"), sem("n_qn"))
        small, wv_in, wqk_in, w_h, w_l, w_q, mm, out_h, out_l, freed = (
            sem("small"), sem("wv_in"), sem("wqk_in"), sem("w_h"), sem("w_l"), sem("w_q"), sem("mm"), sem("out_h"), sem("out_l"),
            sem("freed"))
        sent = [sem(f"sent{n}") for n in range(4)]
        vsent = [sem(f"vsent{n}") for n in range(2)]
        block = ph.enter_context(nc.Block())

        use = lambda i, c, w: i * (NM + NV) + c * (NQK + TPC) + w
        tile = lambda i, c, n: i * NM + c * NQK + n
        NEXT_T, NEXT_MOD, NEXT_HIGH = 1, 3, 4
        heads = lambda t: t.rearrange("p (t h) -> p t h", h=4)

        def slot_free(eng, i, c, n):
            g = c * NQK + n
            eng.wait_ge(sent[g % 4], (i * (NM // 4) + g // 4 + 1) * 32)

        @block.sync
        def _(sp):
            sp.dma_start(bqk[:, :], d[f"bqk{l}"]).then_inc(small, 16)
            sp.dma_start(bv[:, :], d[f"bv{l}"].partition_broadcast(P)).then_inc(small, 16)
            if norm:
                sp.dma_start(gb[:, :], d["qkn"]).then_inc(small, 16)
            sp.dma_start(raw[:, :, QK:NW], d[f"wqkv{l}"][:, :, QK:NW]).then_inc(wv_in, 16)
            sp.dma_start(raw[:, :, 0:QK], d[f"wqkv{l}"][:, :, 0:QK]).then_inc(wqk_in, 16)
            for s in sent:
                sp.sem_inc(s, 32)
            for s in vsent:
                sp.sem_inc(s, 16)
            with sp.Fori(0, NB) as i:
                for c in range(CPB):
                    for t in range(TPC):
                        sp.wait_ge(freed, use(i, c, t) + RING + 1)
                        sp.dma_start(v_scr[bass.ds(i * QUADS, QUADS), c * TPC + t, :, :].rearrange("q p c -> p q c"),
                                     vst[:, t % 2, :].rearrange("p (q c) -> p q c", q=QUADS)).then_inc(vsent[t % 2], 16)
                    for n in range(NQK):
                        sp.wait_ge(out_l, tile(i, c, n) + 3)
                        for part, st in ((0, hst), (1, lst)):
                            dst = qk_scr[part, n // QUADS, bass.ds(i * QUADS + n % QUADS, 1), :, c * CH:(c + 1) * CH]
                            sp.dma_start(dst.rearrange("o p c -> p (o c)"),
                                         st[:, n % 4, :].bitcast(F32)).then_inc(sent[n % 4], 16)
            for s in sent:
                sp.wait_ge(s, 32 * (NB * NM // 4 + 1))
            for s in vsent:
                sp.wait_ge(s, 16 * (NB * NV // 2 + 1))

        @block.gpsimd
        def _(pool):
            pool.wait_ge(w_h, 1)
            pool.tensor_tensor(WL[:, :, QK:NW], raw[:, 0:2, QK:NW], WH[:, :, QK:NW].bitcast(F32), ALU.subtract).then_inc(w_l, 1)
            for n, b in enumerate((1, 3)):
                pool.wait_ge(w_l, n + 1)
                rows = slice(HP * b, HP * (b + 1))
                pool.tensor_tensor(W8[rows, QK:NW], raw[rows, 2, QK:NW], W8[rows, QK:NW].bitcast(F32), ALU.subtract).then_inc(w_l, 1)
            pool.wait_ge(w_l, 3)

            def low(g, p):
                prep.low(pool, g, p, XH[:, p, :, :], XL[:, p, :, :], X8[:, p, :])

            low(0, 0)
            batches(pool, lambda i, c, g, more: low(g + 1, 1 - c) if more else None)

        @block.scalar
        def _(act):
            act.wait_ge(small, 48 if norm else 32)

            def high(g, p, first=False):
                if not first:
                    act.wait_ge(mm, (g + 1) * (NQK + TPC))
                prep.high(act, g, p, XH[:, p, :, :], X8[:, p, :])

            prep.deviation(act, 0, 0)
            act.wait_ge(wv_in, 16)
            act.activation(WH[:, :, QK:NW], raw[:, 0:2, QK:NW], ACT.Copy)
            act.activation(W8[:, QK:NW], raw[:, 2, QK:NW], ACT.Copy).then_inc(w_h, 1)
            high(0, 0, first=True)
            act.wait_ge(wqk_in, 16)
            if norm:
                act.wait_ge(wcen, 3)
            act.activation(WH[:, :, 0:QK], raw[:, 0:2, 0:QK], ACT.Copy)
            act.activation(W8[:, 0:QK], raw[:, 2, 0:QK], ACT.Copy).then_inc(w_h, 1)
            if norm:
                act.wait_ge(bc_mm, 1)
                act.activation(bcen[:, :], psV[:, 0:NQK], ACT.Copy).then_inc(bc_ok, 1)
                act.wait_ge(bc_ok, 1)
                act.sem_inc(n_dev, 2)
                act.sem_inc(n_rg, 2)
                act.sem_inc(n_sq, 2)

            def body(i, c, g_chunk, more):
                if more:
                    prep.deviation(act, g_chunk + 1, 1 - c)
                for n in range(NQK if not norm else NQK + 3):
                    if more and n == NEXT_HIGH:
                        high(g_chunk + 1, 1 - c)
                    if not norm:
                        act.wait_ge(mm, use(i, c, TPC + n) + 1 + MM0)
                        slot_free(act, i, c, n)
                        act.activation(hst[:, n % 4, :], ps[:, (TPC + n) % RING, :], ACT.Identity,
                                       bias=bqk[:, n:n + 1]).then_inc(out_h, 1)
                        continue
                    if n >= 3:
                        g, m = tile(i, c, n - 3), n - 3
                        w = 2 * (m // QUADS)
                        act.wait_ge(n_qn, g + 3)
                        slot_free(act, i, c, m)
                        act.activation(hst[:, m % 4, :], qn[:, m % 2, :], ACT.Identity,
                                       bias=gb[:, w + 1:w + 2]).then_inc(out_h, 1)
                    if 2 <= n <= NQK + 1:
                        g, w = tile(i, c, n - 2), 2 * ((n - 2) // QUADS)
                        act.wait_ge(n_qn, g + 1)
                        act.wait_ge(n_spread, g + 3)
                        act.activation(rg[:, n % 2, :], psI[:, :], ACT.Identity, scale=gb[:, w:w + 1]).then_inc(n_rg, 1)
                    if 1 <= n <= NQK:
                        g = tile(i, c, n - 1)
                        act.wait_ge(n_rdev, g + 1)
                        act.wait_ge(n_var, g + 3)
                        act.activation(sdev[:, (n - 1) % 2, :, :], heads(psV[:, 0:4 * TPC]), ACT.Sqrt,
                                       bias=k["eps"][:, 1:2]).then_inc(n_dev, 1)
                    if n < NQK:
                        g = tile(i, c, n)
                        act.wait_ge(mm, use(i, c, TPC + n) + 1 + MM0)
                        act.wait_ge(n_var, g + 1)
                        act.activation(sq[:, n % 2, :], ps[:, (TPC + n) % RING, :], ACT.Square,
                                       bias=bcen[:, n:n + 1]).then_inc(n_sq, 1)

            batches(act, body)

        @block.vector
        def _(dve):
            prep.credits(dve)
            dve.sem_inc(freed, RING)
            dve.sem_inc(out_l, 2)
            if norm:
                dve.sem_inc(n_rdev, 2)
                dve.sem_inc(n_qn, 2)
            dve.wait_ge(small, 48 if norm else 32)
            prep.statistics(dve, 0, 0)
            prep.normalise(dve, 0, 0)
            prep.modulate(dve, 0, 0, 0)
            dve.wait_ge(wqk_in, 16)
            if norm:
                w = raw[:, :, 0:QK].rearrange("p f (h e) -> p f h e", e=HP)[:, :, :, 0:HD]
                dve.tensor_reduce(wmean[:, :, :], w, AX, ALU.add).then_inc(wcen, 1)
                dve.wait_ge(wcen, 1)
                dve.tensor_scalar(wmean[:, :, :], wmean[:, :, :], 1.0 / HD, None, ALU.mult).then_inc(wcen, 1)
                dve.wait_ge(wcen, 2)
                dve.tensor_tensor(w, w, wmean[:, :, :].unsqueeze(3).broadcast_to([P, FT, 2 * NH, HD]), ALU.subtract).then_inc(wcen, 1)
                dve.wait_ge(wcen, 3)
            dve.wait_ge(w_h, 2)
            dve.tensor_tensor(WL[:, :, 0:QK], raw[:, 0:2, 0:QK], WH[:, :, 0:QK].bitcast(F32), ALU.subtract).then_inc(w_q, 1)
            for b in (1, 3):
                rows = slice(HP * b, HP * (b + 1))
                dve.tensor_tensor(W8[rows, 0:QK], raw[rows, 2, 0:QK], W8[rows, 0:QK].bitcast(F32), ALU.subtract).then_inc(w_q, 1)

            def body(i, c, g_chunk, more):
                if more:
                    prep.statistics(dve, g_chunk + 1, 1 - c)
                for t in range(TPC):
                    if more and t == 2:
                        prep.normalise(dve, g_chunk + 1, 1 - c)
                    dve.wait_ge(mm, use(i, c, t) + 1 + MM0)
                    dve.wait_ge(vsent[t % 2], (i * (NV // 2) + (c * TPC + t) // 2 + 1) * 16)
                    dve.tensor_tensor(vst[:, t % 2, :], ps[:, t % RING, :], bv[:, :], ALU.add).then_inc(freed, 1)
                for n in range(NQK if not norm else NQK + 3):
                    if more and n == NEXT_MOD:
                        j, e = (i, 1) if c == 0 else (i + 1, 0)
                        prep.modulate(dve, j, g_chunk + 1, e)
                    if not norm:
                        dve.wait_ge(out_h, tile(i, c, n) + 1)
                        slot_free(dve, i, c, n)
                        dve.scalar_tensor_tensor(out=lst[:, n % 4, :], in0=ps[:, (TPC + n) % RING, :],
                                                 scalar=bqk[:, n:n + 1], in1=hst[:, n % 4, :].bitcast(F32),
                                                 op0=ALU.add, op1=ALU.subtract).then_inc(out_l, 1)
                        dve.wait_ge(out_l, tile(i, c, n) + 3)
                        dve.sem_inc(freed, 1)
                        continue
                    if 2 <= n <= NQK + 1:
                        g, m = tile(i, c, n - 2), n - 2
                        dve.wait_ge(out_l, g + 1)
                        dve.wait_ge(n_rg, g + 3)
                        dve.wait_ge(n_sq, g + 3)
                        dve.scalar_tensor_tensor(out=qn[:, m % 2, :], in0=ps[:, (TPC + m) % RING, :],
                                                 scalar=bcen[:, m:m + 1], in1=rg[:, m % 2, :],
                                                 op0=ALU.add, op1=ALU.mult).then_inc(n_qn, 1)
                        dve.wait_ge(n_qn, g + 3)
                        dve.sem_inc(freed, 1)
                    if 1 <= n <= NQK:
                        g = tile(i, c, n - 1)
                        dve.wait_ge(n_spread, g + 1)
                        dve.wait_ge(n_dev, g + 3)
                        dve.reciprocal(rdev[:, (n - 1) % 2, :, :], sdev[:, (n - 1) % 2, :, :]).then_inc(n_rdev, 1)
                    if n >= 3:
                        g, m = tile(i, c, n - 3), n - 3
                        w = 2 * (m // QUADS)
                        dve.wait_ge(out_h, g + 1)
                        slot_free(dve, i, c, m)
                        dve.scalar_tensor_tensor(out=lst[:, m % 4, :], in0=qn[:, m % 2, :], scalar=gb[:, w + 1:w + 2],
                                                 in1=hst[:, m % 4, :].bitcast(F32),
                                                 op0=ALU.add, op1=ALU.subtract).then_inc(out_l, 1)

            batches(dve, body)

        @block.tensor
        def _(pe):
            pe.sem_inc(mm, MM0)
            if norm:
                pe.sem_inc(n_var, 2)
                pe.sem_inc(n_spread, 2)
                pe.wait_ge(small, 48)
                pe.matmul(psV[:, 0:NQK], k["center"][:, :], bqk[:, :], start=True, stop=True).then_inc(bc_mm, 1)
            pe.sem_inc(prep.s_T, 2)
            prep.transpose(pe, 0, 0)
            if norm:
                pe.wait_ge(bc_ok, 1)
            pe.wait_ge(w_h, 1)
            pe.wait_ge(w_l, 3)

            def body(i, c, g_chunk, more):
                pe.wait_ge(prep.s_l, g_chunk + 3)
                pe.wait_ge(prep.s_h, g_chunk + 1)
                for t in range(TPC):
                    pe.wait_ge(freed, use(i, c, t) + 1)
                    cols = slice(t * P, (t + 1) * P)
                    vw = slice(NQK * P, NW)
                    terms = [(x_[:, c, f, cols], w_[:, f, vw]) for x_, w_ in ((XH, WH), (XL, WH), (XH, WL)) for f in range(2)]
                    terms.append((X8[:, c, cols], W8[:, vw]))
                    for a, (lhs, rhs) in enumerate(terms):
                        r = pe.matmul(ps[:, t % RING, :], lhs, rhs, start=(a == 0), stop=(a == 6))
                    r.then_inc(mm, 1)
                pe.wait_ge(w_q, 3)
                for n in range(NQK if not norm else NQK + 2):
                    if more and n == NEXT_T:
                        prep.transpose(pe, g_chunk + 1, 1 - c)
                    if norm and n >= 2:
                        g, m = tile(i, c, n - 2), n - 2
                        pe.wait_ge(n_rdev, g + 3)
                        pe.wait_ge(n_rg, g + 2)
                        for t in range(TPC):
                            for h in range(4):
                                r = pe.matmul(psI[HP * h:HP * (h + 1), t * P:(t + 1) * P],
                                              rdev[:, m % 2, t, h:h + 1].broadcast_to([P, HP]), k["ident"][:, :],
                                              start=True, stop=True)
                        r.then_inc(n_spread, 1)
                    if norm and 1 <= n <= NQK:
                        g, m = tile(i, c, n - 1), n - 1
                        pe.wait_ge(n_sq, g + 3)
                        pe.wait_ge(n_dev, g + 2)
                        for t in range(TPC):
                            r = pe.matmul(psV[:, 4 * t:4 * t + 4], sq[:, m % 2, t * P:(t + 1) * P],
                                          k["blocks"][:, 0:P:HP], start=True, stop=True)
                        r.then_inc(n_var, 1)
                    if n < NQK:
                        pe.wait_ge(freed, use(i, c, TPC + n) + 1)
                        cols = slice(n * P, (n + 1) * P)
                        terms = [(w_[:, f, cols], x_[:, c, f, :]) for x_, w_ in ((XH, WH), (XL, WH), (XH, WL)) for f in range(2)]
                        terms.append((W8[:, cols], X8[:, c, :]))
                        for a, (lhs, rhs) in enumerate(terms):
                            r = pe.matmul(ps[:, (TPC + n) % RING, :], lhs, rhs, start=(a == 0), stop=(a == 6))
                        r.then_inc(mm, 1)

            batches(pe, body)


RING = 3
EARLY = 18


def ring_plan(find, ahead):
    seq = []
    if find:
        seq += [("max", e) for e in range(EARLY, NMX)]
        seq.insert(NMX // 2 + 4 - EARLY, ("turn", 0))
        early = [("max2", e) for e in range(EARLY if ahead else 0)]
        early.insert(4, ("turn", 1))
        seq += early
    span = NS if ahead else NS - 4
    steps = [seq[len(seq) * s // span:len(seq) * (s + 1) // span] for s in range(NS)]
    for half, s in ((1, 1), (0, TPB + 1)):
        steps[s].append(("sums", half))
        steps[s + 1].append(("spread", half))
    return steps


NS = 2 * TPB
NMX = 4 * TPB * 2
WIDTH = lambda kind: 2 if kind == "turn" else 1
UNIT_USES = NMX + 2 * 2 + 4
FIRST_USES = NMX + 2 * 2 + EARLY
assert UNIT_USES % RING == 0 and EARLY % RING == 0


def attend(nc, d, k, l, qk_scr, v_scr, oT, weights):
    with ExitStack() as ph:
        tag = f"a{l}_"
        sb = lambda n, s, dt=F32: ph.enter_context(nc.sbuf_tensor(tag + n, s, dt))
        sem = ph.enter_context(signals(nc, tag))
        qd = [sb(f"qd{p}", [P, 4, SEQ], F32R) for p in range(2)]
        kd = [sb(f"kd{p}", [P, SEQ], F32R) for p in range(2)]
        qr = [sb(f"qr{p}", [P, 4, SEQ], F32R) for p in range(2)]
        kr = [sb(f"kr{p}", [P, 4, SEQ], F32R) for p in range(2)]
        vq = [sb(f"vq{p}", [P, TPB, P]) for p in range(2)]
        probs = [sb(f"probs{p}", [P, 4, CH]) for p in range(2)]
        mx = sb("mx", [P, 4 * TPB, 2])
        mm_ = sb("mm", [P, 4 * TPB])
        mh = [sb(f"mh{p}", [2 * TPB, P], F32R) for p in range(2)]
        ml = [sb(f"ml{p}", [2 * TPB, P], F32R) for p in range(2)]
        u = sb("u", [P, CH])
        inv = sb("inv", [P, TPC, 4])
        psS = ph.enter_context(nc.psum_tensor(tag + "psS", [P, 4, CH], F32))
        psO = ph.enter_context(nc.psum_tensor(tag + "psO", [P, CH], F32))
        psM = ph.enter_context(nc.psum_tensor(tag + "psM", [P, RING, CH], F32))
        zero_d, zeroed, ring_ready, ring_free, comb, mh_ok, sc, ex, pv, u_ok, inv_ok, o_ok = (
            sem("zero_d"), sem("zeroed"), sem("ring_ready"), sem("ring_free"), sem("comb"), sem("mh_ok"), sem("sc"),
            sem("ex"), sem("pv"), sem("u_ok"), sem("inv_ok"), sem("o_ok"))
        d_in = [sem(f"d_in{p}") for p in range(2)]
        r_in = [sem(f"r_in{p}") for p in range(2)]
        v_in = [sem(f"v_in{p}") for p in range(2)]
        m_in = [sem(f"m_in{p}") for p in range(2)]
        block = ph.enter_context(nc.Block())
        f = lambda ap: ap.bitcast(F32)

        def unit(scr, n):
            return scr[bass.ds(n, 1)].rearrange("o p c -> p (o c)")

        def load_d(eng, n, p):
            q, kk = qk_scr[0, 0], qk_scr[0, 1]
            eng.dma_start(f(kd[p][:, :]), unit(kk, n)).then_inc(d_in[p], 16)
            for h in range(4):
                r = slice(HP * h, HP * h + HD)
                eng.dma_start(f(qd[p][r, h, :]), unit(q[:, r, :], n)).then_inc(d_in[p], 16)

        def load_r(eng, n, p):
            for b in range(4):
                q = qk_scr[b // 2, 0, bass.ds(n, 1)].rearrange("o (h e) c -> e (o h) c", h=4)
                kk = qk_scr[b % 2, 1, bass.ds(n, 1)].rearrange("o (h e) c -> e (o h) c", h=4)
                eng.dma_start(f(qr[p][HP * b:HP * b + HD, :, :]), q[0:HD]).then_inc(r_in[p], 16)
                eng.dma_start(f(kr[p][HP * b:HP * b + HD + 1, :, :]), kk[0:HD + 1]).then_inc(r_in[p], 16)

        def load_v(eng, n, p):
            eng.dma_start(vq[p][:, :, :], v_scr[bass.ds(n, 1)].rearrange("o t p c -> p (o t) c")).then_inc(v_in[p], 16)

        def load_m(eng, p, half):
            for b in range(4):
                src = (mh if b < 2 else ml)[half]
                row = HP * b + HD
                eng.dma_start(f(qr[p][row:row + 1, 2 * half:2 * half + 2, :]).rearrange("o h (t c) -> o (h t) c", c=P),
                              f(src[:, :])).then_inc(m_in[p], 16)

        def iterations(eng, body):
            with eng.Fori(0, NQ // 2 - 1) as i:
                for p in range(2):
                    body(i * 2 + p, i, p, FIRST_USES + (i * 2 + p) * UNIT_USES, True, True)
            start = FIRST_USES + (NQ - 2) * UNIT_USES
            body(NQ - 2, NQ // 2 - 1, 0, start, True, False)
            body(NQ - 1, NQ // 2 - 1, 1, start + UNIT_USES - EARLY, False, False)

        def uses(find, ahead):
            at, steps = 0, []
            for step in ring_plan(find, ahead):
                steps.append([])
                for kind, e in step:
                    steps[-1].append((kind, e, at, (FIRST_USES + at) % RING))
                    at += WIDTH(kind)
            return steps

        first = [("max", e) for e in range(NMX)]
        first.insert(NMX // 2 + 4, ("turn", 0))
        first += [("max2", e) for e in range(EARLY)]
        first.insert(NMX + 1 + 4, ("turn", 1))
        opening, at = [], 0
        for kind, e in first:
            opening.append((kind, e, at, at % RING))
            at += WIDTH(kind)
        assert at == FIRST_USES
        opening_turn = [a for kind, e, a, b in opening if kind == "turn"]
        END = FIRST_USES + (NQ - 1) * UNIT_USES - EARLY + 4

        @block.sync
        def _(sp):
            sp.wait_ge(zero_d, 2)
            load_d(sp, 0, 0)
            sp.wait_ge(zeroed, 1)
            load_d(sp, 1, 1)
            sp.wait_ge(zeroed, 3)
            load_r(sp, 0, 0)
            load_v(sp, 0, 0)
            sp.wait_ge(zeroed, 5)
            load_r(sp, 1, 1)
            load_v(sp, 1, 1)
            for half in range(2):
                sp.wait_ge(ring_free, RING + opening_turn[half] + 2)
                load_m(sp, 0, half)
            if weights:
                weights.load(sp, d)

            def body(n, i, p, start, find, ahead):
                if ahead:
                    sp.wait_ge(ring_ready, start)
                    load_d(sp, n + 2, p)
                turns = {e: a for step in uses(find, ahead) for kind, e, a, b in step if kind == "turn"}
                for half in turns:
                    sp.wait_ge(ring_free, RING + start + turns[half] + 2)
                    load_m(sp, 1 - p, half)
                if ahead:
                    sp.wait_ge(sc, 2 * NS * (n + 1))
                    load_r(sp, n + 2, p)
                    sp.wait_ge(pv, 2 + NS * (n + 1))
                    load_v(sp, n + 2, p)

            iterations(sp, body)

        @block.gpsimd
        def _(pool):
            pool.memset(u[:, :], 1.0).then_inc(u_ok, 1)
            pool.memset(f(qd[0][:, 2:4, :]), 0.0).then_inc(zero_d, 1)
            pool.memset(f(qd[1][:, :, :]), 0.0).then_inc(zeroed, 1)
            for p in range(2):
                pool.memset(f(qr[p][:, :, :]), 0.0).then_inc(zeroed, 1)
                pool.memset(f(kr[p][:, :, :]), 0.0).then_inc(zeroed, 1)

        @block.scalar
        def _(act):
            act.sem_inc(ex, 2)

            def exps(n, s):
                for pr in range(2):
                    act.wait_ge(sc, 2 * NS * n + 2 * s + pr + 1)
                    act.wait_ge(pv, NS * n + s + 1)
                    act.activation(probs[s % 2][:, 2 * pr:2 * pr + 2, :], psS[:, 2 * pr:2 * pr + 2, :],
                                   ACT.Exp, scale=SCALE).then_inc(ex, 1)

            def take(n, half):
                act.wait_ge(pv, 2 + NS * n + TPB * (half + 1))
                act.wait_ge(o_ok, 2 * n + half + 1)
                act.activation(u[:, :], psO[:, :], ACT.Copy).then_inc(u_ok, 1)

            exps(0, 0)

            def body(n, i, p, start, find, ahead):
                for s in range(1, NS):
                    exps(n, s)
                    if s == TPB:
                        take(n, 0)
                if find:
                    exps(n + 1, 0)
                take(n, 1)

            iterations(act, body)

        @block.vector
        def _(dve):
            dve.memset(f(qd[0][:, 0:2, :]), 0.0).then_inc(zero_d, 1)
            dve.sem_inc(ring_free, RING)

            def serve(kind, e, use, bank, m, n, sent=None):
                dve.wait_ge(ring_ready, use + WIDTH(kind))
                if kind == "max":
                    dve.tensor_reduce(mx[:, e // 2, e % 2:e % 2 + 1], psM[:, bank, :], AX, ALU.max).then_inc(ring_free, 1)
                    if (e + 1) % (NMX // 2) == 0:
                        half = e // (NMX // 2)
                        cols = slice(half * 2 * TPB, (half + 1) * 2 * TPB)
                        dve.wait_ge(ring_free, RING + use + 1)
                        dve.tensor_tensor(mm_[:, cols], mx[:, cols, 0], mx[:, cols, 1], ALU.max).then_inc(comb, 1)
                elif kind == "turn":
                    src = psM[0:2 * TPB, bank, 0:P]
                    if sent and e == 0:
                        sent()
                    dve.tensor_scalar(mh[e][:, :], src, -1.0, None, ALU.mult).then_inc(mh_ok, 1)
                    dve.wait_ge(mh_ok, 2 * m + e + 1)
                    dve.scalar_tensor_tensor(out=ml[e][:, :], in0=src, scalar=-1.0, in1=f(mh[e][:, :]),
                                             op0=ALU.mult, op1=ALU.subtract).then_inc(ring_free, 2)
                elif kind == "sums":
                    dve.reciprocal(inv[:, :, :], psM[:, bank, 0:TPC * 4].rearrange("p (t h) -> p t h", h=4)).then_inc(inv_ok, 1)
                    dve.wait_ge(inv_ok, 2 * n + 2 - e)
                    dve.sem_inc(ring_free, 1)
                else:
                    dve.wait_ge(u_ok, 2 * n + 2 - e)
                    dve.tensor_tensor(oT[:, bass.ds(n + 1 - e, 1), e * CH:(e + 1) * CH].rearrange("p o c -> p (o c)"),
                                      u[:, :], psM[:, bank, :], ALU.mult).then_inc(o_ok, 1)
                    dve.wait_ge(o_ok, 2 * n + 2 - e)
                    dve.sem_inc(ring_free, 1)

            for kind, e, use, bank in opening:
                if kind == "max2" and e == 0:
                    dve.wait_ge(comb, 2)
                serve("max" if kind == "max2" else kind, e, use, bank, 0, 0)

            def body(n, i, p, start, find, ahead):
                sent = lambda: dve.wait_ge(m_in[p], 128 * (i + 1))
                for step in uses(find, ahead):
                    for kind, e, at, bank in step:
                        if kind == "max2" and e == 0:
                            dve.wait_ge(comb, 2 * (n + 2))
                        serve("max" if kind == "max2" else kind, e, start + at, bank, n + 1, n, sent)

            iterations(dve, body)
            serve("sums", 1, END, END % RING, None, NQ)
            serve("spread", 1, END + 1, (END + 1) % RING, None, NQ)

        @block.tensor
        def _(pe):
            pe.sem_inc(pv, 2)

            def fill(kind, e, use, bank, m, pm, n):
                pe.wait_ge(ring_free, use + 1)
                if kind == "max":
                    h, t, kh = e // (2 * TPB), e // 2 % TPB, e % 2
                    pe.matmul(psM[:, bank, :], qd[pm][:, h, t * P:(t + 1) * P], kd[pm][:, kh * CH:(kh + 1) * CH],
                              start=True, stop=True).then_inc(ring_ready, 1)
                elif kind == "turn":
                    pe.wait_ge(comb, 2 * m + e + 1)
                    pe.transpose(psM[0:2 * TPB, bank, 0:P], mm_[:, e * 2 * TPB:(e + 1) * 2 * TPB],
                                 k["ident"][:, :]).then_inc(ring_ready, 2)
                elif kind == "sums":
                    pe.wait_ge(u_ok, 2 * n + 2 - e)
                    for t in range(TPC):
                        r = pe.matmul(psM[:, bank, 4 * t:4 * t + 4], u[:, t * P:(t + 1) * P], k["sumrow"][:, :],
                                      start=True, stop=True)
                    r.then_inc(ring_ready, 1)
                else:
                    pe.wait_ge(inv_ok, 2 * n + 2 - e)
                    for t in range(TPC):
                        for h in range(4):
                            r = pe.matmul(psM[HP * h:HP * (h + 1), bank, t * P:(t + 1) * P],
                                          inv[:, t, h:h + 1].broadcast_to([P, HP]), k["ident"][:, :], start=True, stop=True)
                    r.then_inc(ring_ready, 1)

            def scores(n, p, s, pr):
                half, kt = s // TPB, s % TPB
                pe.wait_ge(ex, 2 * NS * n + 2 * s + pr + 1)
                for h in (2 * pr, 2 * pr + 1):
                    r = pe.matmul(psS[:, h, :], kr[p][:, h, kt * P:(kt + 1) * P],
                                  qr[p][:, h, half * CH:(half + 1) * CH], start=True, stop=True)
                r.then_inc(sc, 1)

            def pv_step(n, i, p, s):
                half, kt = s // TPB, s % TPB
                if s == 0:
                    pe.wait_ge(v_in[p], 16 * (i + 1))
                if kt == 0:
                    pe.wait_ge(u_ok, 2 * n + half + 1)
                pe.wait_ge(ex, 2 + 2 * NS * n + 2 * s + 2)
                for h in range(4):
                    r = pe.matmul(psO[HP * h:HP * (h + 1), :], vq[p][:, kt, HP * h:HP * (h + 1)], probs[s % 2][:, h, :],
                                  start=(kt == 0), stop=(kt == TPB - 1))
                r.then_inc(pv, 1)

            def loaded(n, i, p):
                pe.wait_ge(r_in[p], 128 * (i + 1))
                pe.wait_ge(m_in[p], 128 * (i + 1))

            pe.wait_ge(d_in[0], 80)
            for kind, e, use, bank in opening:
                if kind == "max2" and e == 0:
                    pe.wait_ge(d_in[1], 80)
                fill("max" if kind == "max2" else kind, e, use, bank, 0, int(kind == "max2"), 0)
            loaded(0, 0, 0)
            for pr in range(2):
                scores(0, 0, 0, pr)

            def body(n, i, p, start, find, ahead):
                plan = uses(find, ahead)
                for s in range(NS):
                    if s == NS - 1 and find:
                        loaded(n + 1, i + p, 1 - p)
                    for part, (begin, end) in enumerate(((0, 2), (2, 3), (3, None))):
                        if part < 2 and s < NS - 1:
                            scores(n, p, s + 1, part)
                        elif part < 2 and find:
                            scores(n + 1, 1 - p, 0, part)
                        elif part == 2:
                            pv_step(n, i, p, s)
                        for kind, e, at, bank in plan[s][begin:end]:
                            if kind == "max2" and e == 0:
                                pe.wait_ge(d_in[p], 80 * (i + 2))
                            fill("max" if kind == "max2" else kind, e, start + at, bank, n + 1,
                                 p if kind == "max2" else 1 - p, n)

            iterations(pe, body)
            fill("sums", 1, END, END % RING, None, None, NQ)
            fill("spread", 1, END + 1, (END + 1) % RING, None, None, NQ)


class FeedTensors:

    def __init__(self, nc, ctx, l):
        tag = f"f{l}_"
        sb = lambda n, s, dt=F32: ctx.enter_context(nc.sbuf_tensor(tag + n, s, dt))
        sem = ctx.enter_context(signals(nc, tag))
        self.moe = l == 0
        self.n_exp = n = NE if self.moe else 1
        self.XH = sb("XH", [P, 2, TOK], F32R)
        self.XL = sb("XL", [P, 2, TOK], F32R)
        self.X8 = sb("X8", [P, TOK], F32R)
        self.b1 = sb("b1", [P, n, KT])
        self.b2 = sb("b2", [P, n, C])
        self.gate = sb("gate", [P, NB, C])
        self.cw = sb("cw", [P, TILES, NE]) if self.moe else None
        self.b_in, self.raw_in, self.split, self.h_ok, self.h2_ok = (
            sem("b_in"), sem("raw_in"), sem("split"), sem("h_ok"), sem("h2_ok"))
        self.slots = [self.slot(sb, 0)]

    @staticmethod
    def slot(sb, p):
        return (sb(f"W1H{p}", [P, 2, FF], F32R), sb(f"W1L{p}", [P, 2, FF], F32R), sb(f"W18{p}", [P, FF], F32R),
                sb(f"W2H{p}", [P, KT, C], F32R), sb(f"W2L{p}", [P, KT, C], F32R), sb(f"b1e{p}", [P, KT]))


class FirstWeights:

    def __init__(self, nc, ctx, l):
        self.raw = ctx.enter_context(nc.sbuf_tensor(f"first{l}", [P, FT, FF], F32))
        self.loaded = ctx.enter_context(signals(nc, f"first{l}_"))("loaded")
        self.l = l

    def load(self, sp, d):
        sp.dma_start(self.raw[:, :, :], d[f"w1_{self.l}"][0]).then_inc(self.loaded, 16)


def low_parts(pool, ff, raw1, raw2, e, slot):
    W1H, W1L, W18, W2H, W2L, b1e = slot
    pool.tensor_tensor(W1L[:, :, :], raw1[:, 0:2, :], W1H[:, :, :].bitcast(F32), ALU.subtract).then_inc(ff.h_ok, 1)
    for n, b in enumerate((1, 3)):
        pool.wait_ge(ff.h_ok, 4 * e + 2 + n)
        rows = slice(32 * b, 32 * b + 32)
        pool.tensor_tensor(W18[rows, :], raw1[rows, 2, :], W18[rows, :].bitcast(F32), ALU.subtract).then_inc(ff.h_ok, 1)
    pool.wait_ge(ff.h_ok, 4 * e + 4)
    pool.wait_ge(ff.h2_ok, e + 1)
    pool.tensor_tensor(W2L[:, :, :], raw2[:, :, :], W2H[:, :, :].bitcast(F32), ALU.subtract).then_inc(ff.split, 1)


def project_and_prepare(nc, d, k, l, x, oT, ff, first):
    moe = ff.moe
    CHUNKS = NB * CPB
    with ExitStack() as ph:
        tag = f"p{l}_"
        sb = lambda n, s, dt=F32: ph.enter_context(nc.sbuf_tensor(tag + n, s, dt))
        sem = ph.enter_context(signals(nc, tag))
        prep = Prep(nc, ph, sem, k, l, 1, x, tag)
        early = first is not None
        first = first or FirstWeights(nc, ph, l)
        raw1 = first.raw
        raw2 = sb("raw2", [P, KT, C])
        gate = sb("gate", [P, NB, C])
        wpg = sb("wpg", [P, NB, QUADS, C])
        ps = ph.enter_context(nc.psum_tensor(tag + "ps", [P, 4, CH], F32))
        w_in, raw2_in, mm, gated, added = sem("w_in"), sem("raw2_in"), sem("mm"), sem("gated"), sem("added")
        if moe:
            cw = ff.cw
            wg = sb("wg", [P, FT, NE])
            lg = sb("lg", [P, TILES, NE])
            cmp = sb("cmp", [P, TILES, NE, NE - 1])
            top = sb("top", [P, TILES])
            ee = sb("ee", [P, TILES, NE])
            psG = ph.enter_context(nc.psum_tensor(tag + "psG", [P, TILES, NE], F32))
            g_in, g_mm, g_got, g_dve, g_exp = sem("g_in"), sem("g_mm"), sem("g_got"), sem("g_dve"), sem("g_exp")
        block = ph.enter_context(nc.Block())

        def stack(g):
            at = slice(g * CH, (g + 1) * CH)
            return ff.XH[:, :, at], ff.XL[:, :, at], ff.X8[:, at]

        @block.sync
        def _(sp):
            for b in range(NB):
                sp.dma_start(wpg[:, b, :, :], d[f"wp{l}"]).then_inc(w_in, 16)
                sp.dma_start(gate[:, b, :], k["mods"][b, l, 2].partition_broadcast(P)).then_inc(w_in, 16)
            if moe:
                sp.dma_start(wg[:, :, :], d["wg"]).then_inc(g_in, 16)
            sp.dma_start(ff.b1[:, :, :], d[f"b1_{l}"]).then_inc(ff.b_in, 16)
            if not early:
                first.load(sp, d)
            sp.dma_start(raw2[:, :, :], d[f"w2_{l}"][0]).then_inc(raw2_in, 16)
            for b in range(NB):
                sp.dma_start(ff.gate[:, b, :], k["mods"][b, l, 5].partition_broadcast(P)).then_inc(ff.b_in, 16)
            for e in range(ff.n_exp):
                sp.dma_start(ff.b2[:, e, :], d[f"b2_{l}"][e].partition_broadcast(P)).then_inc(ff.b_in, 16)

        @block.tensor
        def _(pe):
            pe.sem_inc(prep.s_T, 2)
            if moe:
                pe.wait_ge(g_in, 16)
            for g in range(CHUNKS + 2):
                if g < CHUNKS:
                    for n in range(g * TPC, (g + 1) * TPC):
                        if n % TPB == 0:
                            pe.wait_ge(gated, n // TPB + 1)
                        if n >= 4:
                            pe.wait_ge(added, n - 3)
                        for q in range(QUADS):
                            o = oT[:, 1 + n // TPB * QUADS + q, n % TPB * P:(n % TPB + 1) * P]
                            r = pe.matmul(ps[:, n % 4, 0:C], o, wpg[:, n // TPB, q, :], start=(q == 0), stop=(q == QUADS - 1))
                        r.then_inc(mm, 1)
                if moe and g >= 2:
                    pe.wait_ge(prep.s_y, g + 1)
                    for n in range((g - 2) * TPC, (g - 1) * TPC):
                        cols = slice(n % TPC * P, (n % TPC + 1) * P)
                        for f, rows in enumerate((P, P, TAIL)):
                            r = pe.matmul(psG[:, n, :], prep.y[0:rows, g % 2, f, cols], wg[0:rows, f, :],
                                          start=(f == 0), stop=(f == FT - 1))
                    if g == CHUNKS + 1:
                        r.then_inc(g_mm, 1)
                if 1 <= g <= CHUNKS:
                    prep.transpose(pe, g - 1, (g - 1) % 2)

        @block.scalar
        def _(act):
            W1H, W1L, W18, W2H, W2L, b1e = ff.slots[0]

            def high_up():
                act.wait_ge(first.loaded, 16)
                act.activation(W1H[:, :, :], raw1[:, 0:2, :], ACT.Copy)
                act.activation(W18[:, :], raw1[:, 2, :], ACT.Copy).then_inc(ff.h_ok, 1)

            if early:
                high_up()
            for g in range(CHUNKS + 1):
                if g < CHUNKS:
                    prep.deviation(act, g, g % 2)
                if g == 0:
                    if not early:
                        high_up()
                    act.wait_ge(ff.b_in, 16 * (3 + ff.n_exp))
                    act.activation(b1e[:, :], ff.b1[:, 0, :], ACT.Copy)
                    act.wait_ge(raw2_in, 16)
                    act.activation(W2H[:, :, :], raw2[:, :, :], ACT.Copy).then_inc(ff.h2_ok, 1)
                if g >= 1:
                    h, lo, e8 = stack(g - 1)
                    prep.high(act, g - 1, (g - 1) % 2, h, e8)
            if moe:
                act.wait_ge(g_dve, 2)
                act.activation(ee[:, :, :], ee[:, :, :], ACT.Exp).then_inc(g_exp, 1)

        @block.gpsimd
        def _(pool):
            pool.wait_ge(ff.h_ok, 1)
            low_parts(pool, ff, raw1, raw2, 0, ff.slots[0])
            pool.wait_ge(ff.split, 1)
            for g in range(CHUNKS):
                h, lo, e8 = stack(g)
                prep.low(pool, g, g % 2, h, lo, e8)

        @block.vector
        def _(dve):
            prep.credits(dve)
            dve.wait_ge(w_in, 64)

            def gate_weights(b):
                dve.tensor_tensor(wpg[:, b, :, :], wpg[:, b, :, :], gate[:, b, :].unsqueeze(1).broadcast_to([P, QUADS, C]),
                                  ALU.mult).then_inc(gated, 1)

            gate_weights(0)
            for g in range(CHUNKS + 1):
                if g == 1:
                    gate_weights(1)
                if g < CHUNKS:
                    for n in range(g * TPC, (g + 1) * TPC):
                        dve.wait_ge(mm, n + 1)
                        dve.tensor_tensor(x[:, n, :], ps[:, n % 4, 0:C], x[:, n, :], ALU.add).then_inc(added, 1)
                    dve.wait_ge(added, (g + 1) * TPC)
                    prep.statistics(dve, g, g % 2)
                if g >= 1:
                    prep.modulate(dve, (g - 1) // CPB, g - 1, (g - 1) % 2)
                if g < CHUNKS:
                    prep.normalise(dve, g, g % 2)
            if moe:
                dve.wait_ge(g_mm, 1)
                dve.tensor_copy(lg[:, :, :], psG[:, :, :]).then_inc(g_got, 1)
            if moe:
                done = count(1)

                dve.wait_ge(g_got, 1)
                dve.tensor_reduce(top[:, :], lg[:, :, :], AX, ALU.max).then_inc(g_dve, 1)
                dve.wait_ge(g_dve, next(done))
                dve.tensor_tensor(ee[:, :, :], lg[:, :, :], top[:, :].unsqueeze(2).broadcast_to([P, TILES, NE]), ALU.subtract).then_inc(g_dve, 1)
                dve.wait_ge(g_dve, next(done))
                for e in range(NE):
                    for a, j in enumerate(j for j in range(NE) if j != e):
                        r = dve.tensor_tensor(cmp[:, :, e, a], lg[:, :, j], lg[:, :, e], ALU.is_ge if j < e else ALU.is_gt)
                r.then_inc(g_dve, 1)
                dve.wait_ge(g_dve, next(done))
                dve.tensor_reduce(cw[:, :, :], cmp[:, :, :, :], AX, ALU.add).then_inc(g_dve, 1)
                dve.wait_ge(g_dve, next(done))
                dve.tensor_scalar(cw[:, :, :], cw[:, :, :], 2.0, None, ALU.is_lt).then_inc(g_dve, 1)
                dve.wait_ge(g_dve, next(done))
                dve.wait_ge(g_exp, 1)
                dve.tensor_tensor(cw[:, :, :], cw[:, :, :], ee[:, :, :], ALU.mult).then_inc(g_dve, 1)
                dve.wait_ge(g_dve, next(done))
                dve.tensor_reduce(top[:, :], cw[:, :, :], AX, ALU.add).then_inc(g_dve, 1)
                dve.wait_ge(g_dve, next(done))
                dve.reciprocal(top[:, :], top[:, :]).then_inc(g_dve, 1)
                dve.wait_ge(g_dve, next(done))
                dve.tensor_tensor(cw[:, :, :], cw[:, :, :], top[:, :].unsqueeze(2).broadcast_to([P, TILES, NE]), ALU.mult).then_inc(g_dve, 1)
                dve.wait_ge(g_dve, next(done))


def feed_forward(nc, d, k, l, x, oT, ff, out=None):
    moe, n_exp = ff.moe, ff.n_exp
    func = ACT.Gelu if l == 1 else ACT.Gelu_apprx_tanh
    CHUNKS = NB * CPB
    M = CHUNKS * KT
    DN0 = 2 * M
    XH, XL, X8, b1, b2, gate = ff.XH, ff.XL, ff.X8, ff.b1, ff.b2, ff.gate
    b_in, raw_in, split, h_ok = ff.b_in, ff.raw_in, ff.split, ff.h_ok
    tag = f"g{l}_"
    cw = ff.cw
    with ExitStack() as ph:
        sb = lambda n, s, dt=F32: ph.enter_context(nc.sbuf_tensor(tag + n, s, dt))
        sem = ph.enter_context(signals(nc, tag))
        slots = ff.slots + ([ff.slot(sb, 1)] if moe else [])
        W1H, W1L, W18, W2H, W2L, b1e = zip(*slots)
        cwe = sb("cwe", [P, TILES])
        GS = 3
        room, at = oT[:, :, :].rearrange("p n c -> p (n c)"), 0
        views = []
        for shape in ((FT, FF), (KT, C), (GS, CH), (TPC, C)):
            size = shape[0] * shape[1]
            views.append(room[:, at:at + size].rearrange("p (a c) -> p a c", c=shape[1]))
            at += size
        raw1, raw2, g32, tb = views
        gh = sb("gh", [P, GS, CH], F32R)
        gl = sb("gl", [P, GS, CH], F32R)
        psU = ph.enter_context(nc.psum_tensor(tag + "psU", [P, GS, CH], F32))
        psA = ph.enter_context(nc.psum_tensor(tag + "psA", [P, TPC, CH], F32))
        up, acted, glow, dn, taken, me = (
            sem("up"), sem("acted"), sem("glow"), sem("dn"), sem("taken"), sem("self"))
        stored = sem("stored")
        block = ph.enter_context(nc.Block())

        def experts(eng, body):
            if n_exp == 1:
                body(0, 0)
                return
            with eng.Fori(0, n_exp // 2) as i:
                for p in range(2):
                    body(i * 2 + p, p)

        @block.sync
        def _(sp):
            if moe:
                with sp.Fori(1, NE) as e:
                    sp.wait_ge(split, e)
                    sp.dma_start(raw1[:, :, :], d[f"w1_{l}"][bass.ds(e, 1)].rearrange("o p f n -> p (o f) n")).then_inc(raw_in, 16)
                    sp.dma_start(raw2[:, :, :], d[f"w2_{l}"][bass.ds(e, 1)].rearrange("o p f n -> p (o f) n")).then_inc(raw_in, 16)
            if out is not None:
                rows = out.rearrange("b s c -> (b s) c").rearrange("(t p) c -> p t c", p=P)
                for c in range(CHUNKS):
                    sp.wait_ge(me, 2 * TPC * (c + 1))
                    tiles = slice(c * TPC, (c + 1) * TPC)
                    sp.dma_start(rows[:, tiles, :], x[:, tiles, :]).then_inc(stored, 16)
                sp.wait_ge(stored, 16 * CHUNKS)

        @block.gpsimd
        def _(pool):
            for e in range(1, n_exp):
                p = e % 2
                pool.wait_ge(raw_in, 32 * e)
                pool.wait_ge(dn, DN0 + M * (e - 1))
                pool.tensor_copy(b1e[p][:, :], b1[:, e, :])
                pool.tensor_copy(W1H[p][:, :, :], raw1[:, 0:2, :])
                pool.tensor_copy(W18[p][:, :], raw1[:, 2, :]).then_inc(h_ok, 1)
                pool.tensor_copy(W2H[p][:, :, :], raw2[:, :, :]).then_inc(ff.h2_ok, 1)
                pool.wait_ge(h_ok, 4 * e + 1)
                low_parts(pool, ff, raw1, raw2, e, slots[p])

        @block.scalar
        def _(act):
            act.sem_inc(acted, GS)

            def body(e, p):
                act.wait_ge(split, e + 1)
                for m in range(M):
                    g = M * e + m
                    act.wait_ge(up, g + 1)
                    act.wait_ge(dn, DN0 + g - GS + 1)
                    act.wait_ge(glow, g + 1)
                    bias = b1e[p][:, m % KT:m % KT + 1]
                    act.activation(gh[:, m % GS, :], psU[:, m % GS, :], func, bias=bias)
                    act.activation(g32[:, m % GS, :], psU[:, m % GS, :], func, bias=bias).then_inc(acted, 1)

            experts(act, body)

        @block.vector
        def _(dve):
            dve.sem_inc(glow, GS)
            dve.sem_inc(taken, TPC)
            dve.wait_ge(b_in, 16 * (3 + n_exp))
            per = (1 if moe else 0) + CHUNKS * TPC * 2

            def body(e, p):
                before = e * per + (1 if moe else 0)
                if moe:
                    dve.tensor_copy(cwe[:, :], cw[:, :, bass.ds(e, 1)].rearrange("p t o -> p (t o)")).then_inc(me, 1)

                def take(c):
                    dve.wait_ge(dn, DN0 + M * e + KT * (c + 1))
                    for t in range(TPC):
                        dve.tensor_tensor(tb[:, t, :], psA[:, t, 0:C], b2[:, bass.ds(e, 1), :].rearrange("p o n -> p (o n)"),
                                          ALU.add).then_inc(taken, 1)

                def add(c, t):
                    n = c * TPC + t
                    dve.wait_ge(taken, TPC + CHUNKS * TPC * e + TPC * c + t + 1)
                    if moe and n == 0:
                        dve.wait_ge(me, before)
                    dve.scalar_tensor_tensor(
                        out=tb[:, t, :], in0=tb[:, t, :], scalar=cwe[:, n:n + 1] if moe else 1.0,
                        in1=gate[:, n // TPB, :], op0=ALU.mult, op1=ALU.mult).then_inc(me, 1)
                    dve.wait_ge(me, before + 2 * n + 1)
                    dve.tensor_tensor(x[:, n, :], x[:, n, :], tb[:, t, :], ALU.add).then_inc(me, 1)
                    dve.wait_ge(me, before + 2 * n + 2)

                for m in range(M + 2):
                    g = M * e + m
                    if m < M:
                        dve.wait_ge(acted, g + 1 + GS)
                        dve.wait_ge(dn, DN0 + g - GS + 1)
                        dve.tensor_tensor(gl[:, m % GS, :], g32[:, m % GS, :], gh[:, m % GS, :].bitcast(F32),
                                          ALU.subtract).then_inc(glow, 1)
                    c, r = divmod(m - 2 - (KT - 1), KT)
                    if c >= 0 and r == 0:
                        take(c)
                    if c >= 0 and 1 <= r <= TPC:
                        add(c, r - 1)
                for t in range(TPC):
                    add(CHUNKS - 1, t)

            experts(dve, body)

        @block.tensor
        def _(pe):
            pe.sem_inc(dn, DN0)

            def down(e, p, m):
                g, c, kt = M * e + m, m // KT, m % KT
                pe.wait_ge(glow, g + 1 + GS)
                for t in range(TPC):
                    if kt == 0:
                        pe.wait_ge(taken, CHUNKS * TPC * e + TPC * c + t + 1)
                    cols = slice(t * P, (t + 1) * P)
                    for a, (lhs, rhs) in enumerate(((gh, W2H), (gl, W2H), (gh, W2L))):
                        r = pe.matmul(psA[:, t, 0:C], lhs[:, m % GS, cols], rhs[p][:, kt, :],
                                      start=(kt == 0 and a == 0), stop=(kt == KT - 1 and a == 2))
                r.then_inc(dn, 1)

            def body(e, p):
                pe.wait_ge(split, e + 1)
                for m in range(M + 2):
                    if m < M:
                        g, c, kt = M * e + m, m // KT, m % KT
                        cols = slice(kt * P, (kt + 1) * P)
                        at = slice(c * CH, (c + 1) * CH)
                        pe.wait_ge(acted, g + 1)
                        terms = [(w_[p][:, f, cols], x_[:, f, at]) for x_, w_ in ((XH, W1H), (XL, W1H), (XH, W1L)) for f in range(2)]
                        terms.append((W18[p][:, cols], X8[:, at]))
                        for a, (lhs, rhs) in enumerate(terms):
                            r = pe.matmul(psU[:, m % GS, :], lhs, rhs, start=(a == 0), stop=(a == 6))
                        r.then_inc(up, 1)
                    if m >= 2:
                        down(e, p, m - 2)

            experts(pe, body)


def build(nc, d, out):
    with ExitStack() as ctx:
        k = {}
        consts(nc, ctx, k)
        x = ctx.enter_context(nc.sbuf_tensor("x", [P, TILES, C], F32))
        qk_scr = nc.dram_tensor("qk_scr", (2, 2, NQ, P, SEQ), F32, kind="Internal").ap()
        v_scr = nc.dram_tensor("v_scr", (NQ, TPB, P, P), F32, kind="Internal").ap()
        rotate(nc, ctx, d, k, x)
        oT = ctx.enter_context(nc.sbuf_tensor("oT", [P, NQ + 1, SEQ], F32))
        for l in range(3):
            project_qkv(nc, d, k, l, x, qk_scr, v_scr)
            with ExitStack() as fed:
                first = FirstWeights(nc, fed, l) if l else None
                attend(nc, d, k, l, qk_scr, v_scr, oT, first)
                ff = FeedTensors(nc, fed, l)
                project_and_prepare(nc, d, k, l, x, oT, ff, first)
                feed_forward(nc, d, k, l, x, oT, ff, out if l == 2 else None)


_OUT = ((NB, SEQ, C), "float32")


def _layout(a):
    import numpy as np

    z = lambda *s: np.zeros(s, np.float32)
    d = {}

    def stack(w):
        tail = np.concatenate([w[2 * P:]] * 4, 0)
        return np.ascontiguousarray(np.stack([w[0:P], w[P:2 * P], tail], 1))

    def heads(w, one=None):
        p = z(*w.shape[:-1], NH, HP)
        p[..., :HD] = w.reshape(*w.shape[:-1], NH, HD)
        if one:
            p[..., SUMCOL] = 1.0
        return p.reshape(*w.shape[:-1], NH * HP)

    d["x"] = a["x"].reshape(TOK, C)
    d["xT"] = np.ascontiguousarray(d["x"].T)
    d["condT"] = np.ascontiguousarray(a["cond_1152"].T)
    d["PT"] = np.ascontiguousarray(a["L0_cond_P"].T)
    iu, ju = np.triu_indices(RD, k=1)
    iu, ju = np.triu_indices(RD, k=1)
    w, b = z(RD, RD, C), z(RD, RD)
    w[iu, ju] = a["L0_cond_W"]
    b[iu, ju] = a["L0_cond_b"]
    pad = NCOND * CW - RD * RD - MODS
    ada = [(a["L1_cond_w_adaln"], a["L1_cond_b_adaln"]), (a["L2_cond_w_ada"], a["L2_cond_b_ada"]),
           (a["L3_cond_W_ada"], a["L3_cond_b_ada"])]
    d["w_cond"] = np.ascontiguousarray(np.concatenate([w.reshape(RD * RD, C).T] + [v for v, _ in ada] + [z(C, pad)], 1))
    d["b_cond"] = np.concatenate([b.reshape(-1)] + [v.reshape(-1) for _, v in ada] + [z(pad)]).reshape(1, -1)
    names = [
        dict(qkv="L1_cond_w_qkv", bqkv="L1_cond_b_qkv",
             p="L1_cond_w_proj", bp="L1_cond_b_proj", w1="L1_cond_w1", b1="L1_cond_b1", w2="L1_cond_w2", b2="L1_cond_b2"),
        dict(qkv="L2_cond_w_qkv", bqkv="L2_cond_b_qkv",
             p="L2_cond_w_proj", bp="L2_cond_b_proj", w1="L2_cond_w1", b1="L2_cond_b1", w2="L2_cond_w2", b2="L2_cond_b2"),
        dict(qkv="L3_cond_W_qkv", bqkv="L3_cond_b_qkv",
             p="L3_cond_W_proj", bp="L3_cond_b_proj", w1="L3_cond_W_fc1", b1="L3_cond_b_fc1", w2="L3_cond_W_fc2", b2="L3_cond_b_fc2"),
    ]
    for l, nm in enumerate(names):
        qkv, bqkv = a[nm["qkv"]].reshape(C, 3, C), a[nm["bqkv"]].reshape(3, C)
        d[f"wqkv{l}"] = stack(np.concatenate([heads(qkv[:, j]) for j in range(3)], 1))
        bq, bk = heads(bqkv[0]), heads(bqkv[1], True)
        d[f"bqk{l}"] = np.ascontiguousarray(np.concatenate([bq, bk]).reshape(2 * QUADS, P).T)
        d[f"bv{l}"] = heads(bqkv[2], True)
        wp = z(NH, HP, C)
        wp[:, :HD] = a[nm["p"]].reshape(NH, HD, C)
        wp[0, SUMCOL] = a[nm["bp"]]
        d[f"wp{l}"] = np.ascontiguousarray(wp.reshape(QUADS, P, C).transpose(1, 0, 2))
        n = NE if l == 0 else 1
        w1, b1 = a[nm["w1"]].reshape(n, C, FF), a[nm["b1"]].reshape(n, KT, P)
        w2, b2 = a[nm["w2"]].reshape(n, KT, P, C), a[nm["b2"]].reshape(n, C)
        d[f"w1_{l}"] = np.stack([stack(w1[e]) for e in range(n)])
        d[f"b1_{l}"] = np.ascontiguousarray(b1.transpose(2, 0, 1))
        d[f"w2_{l}"] = np.ascontiguousarray(w2.transpose(0, 2, 1, 3))
        d[f"b2_{l}"] = b2
    d["wg"] = stack(a["L1_cond_w_gate"])
    g = z(4, 4, HP)
    for j, nm in enumerate(("L2_cond_qn_g", "L2_cond_qn_b", "L2_cond_kn_g", "L2_cond_kn_b")):
        g[j, :, :HD] = a[nm]
    g[3, :, SUMCOL] = 1.0
    d["qkn"] = np.ascontiguousarray(g.reshape(4, P).T)
    return d


def kernel(**inputs):
    import numpy as np
    from concourse import bacc
    from concourse.bass_utils import run_bass_kernel_spmd

    laid = _layout({n: np.asarray(v) for n, v in inputs.items()})
    nc = bacc.Bacc("TRN2", target_bir_lowering=False, num_devices=1)
    arrays, d = {}, {}
    for n, v in laid.items():
        arrays["in_" + n] = v
        d[n] = nc.dram_tensor("in_" + n, v.shape, mybir.dt.from_np(v.dtype), kind="ExternalInput").ap()
    out = nc.dram_tensor("out_0", _OUT[0], F32, kind="ExternalOutput").ap()
    build(nc, d, out)
    r = run_bass_kernel_spmd(nc, [arrays], core_ids=[0])
    return r.results[0]["out_0"]
```
